# Optimizing a Trainium2 kernel written in Bass

```python
import numpy as np
import jax
import jax.numpy as jnp

def _softmax(x, axis=-1):
    return jax.nn.softmax(x, axis=axis)

def _gelu(x):
    return jax.nn.gelu(x, approximate=True)

def _silu(x):
    return jax.nn.silu(x)

def _sigmoid(x):
    return jax.nn.sigmoid(x)

def _layernorm(x, axis=-1, eps=1e-05):
    m = jnp.mean(x, axis=axis, keepdims=True)
    v = jnp.var(x, axis=axis, keepdims=True)
    return (x - m) / jnp.sqrt(v + eps)

def _scatter_add(tgt, idx, src, axis=0):
    return tgt.at[idx].add(src)

def _segment_sum(src, seg, n):
    return jax.ops.segment_sum(src, seg, n)
kernel_name = 'mk_decoder_preln_d2_seqx_r4_46f1f1'

def setup_inputs(seed: int=0):
    np.random.seed(seed)
    _w = jnp.asarray

    def _rec_inputs():
        import jax
        import jax.numpy as jnp
        _rk = jax.random.key(seed)
        x = -0.0002928 + 1 * jax.random.normal(jax.random.fold_in(_rk, 1), (4, 512, 256), jnp.float32)
        _lenS = 512 - jax.random.randint(jax.random.fold_in(_rk, 7), (4,), 0, max(1, 512 // 4) + 1, jnp.int32)
        _lenS2 = 1601 - jax.random.randint(jax.random.fold_in(_rk, 8), (4,), 0, max(1, 1601 // 4) + 1, jnp.int32)
        _ctx_1024P = jax.random.normal(jax.random.fold_in(_rk, 11), (4, 16, 256), jnp.float32)
        _ctx_1024c = jax.random.dirichlet(jax.random.fold_in(_rk, 511), 0.3 * jnp.ones((16,), jnp.float32), (4, 1601))
        _ctx_1024t = jnp.einsum('bsk,bkd->bsd', _ctx_1024c, _ctx_1024P)
        _ctx_1024t = _ctx_1024t * jax.lax.rsqrt(jnp.mean(jnp.square(_ctx_1024t)) + 1e-12) * 0.953939
        ctx_1024 = -1.39393e-06 + 0.999914 * (_ctx_1024t + 0.3 * jax.random.normal(jax.random.fold_in(_rk, 611), (4, 1601, 256), jnp.float32))
        _validS = jnp.arange(512)[None, :] < _lenS[:, None]
        _validS2 = jnp.arange(1601)[None, :] < _lenS2[:, None]
        _causal = jnp.tril(jnp.ones((512, 512), dtype=bool))
        mask_BxSxS2_bk1 = jnp.broadcast_to(_validS2[:, None, :], (4, 512, 1601))
        return (x, ctx_1024, mask_BxSxS2_bk1)
    x, ctx_1024, mask_BxSxS2_bk1 = _rec_inputs()

    def _L0_attn_setup():
        import jax, jax.numpy as jnp
        import numpy as np
        B, T, D = (2, 512, 256)
        HV, HK = (16, 8)
        DK, DV = (64, 64)
        K_DIM = HK * DK
        V_DIM = HV * DV
        CONV_DIM = 2 * K_DIM + V_DIM
        KS = 4
        EPS = 1e-06

        def _causal_conv_silu(x, w):
            xp = jnp.pad(x, ((0, 0), (KS - 1, 0), (0, 0)))
            y = sum((xp[:, i:i + x.shape[1], :] * w[:, i] for i in range(KS)))
            return jax.nn.silu(y)

        def _l2norm(x):
            return x * jax.lax.rsqrt(jnp.sum(x * x, -1, keepdims=True) + EPS)

        def _forward(hidden_states, W_qkv, W_z, W_b, W_a, dt_bias, A_log, conv_w, norm_w, W_out):
            b_, t_ = hidden_states.shape[:2]
            mixed_qkv = hidden_states @ W_qkv
            z = (hidden_states @ W_z).reshape(b_, t_, HV, DV)
            beta = jax.nn.sigmoid(hidden_states @ W_b)
            g = -jnp.exp(A_log) * jax.nn.softplus(hidden_states @ W_a + dt_bias)
            mixed_qkv = _causal_conv_silu(mixed_qkv, conv_w)
            q, k, v = jnp.split(mixed_qkv, [K_DIM, 2 * K_DIM], axis=-1)
            q = q.reshape(b_, t_, HK, DK)
            k = k.reshape(b_, t_, HK, DK)
            v = v.reshape(b_, t_, HV, DV)
            rep = HV // HK
            q = jnp.repeat(q, rep, axis=2)
            k = jnp.repeat(k, rep, axis=2)
            q = _l2norm(q) * DK ** (-0.5)
            k = _l2norm(k)
            qT = q.transpose(1, 0, 2, 3)
            kT = k.transpose(1, 0, 2, 3)
            vT = v.transpose(1, 0, 2, 3)
            gT = g.transpose(1, 0, 2)
            bT = beta.transpose(1, 0, 2)

            def step(S, xs):
                q_t, k_t, v_t, g_t, b_t = xs
                S = S * jnp.exp(g_t)[..., None, None]
                kv = jnp.einsum('bhk,bhkv->bhv', k_t, S)
                S = S + jnp.einsum('bhk,bhv->bhkv', k_t, (v_t - kv) * b_t[..., None])
                o_t = jnp.einsum('bhk,bhkv->bhv', q_t, S)
                return (S, o_t)
            S0 = jnp.zeros((b_, HV, DK, DV), jnp.float32)
            _, oT = jax.lax.scan(step, S0, (qT, kT, vT, gT, bT))
            o = oT.transpose(1, 0, 2, 3)
            var = jnp.mean(o * o, axis=-1, keepdims=True)
            o = o * jax.lax.rsqrt(var + EPS) * norm_w * jax.nn.silu(z)
            return o.reshape(b_, t_, V_DIM) @ W_out
        key = jax.random.key(seed)
        ks = jax.random.split(key, 9)
        g = lambda k, shape, sc: jax.random.normal(k, shape, jnp.float32) * sc
        return {'hidden_states': g(ks[0], (B, T, D), 1.0), 'W_qkv': g(ks[1], (D, CONV_DIM), 0.02), 'W_z': g(ks[2], (D, V_DIM), 0.02), 'W_b': g(ks[3], (D, HV), 0.02), 'W_a': g(ks[4], (D, HV), 0.02), 'dt_bias': jnp.ones((HV,), jnp.float32), 'A_log': jnp.log(jax.random.uniform(ks[5], (HV,), jnp.float32, 0.001, 16.0)), 'conv_w': g(ks[6], (CONV_DIM, KS), 0.2), 'norm_w': jnp.ones((DV,), jnp.float32), 'W_out': g(ks[7], (V_DIM, D), 0.02)}
    _L0_attn_all = _L0_attn_setup()
    _L0_attn_in = {k: v for k, v in _L0_attn_all.items() if k in ('W_qkv', 'W_z', 'W_b', 'W_a', 'dt_bias', 'A_log', 'conv_w', 'norm_w', 'W_out')}
    del _L0_attn_all

    def _L0_xattn_setup():
        import jax, jax.numpy as jnp
        import numpy as np
        B, T, C = (2, 512, 256)
        H, DQK, DV = (16, 64, 64)

        def _split_heads(x, d):
            b, t, _ = x.shape
            return x.reshape(b, t, H, d).transpose(0, 2, 1, 3)
        key = jax.random.key(seed)
        ks = jax.random.split(key, 8)
        s = 0.03
        Q = jax.random.normal(ks[0], (B, T, C), jnp.float32)
        K = jax.random.normal(ks[1], (B, T, C), jnp.float32)
        V = jax.random.normal(ks[2], (B, T, C), jnp.float32)
        mask = jnp.broadcast_to(jnp.triu(jnp.ones((T, T), bool), 1), (B, T, T))
        Wq = jax.random.normal(ks[3], (C, H * DQK), jnp.float32) * s
        Wk = jax.random.normal(ks[4], (C, H * DQK), jnp.float32) * s
        Wv = jax.random.normal(ks[5], (C, H * DV), jnp.float32) * s
        Wo = jax.random.normal(ks[6], (H * DV, C), jnp.float32) * s
        bq = jnp.zeros((H * DQK,), jnp.float32)
        bk = jnp.zeros((H * DQK,), jnp.float32)
        bv = jnp.zeros((H * DV,), jnp.float32)
        bo = jnp.zeros((C,), jnp.float32)
        return {'Q': Q, 'K': K, 'V': V, 'mask': mask, 'Wq': Wq, 'bq': bq, 'Wk': Wk, 'bk': bk, 'Wv': Wv, 'bv': bv, 'Wo': Wo, 'bo': bo}
    _L0_xattn_all = _L0_xattn_setup()
    _L0_xattn_in = {k: v for k, v in _L0_xattn_all.items() if k in ('Wq', 'bq', 'Wk', 'bk', 'Wv', 'bv', 'Wo', 'bo')}
    del _L0_xattn_all

    def _L0_ffn_setup():
        import jax, jax.numpy as jnp
        import numpy as np
        D_IN, D_HID = (256, 1024)

        def _ternary(key, shape):
            return jax.random.randint(key, shape, -1, 2).astype(jnp.float32)

        def _tlin(x, w, s):
            return jnp.einsum('bsi,oi->bso', x, w) * s
        key = jax.random.key(seed)
        ks = jax.random.split(key, 12)
        inv = lambda fan: 1.0 / np.sqrt(fan).astype(np.float32)
        return {'x': jax.random.normal(ks[0], (4, 512, D_IN), dtype=jnp.float32), 'w1_w': _ternary(ks[1], (D_HID, D_IN)), 'w1_s': jax.random.uniform(ks[2], (D_HID,), dtype=jnp.float32) * inv(D_IN), 'w2_w': _ternary(ks[3], (D_HID, D_IN)), 'w2_s': jax.random.uniform(ks[4], (D_HID,), dtype=jnp.float32) * inv(D_IN), 'h1_w': _ternary(ks[5], (D_HID, D_HID)), 'h1_s': jax.random.uniform(ks[6], (D_HID,), dtype=jnp.float32) * inv(D_HID), 'h2_w': _ternary(ks[7], (D_HID, D_HID)), 'h2_s': jax.random.uniform(ks[8], (D_HID,), dtype=jnp.float32) * inv(D_HID), 'w3_w': _ternary(ks[9], (D_IN, D_HID)), 'w3_s': jax.random.uniform(ks[10], (D_IN,), dtype=jnp.float32) * inv(D_HID)}
    _L0_ffn_all = _L0_ffn_setup()
    _L0_ffn_in = {k: v for k, v in _L0_ffn_all.items() if k in ('w1_w', 'w1_s', 'w2_w', 'w2_s', 'h1_w', 'h1_s', 'h2_w', 'h2_s', 'w3_w', 'w3_s')}
    del _L0_ffn_all

    def _L1_attn_setup():
        import jax, jax.numpy as jnp
        import numpy as np
        from jax import lax
        B, S, D = (2, 256, 256)
        N = 16
        EXPAND = 2
        DI = EXPAND * D
        K = 4
        H = 16
        DH = D // H
        DT_RANK = D // 16
        SOL_DT = 0.1

        def _ln(x, g, b):
            mu = jnp.mean(x, -1, keepdims=True)
            var = jnp.var(x, -1, keepdims=True)
            return (x - mu) / jnp.sqrt(var + 1e-05) * g + b

        def _forward(x, ln1_g, ln1_b, W_in, b_in, conv_w, conv_b, W_xp, W_dt, b_dt, A_log, D_skip, W_out, b_out, ln2_g, ln2_b, W_si, b_si, gates, alpha, W_so, b_so):
            b, s, d = x.shape
            u = _ln(x, ln1_g, ln1_b)
            xz = u @ W_in + b_in
            xp, z = jnp.split(xz, 2, axis=-1)
            xt = xp.transpose(0, 2, 1)
            yc = lax.conv_general_dilated(xt, conv_w[:, None, :], (1,), [(K - 1, 0)], feature_group_count=DI, dimension_numbers=('NCW', 'OIW', 'NCW'))
            xc = jax.nn.silu(yc.transpose(0, 2, 1) + conv_b)
            dbc = xc @ W_xp
            dtr, Bs, Cs = jnp.split(dbc, [DT_RANK, DT_RANK + N], axis=-1)
            dt = jax.nn.softplus(dtr @ W_dt + b_dt)
            A = -jnp.exp(A_log)
            dA = jnp.exp(dt[..., None] * A)
            dBx = (dt * xc)[..., None] * Bs[:, :, None, :]

            def step(h, inp):
                dA_t, dBx_t, C_t = inp
                h = dA_t * h + dBx_t
                y = jnp.einsum('bdn,bn->bd', h, C_t)
                return (h, y)
            h0 = jnp.zeros((b, DI, N), x.dtype)
            xs = (dA.transpose(1, 0, 2, 3), dBx.transpose(1, 0, 2, 3), Cs.transpose(1, 0, 2))
            _, ys = lax.scan(step, h0, xs)
            y = ys.transpose(1, 0, 2)
            y = (y + xc * D_skip) * jax.nn.silu(z)
            x = x + y @ W_out + b_out
            v = _ln(x, ln2_g, ln2_b)
            uu = (v @ W_si + b_si).reshape(b, s, H, DH)
            up = jnp.pad(uu, ((0, 0), (2, 2), (0, 0), (0, 0)), mode='edge')
            ux = (up[:, 3:-1] - up[:, 1:-3]) * 0.5
            uxx = up[:, 3:-1] - 2.0 * uu + up[:, 1:-3]
            uxxx = (up[:, 4:] - 2.0 * up[:, 3:-1] + 2.0 * up[:, 1:-3] - up[:, :-4]) * 0.5
            sg = jnp.sin(uu)
            kdv = -6.0 * uu * ux - uxxx
            hj = (1.0 + alpha[None, None, :, None] * uu) * uxx
            du = gates[None, None, :, 0:1] * sg + gates[None, None, :, 1:2] * kdv + gates[None, None, :, 2:3] * hj
            sol = (SOL_DT * du).reshape(b, s, d) @ W_so + b_so
            return x + sol
        key = jax.random.key(seed)
        ks = jax.random.split(key, 12)

        def nrm(k, sh, sc=0.02):
            return jax.random.normal(k, sh, jnp.float32) * sc
        return {'x': nrm(ks[0], (B, S, D), 1.0), 'ln1_g': jnp.ones(D), 'ln1_b': jnp.zeros(D), 'W_in': nrm(ks[1], (D, 2 * DI)), 'b_in': jnp.zeros(2 * DI), 'conv_w': nrm(ks[2], (DI, K), 0.1), 'conv_b': jnp.zeros(DI), 'W_xp': nrm(ks[3], (DI, DT_RANK + 2 * N)), 'W_dt': nrm(ks[4], (DT_RANK, DI), 0.1), 'b_dt': jnp.full((DI,), -4.6), 'A_log': jnp.log(jnp.broadcast_to(jnp.arange(1, N + 1, dtype=jnp.float32), (DI, N))), 'D_skip': jnp.ones(DI), 'W_out': nrm(ks[5], (DI, D)), 'b_out': jnp.zeros(D), 'ln2_g': jnp.ones(D), 'ln2_b': jnp.zeros(D), 'W_si': nrm(ks[6], (D, D)), 'b_si': jnp.zeros(D), 'gates': nrm(ks[7], (H, 3), 0.1), 'alpha': nrm(ks[8], (H,), 0.1), 'W_so': nrm(ks[9], (D, D)), 'b_so': jnp.zeros(D)}
    _L1_attn_all = _L1_attn_setup()
    _L1_attn_in = {k: v for k, v in _L1_attn_all.items() if k in ('ln1_g', 'ln1_b', 'W_in', 'b_in', 'conv_w', 'conv_b', 'W_xp', 'W_dt', 'b_dt', 'A_log', 'D_skip', 'W_out', 'b_out', 'ln2_g', 'ln2_b', 'W_si', 'b_si', 'gates', 'alpha', 'W_so', 'b_so')}
    del _L1_attn_all

    def _L1_xattn_setup():
        import jax, jax.numpy as jnp
        import numpy as np
        D_MODEL = 256
        NUM_HEADS = 16
        D_K = D_MODEL // NUM_HEADS

        def _split_heads(x):
            B, S, _ = x.shape
            return x.reshape(B, S, NUM_HEADS, D_K).transpose(0, 2, 1, 3)
        key = jax.random.key(seed)
        ks = jax.random.split(key, 11)
        B, S = (2, 512)
        scale = 1.0 / np.sqrt(D_MODEL)
        inp = {'Q': jax.random.normal(ks[0], (B, S, D_MODEL), jnp.float32), 'K': jax.random.normal(ks[1], (B, S, D_MODEL), jnp.float32), 'V': jax.random.normal(ks[2], (B, S, D_MODEL), jnp.float32), 'W_q': jax.random.normal(ks[3], (D_MODEL, D_MODEL), jnp.float32) * scale, 'b_q': jnp.zeros((D_MODEL,), jnp.float32), 'W_k': jax.random.normal(ks[4], (D_MODEL, D_MODEL), jnp.float32) * scale, 'b_k': jnp.zeros((D_MODEL,), jnp.float32), 'W_v': jax.random.normal(ks[5], (D_MODEL, D_MODEL), jnp.float32) * scale, 'b_v': jnp.zeros((D_MODEL,), jnp.float32), 'W_o': jax.random.normal(ks[6], (D_MODEL, D_MODEL), jnp.float32) * scale, 'b_o': jnp.zeros((D_MODEL,), jnp.float32)}
        return inp
    _L1_xattn_all = _L1_xattn_setup()
    _L1_xattn_in = {k: v for k, v in _L1_xattn_all.items() if k in ('W_q', 'b_q', 'W_k', 'b_k', 'W_v', 'b_v', 'W_o', 'b_o')}
    del _L1_xattn_all

    def _L1_ffn_setup():
        import math
        import jax, jax.numpy as jnp
        import numpy as np
        D_MODEL = 256
        D_FF = 1024
        N_EXPERTS = 8
        CAPACITY_FACTOR = 1.25
        L, B = (128, 8)

        def _route(tokens, router_w):
            T = tokens.shape[0]
            E = router_w.shape[0]
            capacity = int(math.ceil(T / E * CAPACITY_FACTOR))
            logits = tokens @ router_w.T
            probs = jax.nn.softmax(logits, axis=-1)
            top1_idx = jnp.argmax(probs, axis=-1)
            top1_prob = jnp.max(probs, axis=-1)
            order = jnp.lexsort((-top1_prob, top1_idx))
            sorted_e = top1_idx[order]
            counts = jnp.bincount(top1_idx, length=E)
            start = jnp.cumsum(counts) - counts
            pos_in_group = jnp.arange(T) - start[sorted_e]
            keep_sorted = pos_in_group < capacity
            keep = jnp.zeros((T,), bool).at[order].set(keep_sorted)
            return jnp.where(keep, top1_idx, 0).astype(jnp.int32)
        key = jax.random.key(seed)
        ks = jax.random.split(key, 6)
        s_in = 1.0 / math.sqrt(D_MODEL)
        s_ff = 1.0 / math.sqrt(D_FF)
        return {'x': jax.random.normal(ks[0], (L, B, D_MODEL), dtype=jnp.float32), 'router_w': jax.random.uniform(ks[1], (N_EXPERTS, D_MODEL), minval=-s_in, maxval=s_in), 'W1': jax.random.uniform(ks[2], (N_EXPERTS, D_MODEL, D_FF), minval=-s_in, maxval=s_in), 'b1': jax.random.uniform(ks[3], (N_EXPERTS, D_FF), minval=-s_in, maxval=s_in), 'W2': jax.random.uniform(ks[4], (N_EXPERTS, D_FF, D_MODEL), minval=-s_ff, maxval=s_ff), 'b2': jax.random.uniform(ks[5], (N_EXPERTS, D_MODEL), minval=-s_ff, maxval=s_ff)}
    _L1_ffn_all = _L1_ffn_setup()
    _L1_ffn_in = {k: v for k, v in _L1_ffn_all.items() if k in ('router_w', 'W1', 'b1', 'W2', 'b2')}
    del _L1_ffn_all
    return {'x': x, 'ctx_1024': ctx_1024, 'mask_BxSxS2_bk1': mask_BxSxS2_bk1, 'L0_attn_W_qkv': _L0_attn_in['W_qkv'], 'L0_attn_W_z': _L0_attn_in['W_z'], 'L0_attn_W_b': _L0_attn_in['W_b'], 'L0_attn_W_a': _L0_attn_in['W_a'], 'L0_attn_dt_bias': _L0_attn_in['dt_bias'], 'L0_attn_A_log': _L0_attn_in['A_log'], 'L0_attn_conv_w': _L0_attn_in['conv_w'], 'L0_attn_norm_w': _L0_attn_in['norm_w'], 'L0_attn_W_out': _L0_attn_in['W_out'], 'L0_xattn_Wq': _L0_xattn_in['Wq'], 'L0_xattn_bq': _L0_xattn_in['bq'], 'L0_xattn_Wk': _L0_xattn_in['Wk'], 'L0_xattn_bk': _L0_xattn_in['bk'], 'L0_xattn_Wv': _L0_xattn_in['Wv'], 'L0_xattn_bv': _L0_xattn_in['bv'], 'L0_xattn_Wo': _L0_xattn_in['Wo'], 'L0_xattn_bo': _L0_xattn_in['bo'], 'L0_ffn_w1_w': _L0_ffn_in['w1_w'], 'L0_ffn_w1_s': _L0_ffn_in['w1_s'], 'L0_ffn_w2_w': _L0_ffn_in['w2_w'], 'L0_ffn_w2_s': _L0_ffn_in['w2_s'], 'L0_ffn_h1_w': _L0_ffn_in['h1_w'], 'L0_ffn_h1_s': _L0_ffn_in['h1_s'], 'L0_ffn_h2_w': _L0_ffn_in['h2_w'], 'L0_ffn_h2_s': _L0_ffn_in['h2_s'], 'L0_ffn_w3_w': _L0_ffn_in['w3_w'], 'L0_ffn_w3_s': _L0_ffn_in['w3_s'], 'L1_attn_ln1_g': _L1_attn_in['ln1_g'], 'L1_attn_ln1_b': _L1_attn_in['ln1_b'], 'L1_attn_W_in': _L1_attn_in['W_in'], 'L1_attn_b_in': _L1_attn_in['b_in'], 'L1_attn_conv_w': _L1_attn_in['conv_w'], 'L1_attn_conv_b': _L1_attn_in['conv_b'], 'L1_attn_W_xp': _L1_attn_in['W_xp'], 'L1_attn_W_dt': _L1_attn_in['W_dt'], 'L1_attn_b_dt': _L1_attn_in['b_dt'], 'L1_attn_A_log': _L1_attn_in['A_log'], 'L1_attn_D_skip': _L1_attn_in['D_skip'], 'L1_attn_W_out': _L1_attn_in['W_out'], 'L1_attn_b_out': _L1_attn_in['b_out'], 'L1_attn_ln2_g': _L1_attn_in['ln2_g'], 'L1_attn_ln2_b': _L1_attn_in['ln2_b'], 'L1_attn_W_si': _L1_attn_in['W_si'], 'L1_attn_b_si': _L1_attn_in['b_si'], 'L1_attn_gates': _L1_attn_in['gates'], 'L1_attn_alpha': _L1_attn_in['alpha'], 'L1_attn_W_so': _L1_attn_in['W_so'], 'L1_attn_b_so': _L1_attn_in['b_so'], 'L1_xattn_W_q': _L1_xattn_in['W_q'], 'L1_xattn_b_q': _L1_xattn_in['b_q'], 'L1_xattn_W_k': _L1_xattn_in['W_k'], 'L1_xattn_b_k': _L1_xattn_in['b_k'], 'L1_xattn_W_v': _L1_xattn_in['W_v'], 'L1_xattn_b_v': _L1_xattn_in['b_v'], 'L1_xattn_W_o': _L1_xattn_in['W_o'], 'L1_xattn_b_o': _L1_xattn_in['b_o'], 'L1_ffn_router_w': _L1_ffn_in['router_w'], 'L1_ffn_W1': _L1_ffn_in['W1'], 'L1_ffn_b1': _L1_ffn_in['b1'], 'L1_ffn_W2': _L1_ffn_in['W2'], 'L1_ffn_b2': _L1_ffn_in['b2']}

def reference(x, ctx_1024, mask_BxSxS2_bk1, L0_attn_W_qkv, L0_attn_W_z, L0_attn_W_b, L0_attn_W_a, L0_attn_dt_bias, L0_attn_A_log, L0_attn_conv_w, L0_attn_norm_w, L0_attn_W_out, L0_xattn_Wq, L0_xattn_bq, L0_xattn_Wk, L0_xattn_bk, L0_xattn_Wv, L0_xattn_bv, L0_xattn_Wo, L0_xattn_bo, L0_ffn_w1_w, L0_ffn_w1_s, L0_ffn_w2_w, L0_ffn_w2_s, L0_ffn_h1_w, L0_ffn_h1_s, L0_ffn_h2_w, L0_ffn_h2_s, L0_ffn_w3_w, L0_ffn_w3_s, L1_attn_ln1_g, L1_attn_ln1_b, L1_attn_W_in, L1_attn_b_in, L1_attn_conv_w, L1_attn_conv_b, L1_attn_W_xp, L1_attn_W_dt, L1_attn_b_dt, L1_attn_A_log, L1_attn_D_skip, L1_attn_W_out, L1_attn_b_out, L1_attn_ln2_g, L1_attn_ln2_b, L1_attn_W_si, L1_attn_b_si, L1_attn_gates, L1_attn_alpha, L1_attn_W_so, L1_attn_b_so, L1_xattn_W_q, L1_xattn_b_q, L1_xattn_W_k, L1_xattn_b_k, L1_xattn_W_v, L1_xattn_b_v, L1_xattn_W_o, L1_xattn_b_o, L1_ffn_router_w, L1_ffn_W1, L1_ffn_b1, L1_ffn_W2, L1_ffn_b2):
    import jax
    import jax.numpy as jnp

    def _L0_attn_ref(hidden_states, W_qkv, W_z, W_b, W_a, dt_bias, A_log, conv_w, norm_w, W_out):
        import jax, jax.numpy as jnp
        import numpy as np
        B, T, D = (2, 512, 256)
        HV, HK = (16, 8)
        DK, DV = (64, 64)
        K_DIM = HK * DK
        V_DIM = HV * DV
        CONV_DIM = 2 * K_DIM + V_DIM
        KS = 4
        EPS = 1e-06

        def _causal_conv_silu(x, w):
            xp = jnp.pad(x, ((0, 0), (KS - 1, 0), (0, 0)))
            y = sum((xp[:, i:i + x.shape[1], :] * w[:, i] for i in range(KS)))
            return jax.nn.silu(y)

        def _l2norm(x):
            return x * jax.lax.rsqrt(jnp.sum(x * x, -1, keepdims=True) + EPS)

        def _forward(hidden_states, W_qkv, W_z, W_b, W_a, dt_bias, A_log, conv_w, norm_w, W_out):
            b_, t_ = hidden_states.shape[:2]
            mixed_qkv = hidden_states @ W_qkv
            z = (hidden_states @ W_z).reshape(b_, t_, HV, DV)
            beta = jax.nn.sigmoid(hidden_states @ W_b)
            g = -jnp.exp(A_log) * jax.nn.softplus(hidden_states @ W_a + dt_bias)
            mixed_qkv = _causal_conv_silu(mixed_qkv, conv_w)
            q, k, v = jnp.split(mixed_qkv, [K_DIM, 2 * K_DIM], axis=-1)
            q = q.reshape(b_, t_, HK, DK)
            k = k.reshape(b_, t_, HK, DK)
            v = v.reshape(b_, t_, HV, DV)
            rep = HV // HK
            q = jnp.repeat(q, rep, axis=2)
            k = jnp.repeat(k, rep, axis=2)
            q = _l2norm(q) * DK ** (-0.5)
            k = _l2norm(k)
            qT = q.transpose(1, 0, 2, 3)
            kT = k.transpose(1, 0, 2, 3)
            vT = v.transpose(1, 0, 2, 3)
            gT = g.transpose(1, 0, 2)
            bT = beta.transpose(1, 0, 2)

            def step(S, xs):
                q_t, k_t, v_t, g_t, b_t = xs
                S = S * jnp.exp(g_t)[..., None, None]
                kv = jnp.einsum('bhk,bhkv->bhv', k_t, S)
                S = S + jnp.einsum('bhk,bhv->bhkv', k_t, (v_t - kv) * b_t[..., None])
                o_t = jnp.einsum('bhk,bhkv->bhv', q_t, S)
                return (S, o_t)
            S0 = jnp.zeros((b_, HV, DK, DV), jnp.float32)
            _, oT = jax.lax.scan(step, S0, (qT, kT, vT, gT, bT))
            o = oT.transpose(1, 0, 2, 3)
            var = jnp.mean(o * o, axis=-1, keepdims=True)
            o = o * jax.lax.rsqrt(var + EPS) * norm_w * jax.nn.silu(z)
            return o.reshape(b_, t_, V_DIM) @ W_out
        return _forward(hidden_states, W_qkv, W_z, W_b, W_a, dt_bias, A_log, conv_w, norm_w, W_out)

    def _L0_xattn_ref(Q, K, V, mask, Wq, bq, Wk, bk, Wv, bv, Wo, bo):
        import jax, jax.numpy as jnp
        import numpy as np
        B, T, C = (2, 512, 256)
        H, DQK, DV = (16, 64, 64)

        def _split_heads(x, d):
            b, t, _ = x.shape
            return x.reshape(b, t, H, d).transpose(0, 2, 1, 3)
        q = _split_heads(Q @ Wq + bq, DQK)
        k = _split_heads(K @ Wk + bk, DQK)
        v = _split_heads(V @ Wv + bv, DV)
        scores = jnp.einsum('bhqd,bhkd->bhqk', q, k) / jnp.sqrt(jnp.float32(DQK))
        scores = jnp.where(mask[:, None, :, :], -jnp.inf, scores)
        weights = jax.nn.softmax(scores, axis=-1)
        attn = jnp.einsum('bhqk,bhkd->bhqd', weights, v)
        out = attn.transpose(0, 2, 1, 3).reshape(Q.shape[0], Q.shape[1], H * DV)
        return out @ Wo + bo

    def _L0_ffn_ref(x, w1_w, w1_s, w2_w, w2_s, h1_w, h1_s, h2_w, h2_s, w3_w, w3_s):
        import jax, jax.numpy as jnp
        import numpy as np
        D_IN, D_HID = (256, 1024)

        def _ternary(key, shape):
            return jax.random.randint(key, shape, -1, 2).astype(jnp.float32)

        def _tlin(x, w, s):
            return jnp.einsum('bsi,oi->bso', x, w) * s
        h = jax.nn.silu(_tlin(x, w1_w, w1_s)) * _tlin(x, w2_w, w2_s)
        h = jax.nn.gelu(_tlin(h, h1_w, h1_s), approximate=False)
        h = jax.nn.gelu(_tlin(h, h2_w, h2_s), approximate=False)
        return _tlin(h, w3_w, w3_s)

    def _L1_attn_ref(x, ln1_g, ln1_b, W_in, b_in, conv_w, conv_b, W_xp, W_dt, b_dt, A_log, D_skip, W_out, b_out, ln2_g, ln2_b, W_si, b_si, gates, alpha, W_so, b_so):
        import jax, jax.numpy as jnp
        import numpy as np
        from jax import lax
        B, S, D = (2, 256, 256)
        N = 16
        EXPAND = 2
        DI = EXPAND * D
        K = 4
        H = 16
        DH = D // H
        DT_RANK = D // 16
        SOL_DT = 0.1

        def _ln(x, g, b):
            mu = jnp.mean(x, -1, keepdims=True)
            var = jnp.var(x, -1, keepdims=True)
            return (x - mu) / jnp.sqrt(var + 1e-05) * g + b

        def _forward(x, ln1_g, ln1_b, W_in, b_in, conv_w, conv_b, W_xp, W_dt, b_dt, A_log, D_skip, W_out, b_out, ln2_g, ln2_b, W_si, b_si, gates, alpha, W_so, b_so):
            b, s, d = x.shape
            u = _ln(x, ln1_g, ln1_b)
            xz = u @ W_in + b_in
            xp, z = jnp.split(xz, 2, axis=-1)
            xt = xp.transpose(0, 2, 1)
            yc = lax.conv_general_dilated(xt, conv_w[:, None, :], (1,), [(K - 1, 0)], feature_group_count=DI, dimension_numbers=('NCW', 'OIW', 'NCW'))
            xc = jax.nn.silu(yc.transpose(0, 2, 1) + conv_b)
            dbc = xc @ W_xp
            dtr, Bs, Cs = jnp.split(dbc, [DT_RANK, DT_RANK + N], axis=-1)
            dt = jax.nn.softplus(dtr @ W_dt + b_dt)
            A = -jnp.exp(A_log)
            dA = jnp.exp(dt[..., None] * A)
            dBx = (dt * xc)[..., None] * Bs[:, :, None, :]

            def step(h, inp):
                dA_t, dBx_t, C_t = inp
                h = dA_t * h + dBx_t
                y = jnp.einsum('bdn,bn->bd', h, C_t)
                return (h, y)
            h0 = jnp.zeros((b, DI, N), x.dtype)
            xs = (dA.transpose(1, 0, 2, 3), dBx.transpose(1, 0, 2, 3), Cs.transpose(1, 0, 2))
            _, ys = lax.scan(step, h0, xs)
            y = ys.transpose(1, 0, 2)
            y = (y + xc * D_skip) * jax.nn.silu(z)
            x = x + y @ W_out + b_out
            v = _ln(x, ln2_g, ln2_b)
            uu = (v @ W_si + b_si).reshape(b, s, H, DH)
            up = jnp.pad(uu, ((0, 0), (2, 2), (0, 0), (0, 0)), mode='edge')
            ux = (up[:, 3:-1] - up[:, 1:-3]) * 0.5
            uxx = up[:, 3:-1] - 2.0 * uu + up[:, 1:-3]
            uxxx = (up[:, 4:] - 2.0 * up[:, 3:-1] + 2.0 * up[:, 1:-3] - up[:, :-4]) * 0.5
            sg = jnp.sin(uu)
            kdv = -6.0 * uu * ux - uxxx
            hj = (1.0 + alpha[None, None, :, None] * uu) * uxx
            du = gates[None, None, :, 0:1] * sg + gates[None, None, :, 1:2] * kdv + gates[None, None, :, 2:3] * hj
            sol = (SOL_DT * du).reshape(b, s, d) @ W_so + b_so
            return x + sol
        return _forward(x, ln1_g, ln1_b, W_in, b_in, conv_w, conv_b, W_xp, W_dt, b_dt, A_log, D_skip, W_out, b_out, ln2_g, ln2_b, W_si, b_si, gates, alpha, W_so, b_so)

    def _L1_xattn_ref(Q, K, V, W_q, b_q, W_k, b_k, W_v, b_v, W_o, b_o):
        import jax, jax.numpy as jnp
        import numpy as np
        D_MODEL = 256
        NUM_HEADS = 16
        D_K = D_MODEL // NUM_HEADS

        def _split_heads(x):
            B, S, _ = x.shape
            return x.reshape(B, S, NUM_HEADS, D_K).transpose(0, 2, 1, 3)
        q = _split_heads(Q @ W_q.T + b_q)
        k = _split_heads(K @ W_k.T + b_k)
        v = _split_heads(V @ W_v.T + b_v)
        scores = jnp.einsum('bhqd,bhkd->bhqk', q, k) / jnp.sqrt(jnp.float32(D_K))
        probs = jax.nn.softmax(scores, axis=-1)
        ctx = jnp.einsum('bhqk,bhkd->bhqd', probs, v)
        B, H, S, d = ctx.shape
        ctx = ctx.transpose(0, 2, 1, 3).reshape(B, S, H * d)
        return ctx @ W_o.T + b_o

    def _L1_ffn_ref(x, router_w, W1, b1, W2, b2):
        import math
        import jax, jax.numpy as jnp
        import numpy as np
        D_MODEL = 256
        D_FF = 1024
        N_EXPERTS = 8
        CAPACITY_FACTOR = 1.25
        L, B = (128, 8)

        def _route(tokens, router_w):
            T = tokens.shape[0]
            E = router_w.shape[0]
            capacity = int(math.ceil(T / E * CAPACITY_FACTOR))
            logits = tokens @ router_w.T
            probs = jax.nn.softmax(logits, axis=-1)
            top1_idx = jnp.argmax(probs, axis=-1)
            top1_prob = jnp.max(probs, axis=-1)
            order = jnp.lexsort((-top1_prob, top1_idx))
            sorted_e = top1_idx[order]
            counts = jnp.bincount(top1_idx, length=E)
            start = jnp.cumsum(counts) - counts
            pos_in_group = jnp.arange(T) - start[sorted_e]
            keep_sorted = pos_in_group < capacity
            keep = jnp.zeros((T,), bool).at[order].set(keep_sorted)
            return jnp.where(keep, top1_idx, 0).astype(jnp.int32)
        Lx, Bx, D = x.shape
        T = Lx * Bx
        E = router_w.shape[0]
        tokens = x.reshape(T, D)
        final_e = _route(tokens, router_w)
        out = jnp.zeros_like(tokens)
        for e in range(E):
            h = jax.nn.relu(tokens @ W1[e] + b1[e])
            y = h @ W2[e] + b2[e]
            out = out + jnp.where((final_e == e)[:, None], y, 0.0)
        return out.reshape(Lx, Bx, D)
    x = x + _L0_attn_ref(_layernorm(x, axis=-1), L0_attn_W_qkv, L0_attn_W_z, L0_attn_W_b, L0_attn_W_a, L0_attn_dt_bias, L0_attn_A_log, L0_attn_conv_w, L0_attn_norm_w, L0_attn_W_out)
    x = x + _L0_xattn_ref(_layernorm(x, axis=-1), ctx_1024, ctx_1024, mask_BxSxS2_bk1, L0_xattn_Wq, L0_xattn_bq, L0_xattn_Wk, L0_xattn_bk, L0_xattn_Wv, L0_xattn_bv, L0_xattn_Wo, L0_xattn_bo)
    x = x + _L0_ffn_ref(_layernorm(x, axis=-1), L0_ffn_w1_w, L0_ffn_w1_s, L0_ffn_w2_w, L0_ffn_w2_s, L0_ffn_h1_w, L0_ffn_h1_s, L0_ffn_h2_w, L0_ffn_h2_s, L0_ffn_w3_w, L0_ffn_w3_s)
    x = x + _L1_attn_ref(_layernorm(x, axis=-1), L1_attn_ln1_g, L1_attn_ln1_b, L1_attn_W_in, L1_attn_b_in, L1_attn_conv_w, L1_attn_conv_b, L1_attn_W_xp, L1_attn_W_dt, L1_attn_b_dt, L1_attn_A_log, L1_attn_D_skip, L1_attn_W_out, L1_attn_b_out, L1_attn_ln2_g, L1_attn_ln2_b, L1_attn_W_si, L1_attn_b_si, L1_attn_gates, L1_attn_alpha, L1_attn_W_so, L1_attn_b_so)
    x = x + _L1_xattn_ref(_layernorm(x, axis=-1), ctx_1024, ctx_1024, L1_xattn_W_q, L1_xattn_b_q, L1_xattn_W_k, L1_xattn_b_k, L1_xattn_W_v, L1_xattn_b_v, L1_xattn_W_o, L1_xattn_b_o)
    x = x + _L1_ffn_ref(_layernorm(x, axis=-1), L1_ffn_router_w, L1_ffn_W1, L1_ffn_b1, L1_ffn_W2, L1_ffn_b2)
    return x

_drawn_inputs = setup_inputs


def setup_inputs(seed=0):
    import zlib

    import numpy as np

    out = dict(_drawn_inputs(seed))
    spreads = {'L0_attn_dt_bias': (1.0, 0.2),
     'L0_attn_norm_w': (1.0, 0.2),
     'L0_xattn_bq': (0.0, 0.1),
     'L0_xattn_bk': (0.0, 0.1),
     'L0_xattn_bv': (0.0, 0.1),
     'L0_xattn_bo': (0.0, 0.1),
     'L1_attn_ln1_g': (1.0, 0.2),
     'L1_attn_ln1_b': (0.0, 0.1),
     'L1_attn_b_in': (0.0, 0.1),
     'L1_attn_conv_b': (0.0, 0.1),
     'L1_attn_b_dt': (-4.599999904632568, 0.2),
     'L1_attn_D_skip': (1.0, 0.2),
     'L1_attn_b_out': (0.0, 0.1),
     'L1_attn_ln2_g': (1.0, 0.2),
     'L1_attn_ln2_b': (0.0, 0.1),
     'L1_attn_b_si': (0.0, 0.1),
     'L1_attn_b_so': (0.0, 0.1),
     'L1_xattn_b_q': (0.0, 0.1),
     'L1_xattn_b_k': (0.0, 0.1),
     'L1_xattn_b_v': (0.0, 0.1),
     'L1_xattn_b_o': (0.0, 0.1)}
    factors = {}
    for name, (base, spread) in spreads.items():
        noise = np.random.default_rng([zlib.crc32(name.encode()), seed]).standard_normal(out[name].shape)
        drawn = base * np.exp(spread * noise) if base else spread * noise
        out[name] = jnp.asarray(drawn.astype(out[name].dtype))
    for name, factor in factors.items():
        out[name] = (out[name] * factor).astype(out[name].dtype)
    return out
```

```python
from contextlib import ExitStack

import numpy as np

import concourse.bass as bass
from concourse import mybir

ALU = mybir.AluOpType
ACT = mybir.ActivationFunctionType
AX = mybir.AxisListType.X
F32 = mybir.dt.float32
F32R = mybir.dt.float32r
BF16 = mybir.dt.bfloat16
U8 = mybir.dt.uint8
I32 = mybir.dt.int32

P = 128
B, T, D = 4, 512, 256
DC = D // P
NT = B * T // P
TB = T // P
S2 = 1601
KT = -(-S2 // P)
SW = -(-S2 // 4)
LAST = S2 - (KT - 1) * P
NEG = -1.0e30
ds = bass.ds


class Scope:

    def __init__(self, nc, name):
        self.nc, self.name, self.stack, self.sems = nc, name, ExitStack(), []

    def __enter__(self):
        return self

    def __exit__(self, *failure):
        self.stack.close()
        if self.sems:
            self.nc.clear_and_free_semaphores(self.sems)
            self.nc.all_engine_barrier()

    def sb(self, name, shape, dt=F32):
        return self.stack.enter_context(self.nc.sbuf_tensor(f"{self.name}_{name}", shape, dt))

    def ps(self, name, shape, dt=F32):
        return self.stack.enter_context(self.nc.psum_tensor(f"{self.name}_{name}", shape, dt))

    def sem(self, name):
        self.sems.append(self.nc.alloc_semaphore(f"{self.name}_{name}"))
        return self.sems[-1]

    def block(self):
        return self.stack.enter_context(self.nc.Block())


class Chain:

    def __init__(self, eng, sem, per=0, base=0):
        self.eng, self.sem, self.per, self.n, self.turn, self.base = eng, sem, per, 0, 0, base

    def start(self, turn):
        assert self.n in (0, self.per), (self.n, self.per)
        self.turn, self.n = turn, 0

    def link(self, ins):
        self.n += 1
        ins.then_inc(self.sem, 1)
        self.eng.wait_ge(self.sem, self.turn * self.per + (self.base + self.n))

    def close(self):
        assert self.n == self.per, (self.n, self.per)


def constants(nc, c):
    with Scope(nc, "const") as s:
        made = s.sem("made")
        loaded = s.sem("loaded")
        block = s.block()

        @block.gpsimd
        def _(pool):
            nc.gpsimd.memset(c.ident[:], 0.0).then_inc(made, 1)
            nc.gpsimd.memset(c.ones[:], 1.0).then_inc(made, 1)
            nc.gpsimd.memset(c.eps[:], 1e-5).then_inc(made, 1)
            pool.wait_ge(made, 1)
            nc.gpsimd.affine_select(out=c.ident[:], in_=c.ident[:], compare_op=ALU.not_equal, fill=1.0,
                                    base=0, pattern=[[-1, P]], channel_multiplier=1).then_inc(made, 1)

        @block.sync
        def _(sp):
            sp.dma_start(c.x[:], c.dram["x"]).then_inc(loaded, 16)
            sp.wait_ge(loaded, 16)


def layernorm(nc, c, name, src, dst, gain=None, shift=None, keep=None):
    GROUPS = NT // 4
    FREE = 2
    with Scope(nc, name) as s:
        stats = s.sb("stats", [P, 2, 4, 6])
        mv = s.sb("mv", [P, 2, 4, 2])
        std = s.sb("std", [P, 2, 4])
        rstd = s.sb("rstd", [P, 2, 4])
        xn = s.sb("xn", [P, 2, 4, D])
        turned_ps = [s.ps(f"turned{k}", [P, DC, 512]) for k in range(2)]
        vec = s.sem("vec")
        stats_ready = s.sem("stats_ready")
        std_ready = s.sem("std_ready")
        xn_ready = s.sem("xn_ready")
        turned = s.sem("turned")
        copied = s.sem("copied")
        passed = s.sem("passed")
        block = s.block()

        @block.vector
        def _(dve):
            chain = Chain(dve, vec, per=6 if keep is not None else 4)
            with dve.Fori(0, GROUPS // 2) as i:
                chain.start(i)
                for k in range(2):
                    tile = [ds((i * 2 + k) * 4 + t, 1) for t in range(4)]
                    for t in range(4):
                        last = nc.vector.bn_stats(stats[:, k, t, :], src[:, tile[t], :])
                    chain.link(last)
                    dve.sem_inc(passed, 1)
                    for t in range(4):
                        last = nc.vector.bn_aggr(mv[:, k, t, :], stats[:, k, t, :])
                    last.then_inc(stats_ready, 1)
                    dve.wait_ge(std_ready, i * 2 + (k + 1))
                    chain.link(nc.vector.reciprocal(rstd[:, k, :], std[:, k, :]))
                    dve.wait_ge(turned, i * 2 + (k + FREE - 1))
                    for t in range(4):
                        last = nc.vector.tensor_scalar(xn[:, k, t, :], src[:, tile[t], :],
                                                       mv[:, k, t, 0:1], rstd[:, k, t:t + 1],
                                                       ALU.subtract, ALU.mult)
                    last.then_inc(xn_ready, 1)
                    if keep is not None:
                        for t in range(4):
                            last = nc.vector.tensor_scalar(keep[:, tile[t], :], src[:, tile[t], :],
                                                           mv[:, k, t, 0:1], rstd[:, k, t:t + 1],
                                                           ALU.subtract, ALU.mult)
                        chain.link(last)
                chain.close()

        @block.scalar
        def _(act):
            with act.Fori(0, GROUPS // 2) as i:
                for k in range(2):
                    act.wait_ge(stats_ready, i * 2 + (k + 1))
                    nc.scalar.activation(std[:, k, :], mv[:, k, :, 1], ACT.Sqrt, bias=c.eps[:]).then_inc(std_ready, 1)
                    act.wait_ge(turned, i * 2 + (k + 1 + FREE))
                    for d in range(DC):
                        out = dst[:, d, ds((i * 2 + k) * 512, 512)]
                        last = nc.scalar.activation(out, turned_ps[k][:, d, :], ACT.Identity,
                                                    bias=shift[:, d:d + 1] if shift is not None else 0.0,
                                                    scale=gain[:, d:d + 1] if gain is not None else 1.0)
                    last.then_inc(copied, 1)

        @block.tensor
        def _(pe):
            pe.sem_inc(turned, FREE)
            pe.sem_inc(copied, FREE)
            with pe.Fori(0, GROUPS // 2) as i:
                for k in range(2):
                    pe.wait_ge(xn_ready, i * 2 + (k + 1))
                    pe.wait_ge(copied, i * 2 + (k + FREE - 1))
                    for d in range(DC):
                        for t in range(4):
                            last = nc.tensor.transpose(turned_ps[k][:, d, t * P:(t + 1) * P],
                                                       xn[:, k, t, d * P:(d + 1) * P], c.ident[:])
                    last.then_inc(turned, 1)


HV, HK, DK = 16, 8, 64
LEVELS = 7
KOFF, VOFF = HK * DK, 2 * HK * DK
CONV = 4


def lay_gated_delta_net(a, rows, cols):
    p, f = np.arange(P)[:, None], np.arange(P)[None, :]
    levels = np.stack([(p >> s + 1 == f >> s + 1) & (p >> s & 1 == 1) & (f >> s & 1 == 0)
                       for s in range(LEVELS)], 1).astype(np.float32)
    return {
        "gdn_wqkv": rows(a["L0_attn_W_qkv"]),
        "gdn_wz": rows(a["L0_attn_W_z"]),
        "gdn_wba": rows(np.concatenate([a["L0_attn_W_b"], a["L0_attn_W_a"]], 1)),
        "gdn_wout": rows(a["L0_attn_W_out"]),
        "gdn_conv": a["L0_attn_conv_w"].reshape(-1, P, CONV).transpose(1, 0, 2),
        "gdn_dt_bias": a["L0_attn_dt_bias"],
        "gdn_A_log": a["L0_attn_A_log"],
        "gdn_norm": a["L0_attn_norm_w"],
        "gdn_levels": levels,
        "gdn_upto": (p <= f).astype(np.float32),
    }


def gated_delta_net(nc, c):
    layernorm(nc, c, "gdn_ln", c.x, c.xnT)
    NM = 2 * HK * DK // P + HV * DK // P
    HG = HV // 4
    NZ = HV * DK // 512
    with Scope(nc, "gdn") as s:
        wqkv = s.sb("wqkv", [P, DC, NM * P])
        wz = s.sb("wz", [P, DC, HV * DK])
        wba = s.sb("wba", [P, DC, 2 * HV])
        wout = s.sb("wout", [P, HV * DK // P, D])
        convw = s.sb("convw", [P, NM, CONV])
        dt_bias = s.sb("dt_bias", [P, HV])
        neg_a = s.sb("neg_a", [P, HV])
        norm_w = s.sb("norm_w", [P, DK])
        levels = s.sb("levels", [P, LEVELS, P])
        upto = s.sb("upto", [P, P])
        eps = s.sb("eps", [P, 1])
        xb = s.sb("xb", [P, DC, T])
        conv = s.sb("conv", [P, 2, T])
        act_ct = s.sb("act_ct", [P, 2, T])
        qkv = s.sb("qkv", [P, TB, NM * P])
        gate = s.sb("gate", [P, TB, HV * DK])
        o = s.sb("o", [P, TB, HV * DK])
        osq = qkv[:, 0:TB // 2, :].rearrange("p a (b n) -> p (a b) n", n=HV * DK)
        oT = qkv[:, TB // 2:TB, :].rearrange("p a (b n) -> p (a b) n", n=T)
        col = lambda n, h=HV: s.sb(n, [P, TB, h])
        beta, g, G, eG, eGl, eGend = (col(n) for n in ("beta", "g", "G", "eG", "eGl", "eGend"))
        u1, u2, u3 = (col(n) for n in ("u1", "u2", "u3"))
        k_in, k_out, q_in = (col(n) for n in ("k_in", "k_out", "q_in"))
        ss = col("ss")
        rn = col("rn")
        Kn, Qn = (s.sb(n, [P, 2, 2, DK]) for n in ("Kn", "Qn"))
        Kb, Kd, Qe, Vb = (s.sb(n, [P, 2, 4, DK]) for n in ("Kb", "Kd", "Qe", "Vb"))
        Ug = s.sb("Ug", [P, 2, 4, P])
        kqT = s.sb("kqT", [P, 6, P])
        dd = s.sb("dd", [P, 4, P])
        ad = s.sb("ad", [P, 4, P])
        E = s.sb("E", [P, 4, P])
        EU = s.sb("EU", [P, 4, P])
        Tm = s.sb("Tm", [P, 2, 2, P])
        PT = s.sb("PT", [P, 4, P])
        M = s.sb("M", [P, 4, LEVELS, P])
        XX = s.sb("XX", [P, 2, 2, 2, P])
        Y = s.sb("Y", [P, 4, P])
        Bm = s.sb("Bm", [P, 4, DK])
        U = s.sb("U", [P, 4, DK])
        S = s.sb("S", [P, 2, P])

        tps = s.ps("tps", [P, 8, P])
        wps = [s.ps(f"wps{k}", [P, 2, 2, P]) for k in range(2)]
        gps = s.ps("gps", [P, 4, P])
        kps = s.ps("kps", [P, 2, 2, P])
        yps = [s.ps(f"yps{k}", [P, 4, P]) for k in range(2)]
        proj = [tps[:, 0:4, :].rearrange("p a b -> p (a b)"), tps[:, 4:8, :].rearrange("p a b -> p (a b)")]
        zps = [gps[:].rearrange("p a b -> p (a b)"), kps[:].rearrange("p a b c -> p (a b c)")]
        trps = [w[:].rearrange("p a b c -> p (a b) c") for w in wps]
        ba_ps = yps[0][:, 0, :].rearrange("p (t h) -> p t h", t=TB)
        G_ps, end_ps = (yps[1][:, n, 0:TB * HV].rearrange("p (t h) -> p t h", t=TB) for n in range(2))
        m0_ps = wps[0][:]
        r_ps = gps[:, 0:2, :]
        u_ps = gps[:, 2:4, :].rearrange("p a (b d) -> p (a b) d", b=2)
        o_ps = kps[:, 0, :, :].rearrange("p a b -> p (a b)")
        s_ps = gps[:, 0:2, :]

        loaded = s.sem("loaded")
        ready0 = s.sem("ready0")
        xb_ready = s.sem("xb_ready")
        proj_ready = s.sem("proj_ready")
        conv_ready = s.sem("conv_ready")
        act_ready = s.sem("act_ready")
        tr_ready = s.sem("tr_ready")
        tr_copied = s.sem("tr_copied")
        z_ready = s.sem("z_ready")
        z_copied = s.sem("z_copied")
        ba_ready = s.sem("ba_ready")
        gate_sum = s.sem("gate_sum")
        softplus_ready = s.sem("softplus_ready")
        g_ready = s.sem("g_ready")
        Gsum_ready = s.sem("Gsum_ready")
        gl_ready = s.sem("gl_ready")
        exp_ready = s.sem("exp_ready")
        sq_ready = s.sem("sq_ready")
        ss_ready = s.sem("ss_ready")
        len_ready = s.sem("len_ready")
        vec_a = s.sem("vec_a")
        vec_t = s.sem("vec_t")
        vec_e = s.sem("vec_e")
        act_a = s.sem("act_a")
        act_t = s.sem("act_t")
        meet = s.sem("meet")
        prep_ready = s.sem("prep_ready")
        turned = s.sem("turned")
        kqT_ready = s.sem("kqT_ready")
        grow_ready = s.sem("grow_ready")
        kk_low = s.sem("kk_low")
        kk_ready = s.sem("kk_ready")
        dd_ready = s.sem("dd_ready")
        E_ready = s.sem("E_ready")
        EU_ready = s.sem("EU_ready")
        M_ready = s.sem("M_ready")
        PT_ready = s.sem("PT_ready")
        Tm_ready = s.sem("Tm_ready")
        m0_ready = s.sem("m0_ready")
        X0_ready = s.sem("X0_ready")
        y_ready = s.sem("y_ready")
        y_copied = s.sem("y_copied")
        w_ready = s.sem("w_ready")
        X_ready = s.sem("X_ready")
        r_ready = s.sem("r_ready")
        B_ready = s.sem("B_ready")
        u_ready = s.sem("u_ready")
        U_ready = s.sem("U_ready")
        o_ready = s.sem("o_ready")
        o_copied = s.sem("o_copied")
        s_ready = s.sem("s_ready")
        S_ready = s.sem("S_ready")
        osq_ready = s.sem("osq_ready")
        ovar_ready = s.sem("ovar_ready")
        ostd_ready = s.sem("ostd_ready")
        on_ready = s.sem("on_ready")
        oT_ready = s.sem("oT_ready")
        oT_copied = s.sem("oT_copied")
        out_ready = s.sem("out_ready")
        added = s.sem("added")
        passed = s.sem("passed")
        block = s.block()
        LOADS = 10 * 16
        WORKERS = 4
        STAGES = 3

        def stage_end(eng, b, stage):
            eng.drain().then_inc(meet, 1)
            eng.wait_ge(meet, b * (STAGES * WORKERS) + (stage + 1) * WORKERS)
            eng.sem_inc(passed, 1)

        @block.sync
        def _(sp):
            for dst, src in ((wqkv, "wqkv"), (convw, "conv"), (wz, "wz"), (wba, "wba"), (levels, "levels"),
                             (upto, "upto"), (wout, "wout")):
                sp.dma_start(dst[:], c.dram[f"gdn_{src}"]).then_inc(loaded, 16)
            for dst, src in ((dt_bias, "dt_bias"), (neg_a, "A_log"), (norm_w, "norm")):
                sp.dma_start(dst[:], c.dram[f"gdn_{src}"].partition_broadcast(P)).then_inc(loaded, 16)

        @block.gpsimd
        def _(pool):
            nc.gpsimd.memset(eps[:], 1e-6).then_inc(ready0, 1)
            pool.wait_ge(loaded, LOADS)
            with pool.Fori(0, B) as b:
                pool.wait_ge(z_copied, b * (TB * NZ) + TB * NZ)
                for t in range(TB):
                    zt = gate[:, t, :].rearrange("p (h d) -> p h d", d=DK)
                    nc.gpsimd.tensor_tensor(zt, zt, norm_w[:].unsqueeze(1).broadcast_to([P, HV, DK]), ALU.mult)
                stage_end(pool, b, 0)
                with pool.Fori(0, HG) as hg:
                    for ch in range(TB):
                        pool.wait_ge(E_ready, (b * HG + hg) * TB + (ch + 1))
                        nc.gpsimd.tensor_tensor(EU[:], E[:], upto[:].unsqueeze(1).broadcast_to([P, 4, P]),
                                                ALU.mult).then_inc(EU_ready, 1)
                stage_end(pool, b, 1)
                stage_end(pool, b, 2)

        @block.scalar
        def _(act):
            act.wait_ge(loaded, LOADS)
            act.wait_ge(ready0, 1)
            nc.scalar.activation(neg_a[:], neg_a[:], ACT.Exp).then_inc(ready0, 1)
            with act.Fori(0, B) as b:
                chain = Chain(act, act_a, per=2)
                chain.start(b)
                nc.scalar.activation(xb[:], c.xnT[:, :, ds(b * T, T)], ACT.Copy).then_inc(xb_ready, 1)

                def turn_copy(m):
                    act.wait_ge(tr_ready, b * NM + (m + 1))
                    nc.scalar.activation(qkv[:, :, m * P:(m + 1) * P], trps[m % 2], ACT.Copy).then_inc(tr_copied, 1)

                for m in range(NM):
                    act.wait_ge(conv_ready, b * NM + (m + 1))
                    if m >= 2:
                        act.wait_ge(tr_ready, b * NM + (m - 1))
                    nc.scalar.activation(act_ct[:, m % 2, :], conv[:, m % 2, :], ACT.Silu).then_inc(act_ready, 1)
                    if m >= 1:
                        turn_copy(m - 1)
                turn_copy(NM - 1)
                for n in range(TB * NZ):
                    act.wait_ge(z_ready, b * (TB * NZ) + (n + 1))
                    nc.scalar.activation(gate[:, n // NZ, (n % NZ) * 512:(n % NZ + 1) * 512], zps[n % 2],
                                         ACT.Silu).then_inc(z_copied, 1)
                act.wait_ge(gate_sum, b + 1)
                nc.scalar.activation(u1[:], u1[:], ACT.Exp, scale=-1.0)
                chain.link(nc.scalar.activation(u3[:], u2[:], ACT.Abs))
                chain.link(nc.scalar.activation(u3[:], u3[:], ACT.Exp, scale=-1.0))
                nc.scalar.activation(u3[:], u3[:], ACT.Ln, bias=1.0).then_inc(softplus_ready, 1)
                act.wait_ge(gl_ready, b + 1)
                nc.scalar.activation(eG[:], G[:], ACT.Exp)
                nc.scalar.activation(eGend[:], eGend[:], ACT.Exp)
                nc.scalar.activation(eGl[:], u1[:], ACT.Exp).then_inc(exp_ready, 1)
                nc.scalar.activation(o[:], qkv[:, :, 0:VOFF], ACT.Square).then_inc(sq_ready, 1)
                act.wait_ge(ss_ready, b + 1)
                nc.scalar.activation(ss[:], ss[:], ACT.Sqrt, bias=eps[:]).then_inc(len_ready, 1)
                chain.close()
                stage_end(act, b, 0)
                with act.Fori(0, HG) as hg:
                    turn = b * HG + hg
                    chain = Chain(act, act_t, per=TB)
                    chain.start(turn)
                    for ch in range(TB):
                        act.wait_ge(turned, turn * TB + (ch + 1))
                        nc.scalar.activation(kqT[:], tps[:, 0:6, :], ACT.Copy).then_inc(kqT_ready, 1)
                        act.wait_ge(dd_ready, turn * TB + (ch + 1))
                        chain.link(nc.scalar.activation(ad[:], dd[:], ACT.Abs))
                        nc.scalar.activation(E[:], ad[:], ACT.Exp, scale=-1.0).then_inc(E_ready, 1)
                        for lv in range(1, LEVELS):
                            for half in range(2):
                                act.wait_ge(y_ready, turn * (TB * 12) + (ch * 12 + (lv - 1) * 2 + half + 1))
                                nc.scalar.activation(Y[:, 2 * half:2 * half + 2, :], yps[half][:, 0:2, :], ACT.Copy).then_inc(y_copied, 1)
                        act.wait_ge(u_ready, turn * TB + (ch + 1))
                        nc.scalar.activation(U[:], u_ps, ACT.Copy).then_inc(U_ready, 1)
                        act.wait_ge(o_ready, turn * TB + (ch + 1))
                        nc.scalar.activation(o[:, ch, ds(hg * (4 * DK), 4 * DK)], o_ps, ACT.Copy).then_inc(o_copied, 1)
                    chain.close()
                stage_end(act, b, 1)
                nc.scalar.activation(osq, o[:], ACT.Square).then_inc(osq_ready, 1)
                act.wait_ge(ovar_ready, b + 1)
                nc.scalar.activation(ss[:], ss[:], ACT.Sqrt, bias=eps[:], scale=1.0 / DK).then_inc(ostd_ready, 1)
                for m in range(HV * DK // P):
                    act.wait_ge(oT_ready, b * (HV * DK // P) + (m + 1))
                    nc.scalar.activation(oT[:, m, :], proj[m % 2], ACT.Copy).then_inc(oT_copied, 1)
                stage_end(act, b, 2)

        @block.vector
        def _(dve):
            dve.wait_ge(loaded, LOADS)
            dve.wait_ge(ready0, 2)
            nc.vector.tensor_scalar(neg_a[:], neg_a[:], -1.0, None, ALU.mult).then_inc(ready0, 1)
            dve.wait_ge(ready0, 3)
            with dve.Fori(0, B) as b:
                chain = Chain(dve, vec_a, per=NM * 3 + 7)
                chain.start(b)
                for m in range(NM):
                    dve.wait_ge(proj_ready, b * NM + (m + 1))
                    if m >= 2:
                        dve.wait_ge(act_ready, b * NM + (m - 1))
                    y, x = conv[:, m % 2, :], proj[m % 2]
                    chain.link(nc.vector.tensor_scalar(y, x, convw[:, m, CONV - 1:CONV], None, ALU.mult))
                    for back in range(1, CONV):
                        last = nc.vector.scalar_tensor_tensor(
                            out=y[:, back:], in0=x[:, :T - back], scalar=convw[:, m, CONV - 1 - back:CONV - back],
                            in1=y[:, back:], op0=ALU.mult, op1=ALU.add)
                        if back < CONV - 1:
                            chain.link(last)
                    last.then_inc(conv_ready, 1)
                heads = lambda v: v.unsqueeze(1).broadcast_to([P, TB, HV])
                dve.wait_ge(ba_ready, b + 1)
                nc.vector.tensor_copy(u1[:], ba_ps[:, :, 0:HV])
                nc.vector.tensor_tensor(u2[:], ba_ps[:, :, HV:2 * HV], heads(dt_bias[:]), ALU.add).then_inc(gate_sum, 1)
                dve.wait_ge(softplus_ready, b + 1)
                chain.link(nc.vector.tensor_scalar(u1[:], u1[:], 1.0, None, ALU.add))
                chain.link(nc.vector.reciprocal(beta[:], u1[:]))
                chain.link(nc.vector.scalar_tensor_tensor(out=u3[:], in0=u2[:], scalar=0.0, in1=u3[:],
                                                          op0=ALU.max, op1=ALU.add))
                nc.vector.tensor_tensor(g[:], u3[:], heads(neg_a[:]), ALU.mult).then_inc(g_ready, 1)
                dve.wait_ge(Gsum_ready, b + 1)
                nc.vector.tensor_copy(G[:], G_ps)
                chain.link(nc.vector.tensor_copy(eGend[:], end_ps))
                nc.vector.tensor_tensor(u1[:], eGend[:], G[:], ALU.subtract).then_inc(gl_ready, 1)
                dve.wait_ge(sq_ready, b + 1)
                nc.vector.tensor_reduce(ss[:].rearrange("p t h -> p (t h)"),
                                        o[:].rearrange("p t (h d) -> p (t h) d", d=DK), AX, ALU.add).then_inc(ss_ready, 1)
                dve.wait_ge(len_ready, b + 1)
                chain.link(nc.vector.reciprocal(rn[:], ss[:]))
                rq, rk = rn[:, :, 0:HK], rn[:, :, HK:2 * HK]
                chain.link(nc.vector.tensor_scalar(rq, rq, float(DK) ** -0.5, None, ALU.mult))
                dve.wait_ge(exp_ready, b + 1)
                both = lambda v: v.unsqueeze(3).broadcast_to([P, TB, HK, 2])
                split = lambda v: v.rearrange("p t (h r) -> p t h r", r=2)
                chain.link(nc.vector.tensor_tensor(k_in[:], beta[:], eG[:], ALU.mult))
                nc.vector.tensor_tensor(split(k_in[:]), split(k_in[:]), both(rk), ALU.mult)
                nc.vector.tensor_tensor(split(k_out[:]), split(eGl[:]), both(rk), ALU.mult)
                nc.vector.tensor_tensor(split(q_in[:]), split(eG[:]), both(rq), ALU.mult)
                chain.close()
                stage_end(dve, b, 0)
                with dve.Fori(0, HG) as hg:
                    turn = b * HG + hg
                    chain = Chain(dve, vec_t, per=1)
                    chain.start(turn)

                    def prep(ch):
                        k = ch % 2
                        q = qkv[:, ch, ds(hg * P, P)].rearrange("p (h d) -> p h d", d=DK)
                        kk = qkv[:, ch, ds(hg * P + KOFF, P)].rearrange("p (h d) -> p h d", d=DK)
                        v = qkv[:, ch, ds(hg * (2 * P) + VOFF, 2 * P)].rearrange("p (h d) -> p h d", d=DK)
                        key = lambda w, at: w[:, ch, ds(hg * 2 + at, 2)].unsqueeze(2).broadcast_to([P, 2, DK])
                        four = lambda w, n: w[:, ch, ds(hg * 4, 4)].unsqueeze(2).broadcast_to([P, 4, n])
                        twice = lambda w: w.unsqueeze(2).broadcast_to([P, 2, 2, DK])
                        value = lambda w: w[:, ch, ds(hg * 4, 4)].rearrange(
                            "p (h r) -> p h r", r=2).unsqueeze(3).broadcast_to([P, 2, 2, DK])
                        by_key = lambda w: w[:, k].rearrange("p (h r) d -> p h r d", r=2)
                        nc.vector.tensor_tensor(Kn[:, k], kk, key(rn, HK), ALU.mult)
                        nc.vector.tensor_tensor(Qn[:, k], q, key(rn, 0), ALU.mult)
                        nc.vector.tensor_tensor(by_key(Kb), twice(kk), value(k_in), ALU.mult)
                        nc.vector.tensor_tensor(by_key(Kd), twice(kk), value(k_out), ALU.mult)
                        nc.vector.tensor_tensor(by_key(Qe), twice(q), value(q_in), ALU.mult)
                        nc.vector.tensor_tensor(Vb[:, k], v, four(beta, DK), ALU.mult)
                        nc.vector.tensor_tensor(Ug[:, k], upto[:].unsqueeze(1).broadcast_to([P, 4, P]), four(g, P),
                                                ALU.mult).then_inc(prep_ready, 1)

                    dve.wait_ge(S_ready, turn * TB + 1)
                    chain.link(nc.vector.memset(S[:], 0.0))
                    prep(0)
                    for ch in range(TB):
                        at = turn * TB + (ch + 1)
                        dve.wait_ge(grow_ready, at)
                        nc.vector.tensor_tensor(dd[:], gps[:], G[:, ch, ds(hg * 4, 4)].unsqueeze(2).broadcast_to([P, 4, P]),
                                                ALU.subtract).then_inc(dd_ready, 1)
                        kqT_ps = kps[:, :, 1, :].unsqueeze(2).broadcast_to([P, 2, 2, P])
                        by_key = lambda w: w[:].rearrange("p (h r) t -> p h r t", r=2)
                        dve.wait_ge(kk_ready, at)
                        for h in range(4):
                            last = nc.vector.scalar_tensor_tensor(
                                out=M[:, h], in0=kps[:, h // 2, 0, :].unsqueeze(1).broadcast_to([P, LEVELS, P]),
                                scalar=beta[:, ch, ds(hg * 4 + h, 1)], in1=levels[:], op0=ALU.mult, op1=ALU.mult)
                        last.then_inc(M_ready, 1)
                        one = c.ident[:].unsqueeze(1).unsqueeze(1).broadcast_to([P, 2, 2, P])
                        halves = lambda w: w.rearrange("p (a h) t -> p a h t", a=2)
                        dve.wait_ge(M_ready, at)
                        nc.vector.tensor_tensor(XX[:, :, 1], one, halves(M[:, :, 0, :]), ALU.subtract)
                        dve.wait_ge(m0_ready, at)
                        nc.vector.tensor_tensor(XX[:, :, 0], one, m0_ps, ALU.subtract).then_inc(X0_ready, 1)
                        for lv in range(1, LEVELS):
                            for half in range(2):
                                dve.wait_ge(w_ready, turn * (TB * 12) + (ch * 12 + (lv - 1) * 2 + half + 1))
                                n = 2 if lv < LEVELS - 1 else 1
                                nc.vector.tensor_tensor(XX[:, half, 0:n], XX[:, half, 0:n], wps[half][:, 0:n],
                                                        ALU.subtract).then_inc(X_ready, 1)
                            if lv == 1:
                                dve.wait_ge(EU_ready, at)
                                nc.vector.tensor_tensor(by_key(PT), kqT_ps, by_key(EU), ALU.mult).then_inc(PT_ready, 1)
                            if lv == 3 and ch + 1 < TB:
                                prep(ch + 1)
                        dve.wait_ge(X_ready, turn * (TB * 12) + (ch + 1) * 12)
                        nc.vector.tensor_tensor(Tm[:], XX[:, :, 0], E[:].rearrange("p (a h) t -> p a h t", a=2),
                                                ALU.mult).then_inc(Tm_ready, 1)
                        dve.wait_ge(r_ready, at)
                        nc.vector.tensor_tensor(Bm[:], Vb[:, ch % 2], r_ps.rearrange("p a (b d) -> p (a b) d", d=DK),
                                                ALU.subtract).then_inc(B_ready, 1)
                        dve.wait_ge(s_ready, at)
                        for h in range(4):
                            rows, cs = slice(DK * (h % 2), DK * (h % 2) + DK), slice(DK * (h % 2), DK * (h % 2) + DK)
                            last = nc.vector.scalar_tensor_tensor(
                                out=S[rows, h // 2, cs], in0=S[rows, h // 2, cs],
                                scalar=eGend[rows, ch, ds(hg * 4 + h, 1)], in1=s_ps[rows, h // 2, cs],
                                op0=ALU.mult, op1=ALU.add)
                        last.then_inc(S_ready, 1)
                    chain.close()
                stage_end(dve, b, 1)
                dve.wait_ge(osq_ready, b + 1)
                nc.vector.tensor_reduce(ss[:].rearrange("p t h -> p (t h)"),
                                        osq.rearrange("p t (h d) -> p (t h) d", d=DK), AX,
                                        ALU.add).then_inc(ovar_ready, 1)
                dve.wait_ge(ostd_ready, b + 1)
                chain = Chain(dve, vec_e, per=2)
                chain.start(b)
                chain.link(nc.vector.reciprocal(rn[:], ss[:]))
                oh = o[:].rearrange("p t (h d) -> p (t h) d", d=DK)
                chain.link(nc.vector.tensor_tensor(oh, oh, rn[:].rearrange("p t h -> p (t h)").unsqueeze(2).broadcast_to(
                    [P, TB * HV, DK]), ALU.mult))
                nc.vector.tensor_tensor(o[:], o[:], gate[:], ALU.mult).then_inc(on_ready, 1)
                chain.close()
                for t in range(TB):
                    dve.wait_ge(out_ready, b * TB + (t + 1))
                    row = c.x[:, ds(b * TB + t, 1), :].rearrange("p a d -> p (a d)")
                    nc.vector.tensor_tensor(row, row, zps[t % 2][:, 0:D], ALU.add).then_inc(added, 1)
                stage_end(dve, b, 2)

        @block.tensor
        def _(pe):
            pe.wait_ge(loaded, LOADS)
            pe.sem_inc(S_ready, 1)
            pe.sem_inc(o_copied, 1)
            with pe.Fori(0, B) as b:
                pe.wait_ge(xb_ready, b + 1)

                def turn_tile(m):
                    pe.wait_ge(act_ready, b * NM + (m + 1))
                    if m >= 2:
                        pe.wait_ge(tr_copied, b * NM + (m - 1))
                    for t in range(TB):
                        last = nc.tensor.transpose(trps[m % 2][:, t, :], act_ct[:, m % 2, t * P:(t + 1) * P], c.ident[:])
                    last.then_inc(tr_ready, 1)

                for m in range(NM):
                    if m >= 2:
                        pe.wait_ge(conv_ready, b * NM + (m - 1))
                    for k in range(DC):
                        last = nc.tensor.matmul(proj[m % 2], wqkv[:, k, m * P:(m + 1) * P], xb[:, k, :],
                                                start=(k == 0), stop=(k == DC - 1))
                    last.then_inc(proj_ready, 1)
                    if m >= 2:
                        turn_tile(m - 2)
                turn_tile(NM - 2)
                turn_tile(NM - 1)
                for t in range(TB):
                    for k in range(DC):
                        last = nc.tensor.matmul(ba_ps[:, t, :], xb[:, k, t * P:(t + 1) * P], wba[:, k, :],
                                                start=(k == 0), stop=(k == DC - 1))
                last.then_inc(ba_ready, 1)
                for n in range(TB * NZ):
                    t, half = n // NZ, n % NZ
                    if n >= 2:
                        pe.wait_ge(z_copied, b * (TB * NZ) + (n - 1))
                    for k in range(DC):
                        last = nc.tensor.matmul(zps[n % 2], xb[:, k, t * P:(t + 1) * P],
                                                wz[:, k, half * 512:(half + 1) * 512],
                                                start=(k == 0), stop=(k == DC - 1))
                    last.then_inc(z_ready, 1)
                pe.wait_ge(g_ready, b + 1)
                nc.tensor.matmul(G_ps, upto[:], g[:], start=True, stop=True)
                nc.tensor.matmul(end_ps, c.ones[:], g[:], start=True, stop=True).then_inc(Gsum_ready, 1)
                stage_end(pe, b, 0)
                with pe.Fori(0, HG) as hg:
                    turn = b * HG + hg
                    for ch in range(TB):
                        k = ch % 2
                        at = turn * TB + (ch + 1)
                        pe.wait_ge(prep_ready, at)
                        two = lambda w: w.rearrange("p h d -> p (h d)")
                        for n, w in enumerate((Kn[:, k], Qn[:, k], Kb[:, k, 0:2], Kb[:, k, 2:4], Qe[:, k, 0:2],
                                               Qe[:, k, 2:4])):
                            last = nc.tensor.transpose(tps[:, n, :], two(w), c.ident[:])
                        last.then_inc(turned, 1)
                        pe.wait_ge(S_ready, at)
                        nc.tensor.matmul(gps[:], c.ones[:], Ug[:, k], start=True, stop=True).then_inc(grow_ready, 1)
                        pe.wait_ge(kqT_ready, at)
                        pe.wait_ge(o_copied, at)
                        low, high = slice(0, DK), slice(DK, 2 * DK)
                        nc.tensor.matmul(kps[:, 0], kqT[low, 0, :], kqT[low, 0:2, :], start=True,
                                         stop=True).then_inc(kk_low, 1)
                        pe.wait_ge(kk_low, at)
                        nc.tensor.matmul(kps[:, 1], kqT[high, 0, :], kqT[high, 0:2, :], start=True,
                                         stop=True).then_inc(kk_ready, 1)
                        pe.wait_ge(M_ready, at)
                        for h in range(4):
                            last = nc.tensor.transpose(m0_ps[:, h // 2, h % 2, :], M[:, h, 0, :], c.ident[:])
                        last.then_inc(m0_ready, 1)
                        pe.wait_ge(X0_ready, at)
                        for lv in range(1, LEVELS):
                            step = ch * 12 + (lv - 1) * 2
                            for half in range(2):
                                if lv > 1:
                                    pe.wait_ge(X_ready, turn * (TB * 12) + (step - 2 + half + 1))
                                for e in range(2):
                                    h = 2 * half + e
                                    last = nc.tensor.matmul(yps[half][:, e, :], M[:, h, lv, :], XX[:, half, 0, e, :],
                                                            start=True, stop=True)
                                last.then_inc(y_ready, 1)
                            for half in range(2):
                                pe.wait_ge(y_copied, turn * (TB * 12) + (step + half + 1))
                                for e in range(2):
                                    h = 2 * half + e
                                    last = nc.tensor.matmul(wps[half][:, 0, e, :], XX[:, half, 1, e, :], Y[:, h, :],
                                                            start=True, stop=True)
                                    if lv < LEVELS - 1:
                                        last = nc.tensor.matmul(wps[half][:, 1, e, :], Y[:, h, :], XX[:, half, 1, e, :],
                                                                start=True, stop=True)
                                last.then_inc(w_ready, 1)
                        for e in range(2):
                            last = nc.tensor.matmul(r_ps[:, e, :], kqT[:, 2 + e, :], S[:, e, :], start=True, stop=True)
                        last.then_inc(r_ready, 1)
                        pe.wait_ge(Tm_ready, at)
                        pe.wait_ge(B_ready, at)
                        for h in range(4):
                            last = nc.tensor.matmul(u_ps[:, h, :], Tm[:, h // 2, h % 2, :], Bm[:, h, :],
                                                    start=True, stop=True)
                        last.then_inc(u_ready, 1)
                        pe.wait_ge(U_ready, at)
                        pe.wait_ge(PT_ready, at)
                        for e in range(2):
                            nc.tensor.matmul(o_ps[:, e * P:(e + 1) * P], kqT[:, 4 + e, :], S[:, e, :], start=True,
                                             stop=False, skip_group_check=True)
                            for h in (2 * e, 2 * e + 1):
                                last = nc.tensor.matmul(o_ps[:, h * DK:(h + 1) * DK], PT[:, h, :], U[:, h, :], start=False,
                                                        stop=True, skip_group_check=True)
                        last.then_inc(o_ready, 1)
                        for e in range(2):
                            last = nc.tensor.matmul(s_ps[:, e, :], Kd[:, k, 2 * e:2 * e + 2], U[:, 2 * e:2 * e + 2],
                                                    start=True, stop=True)
                        last.then_inc(s_ready, 1)
                stage_end(pe, b, 1)
                pe.wait_ge(on_ready, b + 1)
                for m in range(HV * DK // P):
                    if m >= 2:
                        pe.wait_ge(oT_copied, b * (HV * DK // P) + (m - 1))
                    for t in range(TB):
                        last = nc.tensor.transpose(proj[m % 2][:, t * P:(t + 1) * P], o[:, t, m * P:(m + 1) * P], c.ident[:])
                    last.then_inc(oT_ready, 1)
                pe.wait_ge(oT_copied, b * (HV * DK // P) + HV * DK // P)
                for t in range(TB):
                    if t >= 2:
                        pe.wait_ge(added, b * TB + (t - 1))
                    for m in range(HV * DK // P):
                        last = nc.tensor.matmul(zps[t % 2][:, 0:D], oT[:, m, t * P:(t + 1) * P], wout[:, m, :],
                                                start=(m == 0), stop=(m == HV * DK // P - 1))
                    last.then_inc(out_ready, 1)
                stage_end(pe, b, 2)


def lay_attention(name, a, rows, wq, bq, wk, bk, wv, bv, wo, bo, heads):
    d = wq.shape[1] // heads

    def copies(w):
        w = w.reshape(*w.shape[:-1], heads, d)
        if d < 32:
            w = np.concatenate([w, np.zeros((*w.shape[:-1], 32 - d), w.dtype)], -1)
        return np.concatenate([w] * (P // w.shape[-1]), -1)

    per_head = lambda w: rows(copies(w).reshape(D, heads * P)).reshape(P, DC, heads, P).transpose(2, 0, 1, 3)
    return {
        f"{name}_wqk": np.stack([per_head(wq), per_head(wk)], 2),
        f"{name}_bqk": np.stack([copies(bq).T, copies(bk).T], 1),
        f"{name}_wv": rows(wv),
        f"{name}_bv": bv,
        f"{name}_wo": rows(wo),
        f"{name}_bo": bo,
    }


def lay_masked_attention(a, rows, cols):
    g = lambda n: a["L0_xattn_" + n]
    o = lay_attention("xa0", a, rows, g("Wq"), g("bq"), g("Wk"), g("bk"), g("Wv"), g("bv"), g("Wo"), g("bo"), 16)
    bytes_ = np.pad(a["mask_BxSxS2_bk1"].view(np.uint8).reshape(B, TB, P, S2), [(0, 0)] * 3 + [(0, 4 * SW - S2)])
    o["mask"] = bytes_.view(np.int32)
    return o


def lay_full_attention(a, rows, cols):
    g = lambda n: a["L1_xattn_" + n]
    return lay_attention("xa1", a, rows, g("W_q").T, g("b_q"), g("W_k").T, g("b_k"), g("W_v").T, g("b_v"),
                         g("W_o").T, g("b_o"), 16)


def masked_attention(nc, c):
    attention(nc, c, "xa0", heads=16, dk=64, masked=True)


def full_attention(nc, c):
    attention(nc, c, "xa1", heads=16, dk=16, masked=False)


def attention(nc, c, name, heads, dk, masked):
    layernorm(nc, c, f"{name}_ln", c.x, c.xnT)
    NV = -(-heads * dk // 512)
    HV_ = heads // NV
    VW = HV_ * dk
    NO = heads * dk // P
    SCALE = float(dk) ** -0.5
    KC = [(n * 512, min(512, S2 - n * 512)) for n in range(-(-S2 // 512))]
    WIDE = S2 + S2 % 2
    G4 = [(g, min(g + 4, KT)) for g in range(0, KT, 4)]
    NQ = 2 if dk == 64 else 1
    with Scope(nc, name) as s:
        wv = s.sb("wv", [P, DC, heads * dk])
        wo = s.sb("wo", [P, NO, D])
        bqk = s.sb("bqk", [P, 2, heads])
        bv = s.sb("bv", [P, heads * dk])
        bo = s.sb("bo", [P, D])
        ctxT = s.sb("ctxT", [P, DC, S2])
        wqk = s.sb("wqk", [P, 2, DC, P])
        V = s.sb("V", [P, KT, HV_, 2, dk], F32R)
        Q = s.sb("Q", [P, NQ, T], F32R)
        K = s.sb("K", [P, WIDE], F32R)
        prob = s.sb("prob", [P, 2, S2])
        PT = s.sb("PT", [P, 2, KT, P], F32R)
        mx = s.sb("mx", [P, 2])
        neg = s.sb("neg", [P, 2])
        total = s.sb("total", [P, 2])
        rtotal = s.sb("rtotal", [P, 2])
        part = s.sb("part", [P, dk])
        att = s.sb("att", [P, TB, heads * dk])
        attT = V[:].rearrange("p k h e d -> p (k h e d)").bitcast(F32)[:, 0:NO * T].rearrange("p (n t) -> p n t", t=T)
        if masked:
            mask8 = s.sb("mask8", [P, TB, SW], I32)
            mask = s.sb("mask", [P, TB, S2], BF16)
        sps = s.ps("sps", [P, 2048])
        tps = [s.ps(f"tps{k}", [P, 4, P]) for k in range(2)]
        ops = [s.ps(f"ops{k}", [P, 512]) for k in range(2)]
        flat = [t[:].rearrange("p a b -> p (a b)") for t in tps]

        loaded = s.sem("loaded")
        pad_ready = s.sem("pad_ready")
        ctx_loaded = s.sem("ctx_loaded")
        mask_loaded = s.sem("mask_loaded")
        mask_ready = s.sem("mask_ready")
        w_loaded = s.sem("w_loaded")
        v_ready = s.sem("v_ready")
        v_hi = s.sem("v_hi")
        v_lo = s.sem("v_lo")
        proj_ready = s.sem("proj_ready")
        proj_hi = s.sem("proj_hi")
        proj_lo = s.sem("proj_lo")
        s_ready = s.sem("s_ready")
        max_ready = s.sem("max_ready")
        neg_ready = s.sem("neg_ready")
        p_ready = s.sem("p_ready")
        t_ready = s.sem("t_ready")
        t_hi = s.sem("t_hi")
        t_lo = s.sem("t_lo")
        o_ready = s.sem("o_ready")
        vec = s.sem("vec")
        att_ready = s.sem("att_ready")
        aT_ready = s.sem("aT_ready")
        aT_copied = s.sem("aT_copied")
        out_ready = s.sem("out_ready")
        vec_o = s.sem("vec_o")
        added = s.sem("added")
        passed = s.sem("passed")
        block = s.block()
        LOADS = 5 * 16
        NT_V = KT
        NP = 1 + len(KC)
        NG = len(G4)
        FREE = 1

        def seen(eng):
            eng.sem_inc(passed, 1)

        def keys(kt):
            return P if kt < KT - 1 else LAST

        @block.sync
        def _(sp):
            for dst, src in ((bqk, "bqk"), (wv, "wv"), (wo, "wo")):
                sp.dma_start(dst[:], c.dram[f"{name}_{src}"]).then_inc(loaded, 16)
            for dst, src in ((bv, "bv"), (bo, "bo")):
                sp.dma_start(dst[:], c.dram[f"{name}_{src}"].partition_broadcast(P)).then_inc(loaded, 16)
            with sp.Fori(0, B) as b:
                sp.wait_ge(att_ready, b * NV + FREE)
                sp.dma_start(ctxT[:], c.dram["ctxT"][ds(b, 1)].rearrange("a p c s -> (a p) c s")).then_inc(ctx_loaded, 16)
                if masked:
                    sp.dma_start(mask8[:], c.dram["mask"][ds(b, 1)].rearrange("a t p s -> (a p) t s")).then_inc(mask_loaded, 16)
                with sp.Fori(0, heads) as h:
                    sp.wait_ge(proj_ready, (b * heads + h) * NP + FREE)
                    sp.dma_start(wqk[:], c.dram[f"{name}_wqk"][ds(h, 1)].rearrange("a p e c m -> (a p) e c m")
                                 ).then_inc(w_loaded, 16)

        if masked:
            @block.gpsimd
            def _(pool):
                with pool.Fori(0, B) as b:
                    pool.wait_ge(att_ready, b * NV + FREE)
                    pool.wait_ge(mask_loaded, b * 16 + 16)
                    seen(pool)
                    nc.gpsimd.tensor_scalar(mask[:], mask8[:].bitcast(U8)[:, :, 0:S2], NEG, None, ALU.mult).then_inc(mask_ready, 1)

        @block.scalar
        def _(act):
            act.wait_ge(loaded, LOADS)
            with act.Fori(0, B) as b:
                with act.Fori(0, NV) as gr:
                    tv = b * NV + gr
                    for kt in range(KT):
                        act.wait_ge(v_ready, tv * NT_V + (kt + 1))
                        if kt == 0:
                            act.wait_ge(att_ready, tv + FREE)
                        n = keys(kt)
                        nc.scalar.activation(V[0:n, kt, :, 0, :], flat[kt % 2][0:n, 0:VW].rearrange(
                            "p (h d) -> p h d", d=dk), ACT.Copy).then_inc(v_hi, 1)
                    with act.Fori(0, HV_) as hh:
                        turn = tv * HV_ + hh
                        h = gr * HV_ + hh
                        for n in range(NP):
                            act.wait_ge(proj_ready, turn * NP + (n + 1 + FREE))
                            dst = Q[:, 0, :] if n == 0 else K[:, KC[n - 1][0]:KC[n - 1][0] + KC[n - 1][1]]
                            w = T if n == 0 else KC[n - 1][1]
                            seen(act)
                            nc.scalar.activation(dst, flat[n % 2][:, 0:w], ACT.Identity,
                                                 bias=bqk[:, min(n, 1), ds(h, 1)]).then_inc(proj_hi, 1)

                        def exps(q):
                            act.wait_ge(neg_ready, turn * TB + (q + 1))
                            src = prob[:, q % 2, :] if masked else sps[:, 0:S2]
                            nc.scalar.activation(prob[:, q % 2, :], src, ACT.Exp, bias=neg[:, q % 2:q % 2 + 1],
                                                 scale=SCALE, accum_out=total[:, q % 2:q % 2 + 1]).then_inc(p_ready, 1)

                        exps(0)
                        for q in range(TB):
                            for g, (k0, k1) in enumerate(G4):
                                act.wait_ge(t_ready, turn * (TB * NG) + (q * NG + g + 1))
                                n = keys(k1 - 1) if k1 - k0 == 1 else P
                                nc.scalar.activation(PT[0:n, 0, k0:k1, :], tps[g % 2][0:n, 0:k1 - k0, :],
                                                     ACT.Copy).then_inc(t_hi, 1)
                            if q + 1 < TB:
                                exps(q + 1)
                for m in range(NO):
                    act.wait_ge(aT_ready, b * NO + (m + 1))
                    nc.scalar.activation(attT[:, m, :], flat[m % 2], ACT.Copy).then_inc(aT_copied, 1)

        @block.vector
        def _(dve):
            nc.vector.memset(K[:].bitcast(F32), 0.0).then_inc(pad_ready, 1)
            dve.wait_ge(loaded, LOADS)
            with dve.Fori(0, B) as b:
                if masked:
                    dve.wait_ge(mask_ready, b + 1)
                    seen(dve)
                with dve.Fori(0, NV) as gr:
                    tv = b * NV + gr
                    for kt in range(KT):
                        dve.wait_ge(v_hi, tv * NT_V + (kt + 1))
                        n = keys(kt)
                        nc.vector.tensor_tensor(V[0:n, kt, :, 1, :], flat[kt % 2][0:n, 0:VW].rearrange(
                            "p (h d) -> p h d", d=dk), V[0:n, kt, :, 0, :].bitcast(F32), ALU.subtract).then_inc(v_lo, 1)
                    with dve.Fori(0, HV_) as hh:
                        turn = tv * HV_ + hh
                        h = gr * HV_ + hh
                        chain = Chain(dve, vec, per=2 * TB)
                        chain.start(turn)
                        for n in range(NP):
                            dve.wait_ge(proj_hi, turn * NP + (n + 1))
                            if n == 0:
                                lows = [(slice(0, P), Q[:, 1, :])] if NQ == 2 else [
                                    (slice(r, r + 32), Q[r:r + 32, 0, :]) for r in (32, 96)]
                                hi, w, col = Q[:, 0, :], T, 0
                            else:
                                k0, w = KC[n - 1]
                                hi, col = K[:, k0:k0 + w], 1
                                lows = [(slice(P // 2, P), K[P // 2:P, k0:k0 + w])]
                            for rows, lo in lows:
                                last = nc.vector.scalar_tensor_tensor(
                                    out=lo, in0=flat[n % 2][rows, 0:w], scalar=bqk[rows, col, ds(h, 1)],
                                    in1=hi[rows].bitcast(F32), op0=ALU.add, op1=ALU.subtract)
                            last.then_inc(proj_lo, 1)

                        def row_max(q):
                            e = q % 2
                            dve.wait_ge(s_ready, turn * TB + (q + 1))
                            seen(dve)
                            if masked:
                                last = nc.vector.tensor_tensor_reduce(prob[:, e, :], sps[:, 0:S2], mask[:, q, :], 1.0,
                                                                      -3.0e38, ALU.add, ALU.max, mx[:, e:e + 1])
                            else:
                                last = nc.vector.tensor_reduce(mx[:, e:e + 1], sps[:, 0:S2], AX, ALU.max)
                            last.then_inc(max_ready, 1)
                            dve.wait_ge(max_ready, turn * TB + (q + 1))
                            nc.vector.tensor_scalar(neg[:, e:e + 1], mx[:, e:e + 1], -SCALE, None,
                                                    ALU.mult).then_inc(neg_ready, 1)

                        row_max(0)
                        for q in range(TB):
                            e = q % 2
                            if q + 1 < TB:
                                row_max(q + 1)
                            for g, (k0, k1) in enumerate(G4):
                                dve.wait_ge(t_hi, turn * (TB * NG) + (q * NG + g + 1))
                                n = keys(k1 - 1) if k1 - k0 == 1 else P
                                nc.vector.tensor_tensor(PT[0:n, 1, k0:k1, :], tps[g % 2][0:n, 0:k1 - k0, :],
                                                        PT[0:n, 0, k0:k1, :].bitcast(F32), ALU.subtract).then_inc(t_lo, 1)
                            chain.link(nc.vector.reciprocal(rtotal[:, e:e + 1], total[:, e:e + 1]))
                            dve.wait_ge(o_ready, turn * TB + (q + 1))
                            col = ds(h * dk, dk)
                            chain.link(nc.vector.scalar_tensor_tensor(
                                out=part[:], in0=ops[e][:, 0:dk], scalar=rtotal[:, e:e + 1], in1=bv[:, col],
                                op0=ALU.mult, op1=ALU.add))
                            last = nc.vector.scalar_tensor_tensor(
                                out=att[:, q, col], in0=ops[e][:, dk:2 * dk], scalar=rtotal[:, e:e + 1], in1=part[:],
                                op0=ALU.mult, op1=ALU.add)
                        chain.close()
                    dve.drain().then_inc(att_ready, 1)
                chain = Chain(dve, vec_o, per=TB)
                chain.start(b)
                for t in range(TB):
                    row = c.x[:, ds(b * TB + t, 1), :].rearrange("p a d -> p (a d)")
                    dve.wait_ge(out_ready, b * TB + (t + 1))
                    chain.link(nc.vector.tensor_tensor(row, row, ops[t % 2][:, 0:D], ALU.add))
                    nc.vector.tensor_tensor(row, row, bo[:], ALU.add).then_inc(added, 1)
                chain.close()

        @block.tensor
        def _(pe):
            pe.sem_inc(att_ready, FREE)
            pe.sem_inc(proj_ready, FREE)
            pe.wait_ge(loaded, LOADS)
            pe.wait_ge(pad_ready, 1)
            with pe.Fori(0, B) as b:
                pe.wait_ge(ctx_loaded, b * 16 + 16)
                seen(pe)
                with pe.Fori(0, NV) as gr:
                    tv = b * NV + gr
                    for kt in range(KT):
                        if kt >= 2:
                            pe.wait_ge(v_lo, tv * NT_V + (kt - 1))
                        n = keys(kt)
                        for k in range(DC):
                            last = nc.tensor.matmul(flat[kt % 2][0:n, 0:VW], ctxT[:, k, kt * P:kt * P + n],
                                                    wv[:, k, ds(gr * VW, VW)], start=(k == 0), stop=(k == DC - 1))
                        last.then_inc(v_ready, 1)
                    pe.wait_ge(v_lo, tv * NT_V + NT_V)
                    seen(pe)
                    with pe.Fori(0, HV_) as hh:
                        turn = tv * HV_ + hh
                        pe.wait_ge(w_loaded, turn * 16 + 16)
                        for n in range(NP):
                            if n >= 2:
                                pe.wait_ge(proj_lo, turn * NP + (n - 1))
                            for k in range(DC):
                                rhs = c.xnT[:, k, ds(b * T, T)] if n == 0 else ctxT[:, k, KC[n - 1][0]:sum(KC[n - 1])]
                                last = nc.tensor.matmul(flat[n % 2][:, 0:T if n == 0 else KC[n - 1][1]],
                                                        wqk[:, min(n, 1), k, :], rhs, start=(k == 0), stop=(k == DC - 1))
                            last.then_inc(proj_ready, 1)

                        def scores(q):
                            for n, (k0, w) in enumerate(KC):
                                if q == 0:
                                    pe.wait_ge(proj_lo, turn * NP + (n + 2))
                                w += w % 2
                                for e in range(NQ):
                                    last = nc.tensor.matmul(sps[:, k0:k0 + w], Q[:, e, q * P:(q + 1) * P], K[:, k0:k0 + w],
                                                            start=(e == 0), stop=(e == NQ - 1))
                            last.then_inc(s_ready, 1)

                        scores(0)
                        for q in range(TB):
                            e = q % 2
                            if q + 1 < TB:
                                pe.wait_ge(max_ready if masked else p_ready, turn * TB + (q + 1))
                                scores(q + 1)
                            pe.wait_ge(p_ready, turn * TB + (q + 1))
                            for g, (k0, k1) in enumerate(G4):
                                if g >= 2:
                                    pe.wait_ge(t_lo, turn * (TB * NG) + (q * NG + g - 1))
                                for kt in range(k0, k1):
                                    n = keys(kt)
                                    last = nc.tensor.transpose(tps[g % 2][0:n, kt - k0, :], prob[:, e, kt * P:kt * P + n],
                                                               c.ident[:])
                                last.then_inc(t_ready, 1)
                            for g, (k0, k1) in enumerate(G4):
                                pe.wait_ge(t_lo, turn * (TB * NG) + (q * NG + g + 1))
                                for kt in range(k0, k1):
                                    n = keys(kt)
                                    for half in range(2):
                                        last = nc.tensor.matmul(ops[e][:, 0:2 * dk], PT[0:n, half, kt, :],
                                                                V[0:n, kt, ds(hh, 1)].rearrange("p a e d -> p (a e d)"),
                                                                start=(kt == 0 and half == 0),
                                                                stop=(kt == KT - 1 and half == 1))
                            last.then_inc(o_ready, 1)
                pe.wait_ge(att_ready, b * NV + (NV + FREE))
                for m in range(NO):
                    if m >= 2:
                        pe.wait_ge(aT_copied, b * NO + (m - 1))
                    for t in range(TB):
                        last = nc.tensor.transpose(flat[m % 2][:, t * P:(t + 1) * P], att[:, t, m * P:(m + 1) * P], c.ident[:])
                    last.then_inc(aT_ready, 1)
                pe.wait_ge(aT_copied, b * NO + NO)
                for t in range(TB):
                    if t >= 2:
                        pe.wait_ge(added, b * TB + (t - 1))
                    for m in range(NO):
                        last = nc.tensor.matmul(ops[t % 2][:, 0:D], attT[:, m, t * P:(t + 1) * P], wo[:, m, :],
                                                start=(m == 0), stop=(m == NO - 1))
                    last.then_inc(out_ready, 1)
                pe.wait_ge(added, b * TB + TB)
                seen(pe)


DH = 1024
MH = DH // P


def lay_ternary_mlp(a, rows, cols):
    g = lambda n: a["L0_ffn_" + n]
    o = {f"ffn_{n}": rows(g(n + "_w").T) for n in ("w1", "w2", "h1", "h2", "w3")}
    o.update({f"ffn_{n}_s": cols(g(n + "_s")) for n in ("w1", "w2", "h1", "h2")})
    o["ffn_w3_s"] = g("w3_s")
    return o


def ternary_mlp(nc, c):
    layernorm(nc, c, "ffn_ln", c.x, c.xnT)
    NB = B * T // 512
    NT4 = 512 // P
    with Scope(nc, "ffn") as s:
        names = ("w1", "w2", "h1", "h2", "w3")
        w = {n: s.sb(n, list(c.dram[f"ffn_{n}"].shape)) for n in names}
        sc = {n: s.sb(n + "_s", [P, MH]) for n in names[:4]}
        w3_s = s.sb("w3_s", [P, D])
        gate = s.sb("gate", [P, 2, 512])
        hid = [s.sb(f"hid{k}", [P, MH, 512]) for k in range(3)]
        scaled = s.sb("scaled", [P, 2, D])
        up = [s.ps(f"up{k}", [P, 512]) for k in range(2)]
        lin = [s.ps(f"lin{k}", [P, 512]) for k in range(2)]
        mid = [s.ps(f"mid{k}", [P, 512]) for k in range(2)]
        low = [s.ps(f"low{k}", [P, 512]) for k in range(2)]
        loaded = {n: s.sem(n + "_loaded") for n in names}
        scales = s.sem("scales")
        up_ready = s.sem("up_ready")
        gate_ready = s.sem("gate_ready")
        hid_ready = s.sem("hid_ready")
        mid_ready = [s.sem(f"mid_ready{k}") for k in range(2)]
        act_ready = [s.sem(f"act_ready{k}") for k in range(2)]
        out_ready = s.sem("out_ready")
        scaled_ready = s.sem("scaled_ready")
        added = s.sem("added")
        block = s.block()
        SCALES = 5 * 16

        @block.sync
        def _(sp):
            for n in ("w1", "w2", "h1", "h2"):
                sp.dma_start(sc[n][:], c.dram[f"ffn_{n}_s"]).then_inc(scales, 16)
            sp.dma_start(w3_s[:], c.dram["ffn_w3_s"].partition_broadcast(P)).then_inc(scales, 16)
            for n in names:
                sp.dma_start(w[n][:], c.dram[f"ffn_{n}"]).then_inc(loaded[n], 16)

        @block.scalar
        def _(act):
            act.wait_ge(scales, SCALES)
            with act.Fori(0, NB) as i:
                for m in range(MH):
                    act.wait_ge(up_ready, i * MH + (m + 1))
                    if m >= 2:
                        act.wait_ge(hid_ready, i * MH + (m - 1))
                    nc.scalar.activation(gate[:, m % 2, :], up[m % 2][:], ACT.Silu, scale=sc["w1"][:, m:m + 1]
                                         ).then_inc(gate_ready, 1)
                for k, n in enumerate(("h1", "h2")):
                    for m in range(MH):
                        act.wait_ge(mid_ready[k], i * MH + (m + 1))
                        nc.scalar.activation(hid[1 + k][:, m, :], mid[m % 2][:], ACT.Gelu, scale=sc[n][:, m:m + 1]
                                             ).then_inc(act_ready[k], 1)

        @block.vector
        def _(dve):
            dve.wait_ge(scales, SCALES)
            with dve.Fori(0, NB) as i:
                for m in range(MH):
                    dve.wait_ge(gate_ready, i * MH + (m + 1))
                    nc.vector.scalar_tensor_tensor(out=hid[0][:, m, :], in0=lin[m % 2][:], scalar=sc["w2"][:, m:m + 1],
                                                   in1=gate[:, m % 2, :], op0=ALU.mult, op1=ALU.mult
                                                   ).then_inc(hid_ready, 1)
                for t in range(NT4):
                    row = c.x[:, ds(i * NT4 + t, 1), :].rearrange("p a d -> p (a d)")
                    dve.wait_ge(out_ready, i * NT4 + (t + 1))
                    nc.vector.tensor_tensor(scaled[:, t % 2, :], low[t % 2][:, 0:D], w3_s[:], ALU.mult
                                            ).then_inc(scaled_ready, 1)
                    dve.wait_ge(scaled_ready, i * NT4 + (t + 1))
                    nc.vector.tensor_tensor(row, row, scaled[:, t % 2, :], ALU.add).then_inc(added, 1)

        @block.tensor
        def _(pe):
            for n in names:
                pe.wait_ge(loaded[n], 16)
            with pe.Fori(0, NB) as i:
                for m in range(MH):
                    if m >= 2:
                        pe.wait_ge(hid_ready, i * MH + (m - 1))
                    for dst, n in ((lin, "w2"), (up, "w1")):
                        for k in range(DC):
                            last = nc.tensor.matmul(dst[m % 2][:], w[n][:, k, m * P:(m + 1) * P], c.xnT[:, k, ds(i * 512, 512)],
                                                    start=(k == 0), stop=(k == DC - 1))
                    last.then_inc(up_ready, 1)
                for e, n in enumerate(("h1", "h2")):
                    pe.wait_ge(hid_ready if e == 0 else act_ready[0], i * MH + MH)
                    for m in range(MH):
                        if e == 1 and m < 2:
                            pass
                        elif m >= 2:
                            pe.wait_ge(act_ready[e], i * MH + (m - 1))
                        for k in range(MH):
                            last = nc.tensor.matmul(mid[m % 2][:], w[n][:, k, m * P:(m + 1) * P], hid[e][:, k, :],
                                                    start=(k == 0), stop=(k == MH - 1))
                        last.then_inc(mid_ready[e], 1)
                pe.wait_ge(act_ready[1], i * MH + MH)
                for t in range(NT4):
                    if t >= 2:
                        pe.wait_ge(added, i * NT4 + (t - 1))
                    for k in range(MH):
                        last = nc.tensor.matmul(low[t % 2][:, 0:D], hid[2][:, k, t * P:(t + 1) * P], w["w3"][:, k, :],
                                                start=(k == 0), stop=(k == MH - 1))
                    last.then_inc(out_ready, 1)


CH = 2 * D
CC = CH // P
NS, RANK = 16, D // 16
DBC = RANK + 2 * NS
LOW = 64
SOL = 0.1
TWO_PI_HIGH = 6.28125
TWO_PI_LOW = 2 * np.pi - TWO_PI_HIGH
TO_WHOLE = 1.5 * 2.0 ** 23
PI = 3.1415925


def lay_selective_scan(a, rows, cols):
    g = lambda n: a["L1_attn_" + n]
    gap = np.zeros((CH, LOW - DBC), np.float32)
    pick = np.zeros((LOW + DBC, NS, 2, P), np.float32)
    for n in range(NS):
        for e in range(2):
            row = RANK + e * NS + n
            pick[[row, LOW + row], n, e] = 1
    per_head = lambda v: cols(np.repeat(v, D // v.shape[0]))
    return {
        "scan_ln": np.stack([cols(g(n)) for n in ("ln1_g", "ln1_b", "ln2_g", "ln2_b")], 1),
        "scan_win": rows(g("W_in")), "scan_bin": cols(g("b_in")),
        "scan_conv": g("conv_w").reshape(CC, P, CONV).transpose(1, 0, 2), "scan_conv_b": cols(g("conv_b")),
        "scan_wxp": rows(np.concatenate([g("W_xp"), gap, g("W_xp")], 1)),
        "scan_wdt": g("W_dt"), "scan_bdt": cols(g("b_dt")),
        "scan_A_log": g("A_log").reshape(CC, P, NS).transpose(1, 0, 2),
        "scan_skip": cols(g("D_skip")),
        "scan_wout": rows(g("W_out")), "scan_bout": g("b_out"),
        "scan_pick": pick,
        "wave_wsi": rows(g("W_si")), "wave_bsi": cols(g("b_si")),
        "wave_gates": np.stack([per_head(g("gates")[:, k]) for k in range(3)], 1),
        "wave_alpha": per_head(g("alpha")),
        "wave_wso": rows(g("W_so")), "wave_bso": g("b_so"),
    }


def selective_scan(nc, c):
    with Scope(nc, "ss") as s:
        ln = s.sb("ln", [P, 4, DC])
        xa = s.sb("xa", [P, NT, D])
        load_norms(nc, c, ln)
        layernorm(nc, c, "ss_ln0", c.x, c.xnT, keep=xa)
        layernorm(nc, c, "ss_ln1", xa, c.xnT, gain=ln[:, 0, :], shift=ln[:, 1, :])
        scan_channels(nc, c, xa)
        layernorm(nc, c, "ss_ln2", xa, c.xnT, gain=ln[:, 2, :], shift=ln[:, 3, :])
        waves(nc, c, xa)


def load_norms(nc, c, ln):
    with Scope(nc, "ss_norms") as s:
        loaded = s.sem("loaded")
        block = s.block()

        @block.sync
        def _(sp):
            sp.dma_start(ln[:], c.dram["scan_ln"]).then_inc(loaded, 16)
            sp.wait_ge(loaded, 16)


def scan_channels(nc, c, xa):
    with Scope(nc, "scan") as s:
        win = s.sb("win", [P, DC, 2 * CH])
        b_in = s.sb("bin", [P, 2 * CC])
        convw = s.sb("convw", [P, CC, CONV])
        conv_b = s.sb("conv_b", [P, CC])
        wxp = s.sb("wxp", [P, CC, LOW + DBC])
        wdt = s.sb("wdt", [RANK, CH])
        b_dt = s.sb("bdt", [P, CC])
        neg_a = s.sb("neg_a", [P, CC, NS])
        skip = s.sb("skip", [P, CC])
        wout = s.sb("wout", [P, CC, D])
        b_out = s.sb("bout", [P, D])
        pick = s.sb("pick", [LOW + DBC, NS, 2, P])
        xp = s.sb("xp", [P, 2, T])
        conv = s.sb("conv", [P, 2, T])
        xc = s.sb("xc", [P, CC, T])
        zs = s.sb("zs", [P, CC, T])
        whole = s.sb("whole", [LOW + DBC, T], F32R)
        parts = s.sb("parts", [LOW + DBC, T], F32R)
        low_rank = s.sb("low_rank", [RANK, T])
        v = s.sb("v", [P, CC, T])
        dt = s.sb("dt", [P, CC, T])
        dtx = s.sb("dtx", [P, CC, T])
        picked = s.sb("picked", [LOW + DBC, 2, 2, P], F32R)
        Bs = s.sb("Bs", [P, 2, T])
        dA = s.sb("dA", [P, 2, CC, T])
        dBx = s.sb("dBx", [P, 2, CC, T])
        h = s.sb("h", [P, CC, T])
        hC = s.sb("hC", [P, 2, CC, T])
        e1, e2 = dA[:, 0], dBx[:, 0]
        gated = dBx[:, 1]
        y_ps = [s.ps(f"y{k}", [P, T]) for k in range(CC)]
        B_ps = [s.ps(f"B{k}", [P, T]) for k in range(2)]
        C_ps = [s.ps(f"C{k}", [P, T]) for k in range(2)]

        loaded = s.sem("loaded")
        ready0 = s.sem("ready0")
        proj_ready = s.sem("proj_ready")
        xp_ready = s.sem("xp_ready")
        conv_ready = s.sem("conv_ready")
        xc_ready = s.sem("xc_ready")
        z_ready = s.sem("z_ready")
        dbc_ready = s.sem("dbc_ready")
        whole_ready = s.sem("whole_ready")
        parts_ready = s.sem("parts_ready")
        rank_ready = s.sem("rank_ready")
        step_ready = s.sem("step_ready")
        v_ready = s.sem("v_ready")
        w_ready = s.sem("w_ready")
        log_ready = s.sem("log_ready")
        exp_ready = s.sem("exp_ready")
        dt_ready = s.sem("dt_ready")
        dtx_ready = s.sem("dtx_ready")
        skip_ready = s.sem("skip_ready")
        zero_ready = s.sem("zero_ready")
        pick_ready = s.sem("pick_ready")
        bc_ready = s.sem("bc_ready")
        B_ready = s.sem("B_ready")
        dA_ready = s.sem("dA_ready")
        dBx_ready = s.sem("dBx_ready")
        scanned = s.sem("scanned")
        hC_ready = s.sem("hC_ready")
        summed = s.sem("summed")
        gated_ready = s.sem("gated_ready")
        out_ready = s.sem("out_ready")
        added = s.sem("added")
        vec = s.sem("vec")
        act_a = s.sem("act_a")
        meet = s.sem("meet")
        passed = s.sem("passed")
        block = s.block()
        LOADS = 12 * 16
        WORKERS = 4
        START = 1
        FREE = 2

        def sequence_end(eng, b):
            eng.drain().then_inc(meet, 1)
            eng.wait_ge(meet, b * WORKERS + WORKERS)
            eng.sem_inc(passed, 1)

        @block.sync
        def _(sp):
            for dst, src in ((win, "win"), (b_in, "bin"), (convw, "conv"), (conv_b, "conv_b"), (wxp, "wxp"), (wdt, "wdt"),
                             (b_dt, "bdt"), (neg_a, "A_log"), (skip, "skip"), (wout, "wout"), (pick, "pick")):
                sp.dma_start(dst[:], c.dram[f"scan_{src}"]).then_inc(loaded, 16)
            sp.dma_start(b_out[:], c.dram["scan_bout"].partition_broadcast(P)).then_inc(loaded, 16)

        @block.gpsimd
        def _(pool):
            pool.wait_ge(loaded, LOADS)
            nc.gpsimd.tensor_tensor(xa[:], xa[:], b_out[:].unsqueeze(1).broadcast_to([P, NT, D]), ALU.add
                                    ).then_inc(ready0, 1)
            with pool.Fori(0, B) as b:
                pool.wait_ge(dt_ready, b + 1)
                pool.sem_inc(passed, 1)
                for k in range(2):
                    last = nc.gpsimd.memset(dA[:, k, :, 0:1], 0.0)
                last.then_inc(zero_ready, 1)
                pool.wait_ge(dtx_ready, b + 1)
                pool.sem_inc(passed, 1)
                with pool.Fori(0, NS // 2) as i:
                    for k in range(2):
                        turn = b * NS + i * 2
                        pool.wait_ge(B_ready, turn + (k + 1 + START))
                        pool.wait_ge(scanned, turn + (k + FREE - 1))
                        nc.gpsimd.tensor_tensor(dBx[:, k], dtx[:], Bs[:, k, :].unsqueeze(1).broadcast_to([P, CC, T]),
                                                ALU.mult).then_inc(dBx_ready, 1)
                sequence_end(pool, b)

        @block.scalar
        def _(act):
            act.wait_ge(loaded, LOADS)
            nc.scalar.activation(neg_a[:], neg_a[:], ACT.Exp).then_inc(ready0, 1)
            with act.Fori(0, B) as b:
                chain = Chain(act, act_a, per=1)
                chain.start(b)
                for m in range(CC):
                    act.wait_ge(proj_ready, b * (2 * CC) + (m + 1))
                    if m >= 2:
                        act.wait_ge(conv_ready, b * CC + (m - 1))
                    nc.scalar.activation(xp[:, m % 2, :], y_ps[m][:], ACT.Identity, bias=b_in[:, m:m + 1]
                                         ).then_inc(xp_ready, 1)
                    if m >= 1:
                        act.wait_ge(conv_ready, b * CC + m)
                        nc.scalar.activation(xc[:, m - 1, :], conv[:, (m - 1) % 2, :], ACT.Silu, bias=conv_b[:, m - 1:m]
                                             ).then_inc(xc_ready, 1)
                act.wait_ge(conv_ready, b * CC + CC)
                nc.scalar.activation(xc[:, CC - 1, :], conv[:, (CC - 1) % 2, :], ACT.Silu, bias=conv_b[:, CC - 1:CC]
                                     ).then_inc(xc_ready, 1)
                for m in range(CC):
                    act.wait_ge(proj_ready, b * (2 * CC) + (CC + m + 1))
                    nc.scalar.activation(zs[:, m, :], y_ps[m][:], ACT.Silu, bias=b_in[:, CC + m:CC + m + 1]
                                         ).then_inc(z_ready, 1)
                act.wait_ge(dbc_ready, b + 1)
                nc.scalar.activation(low_rank[:], B_ps[0][0:RANK, :], ACT.Copy).then_inc(rank_ready, 1)
                nc.scalar.activation(whole[:], B_ps[0][0:LOW + DBC, :], ACT.Copy).then_inc(whole_ready, 1)
                for m in range(CC):
                    act.wait_ge(step_ready, b * CC + (m + 1))
                    last = nc.scalar.activation(v[:, m, :], y_ps[m][:], ACT.Identity, bias=b_dt[:, m:m + 1])
                last.then_inc(v_ready, 1)
                act.wait_ge(v_ready, b + 1)
                chain.link(nc.scalar.activation(e1, v[:], ACT.Abs))
                nc.scalar.activation(e1, e1, ACT.Exp, scale=-1.0).then_inc(exp_ready, 1)
                act.wait_ge(w_ready, b + 1)
                nc.scalar.activation(dt[:], e2, ACT.Ln).then_inc(log_ready, 1)
                chain.close()

                def pick_rows(k, n, sync):
                    if sync is not None:
                        act.wait_ge(bc_ready, sync + START)
                    nc.scalar.activation(picked[:, k], pick[:, ds(n, 1)].rearrange("p a e q -> p (a e) q"), ACT.Copy
                                         ).then_inc(pick_ready, 1)

                def spread_and_decay(k, n, turn):
                    act.wait_ge(bc_ready, turn + (1 + START))
                    act.wait_ge(dBx_ready, turn + (FREE - 1))
                    nc.scalar.activation(Bs[:, k, :], B_ps[k][:], ACT.Copy).then_inc(B_ready, 1)
                    act.wait_ge(scanned, turn + (FREE - 1))
                    act.sem_inc(passed, 1)
                    for m in range(CC):
                        last = nc.scalar.activation(dA[:, k, m, 1:], dt[:, m, 1:], ACT.Exp, scale=neg_a[:, m, ds(n, 1)])
                    last.then_inc(dA_ready, 1)

                pick_rows(0, 0, None)
                act.wait_ge(dt_ready, b + 1)
                act.sem_inc(passed, 1)
                with act.Fori(0, NS // 2 - 1) as i:
                    for k in range(2):
                        turn = b * NS + i * 2 + k
                        pick_rows(1 - k, i * 2 + (k + 1), turn)
                        spread_and_decay(k, i * 2 + k, turn)
                pick_rows(1, NS - 1, b * NS + (NS - 2))
                for k in range(2):
                    spread_and_decay(k, NS - 2 + k, b * NS + (NS - 2 + k))
                sequence_end(act, b)

        @block.vector
        def _(dve):
            dve.sem_inc(scanned, FREE)
            dve.wait_ge(loaded, LOADS)
            dve.wait_ge(ready0, 2)
            nc.vector.tensor_scalar(neg_a[:], neg_a[:], -1.0, None, ALU.mult).then_inc(ready0, 1)
            dve.wait_ge(ready0, 3)
            with dve.Fori(0, B) as b:
                chain = Chain(dve, vec, per=CC * (CONV - 1) + 2)
                chain.start(b)
                for m in range(CC):
                    dve.wait_ge(xp_ready, b * CC + (m + 1))
                    if m >= 2:
                        dve.wait_ge(xc_ready, b * CC + (m - 1))
                    y, x = conv[:, m % 2, :], xp[:, m % 2, :]
                    chain.link(nc.vector.tensor_scalar(y, x, convw[:, m, CONV - 1:CONV], None, ALU.mult))
                    for back in range(1, CONV):
                        last = nc.vector.scalar_tensor_tensor(
                            out=y[:, back:], in0=x[:, :T - back], scalar=convw[:, m, CONV - 1 - back:CONV - back],
                            in1=y[:, back:], op0=ALU.mult, op1=ALU.add)
                        if back < CONV - 1:
                            chain.link(last)
                    last.then_inc(conv_ready, 1)
                dve.wait_ge(whole_ready, b + 1)
                nc.vector.tensor_copy(parts[0:LOW, :], whole[0:LOW, :])
                nc.vector.tensor_tensor(parts[LOW:, :], B_ps[0][LOW:LOW + DBC, :], whole[LOW:, :].bitcast(F32), ALU.subtract
                                        ).then_inc(parts_ready, 1)
                for m in range(CC):
                    last = nc.vector.tensor_scalar(hC[:, 1, m, :], xc[:, m, :], skip[:, m:m + 1], None, ALU.mult)
                last.then_inc(skip_ready, 1)
                dve.wait_ge(exp_ready, b + 1)
                nc.vector.tensor_scalar(e2, e1, 1.0, None, ALU.add).then_inc(w_ready, 1)
                dve.wait_ge(w_ready, b + 1)
                chain.link(nc.vector.scalar_tensor_tensor(out=e1, in0=e2, scalar=1.0, in1=e1, op0=ALU.subtract,
                                                          op1=ALU.subtract))
                chain.link(nc.vector.scalar_tensor_tensor(out=e1, in0=v[:], scalar=0.0, in1=e1, op0=ALU.max,
                                                          op1=ALU.subtract))
                dve.wait_ge(log_ready, b + 1)
                nc.vector.tensor_tensor(dt[:], dt[:], e1, ALU.add).then_inc(dt_ready, 1)
                dve.wait_ge(dt_ready, b + 1)
                nc.vector.tensor_tensor(dtx[:], dt[:], xc[:], ALU.mult).then_inc(dtx_ready, 1)
                dve.wait_ge(zero_ready, b + 1)
                dve.sem_inc(passed, 1)
                flat = lambda v: v.rearrange("p c t -> p (c t)")
                with dve.Fori(0, NS // 2) as i:
                    for k in range(2):
                        turn = b * NS + i * 2
                        dve.wait_ge(dA_ready, turn + (k + 1))
                        dve.wait_ge(dBx_ready, turn + (k + FREE + 1))
                        dve.wait_ge(hC_ready, turn + (k + START))
                        nc.vector.tensor_tensor_scan(flat(h[:]), flat(dA[:, k]), flat(dBx[:, k]), 0.0, ALU.mult, ALU.add
                                                     ).then_inc(scanned, 1)
                        dve.wait_ge(scanned, turn + (k + 1 + FREE))
                        dve.wait_ge(summed, b * (NS + 1) + i * 2 + (k + START))
                        nc.vector.tensor_tensor(hC[:, k], h[:], C_ps[k][:].unsqueeze(1).broadcast_to([P, CC, T]), ALU.mult
                                                ).then_inc(hC_ready, 1)
                dve.wait_ge(summed, b * (NS + 1) + (NS + 1 + START))
                for m in range(CC):
                    last = nc.vector.tensor_tensor(gated[:, m, :], y_ps[m][:], zs[:, m, :], ALU.mult)
                last.then_inc(gated_ready, 1)
                for t in range(TB):
                    row = xa[:, ds(b * TB + t, 1), :].rearrange("p a d -> p (a d)")
                    dve.wait_ge(out_ready, b * TB + (t + 1))
                    nc.vector.tensor_tensor(row, row, B_ps[t % 2][:, 0:D], ALU.add).then_inc(added, 1)
                chain.close()
                sequence_end(dve, b)

        @block.tensor
        def _(pe):
            pe.sem_inc(dBx_ready, FREE)
            for sem in (B_ready, hC_ready, bc_ready, summed):
                pe.sem_inc(sem, START)
            pe.wait_ge(loaded, LOADS)
            with pe.Fori(0, B) as b:
                for m in range(2 * CC):
                    if m >= CC:
                        pe.wait_ge(xp_ready, b * CC + (m - CC + 1))
                    for k in range(DC):
                        last = nc.tensor.matmul(y_ps[m % CC][:], win[:, k, m * P:(m + 1) * P], c.xnT[:, k, ds(b * T, T)],
                                                start=(k == 0), stop=(k == DC - 1))
                    last.then_inc(proj_ready, 1)
                pe.wait_ge(xc_ready, b * CC + CC)
                for m in range(CC):
                    last = nc.tensor.matmul(B_ps[0][0:LOW + DBC, :], wxp[:, m, :], xc[:, m, :], start=(m == 0),
                                            stop=(m == CC - 1))
                last.then_inc(dbc_ready, 1)
                pe.wait_ge(rank_ready, b + 1)
                pe.wait_ge(z_ready, b * CC + CC)
                for m in range(CC):
                    nc.tensor.matmul(y_ps[m][:], wdt[:, m * P:(m + 1) * P], low_rank[:], start=True, stop=True
                                     ).then_inc(step_ready, 1)

                def spread(k, turn):
                    pe.wait_ge(pick_ready, turn + 1)
                    for e, dst in enumerate((B_ps, C_ps)):
                        last = nc.tensor.matmul(dst[k][:], picked[:, k, e, :], parts[:], start=True, stop=True)
                    last.then_inc(bc_ready, 1)

                def add_up(k, first):
                    for m in range(CC):
                        last = nc.tensor.matmul(y_ps[m][:], c.ident[:], hC[:, k, m, :], start=first, stop=True,
                                                skip_group_check=True)
                    last.then_inc(summed, 1)

                pe.wait_ge(parts_ready, b + 1)
                spread(0, b * NS)
                pe.wait_ge(v_ready, b + 1)
                pe.wait_ge(skip_ready, b + 1)
                add_up(1, True)
                with pe.Fori(0, NS // 2 - 1) as i:
                    for k in range(2):
                        turn = b * NS + i * 2 + k
                        pe.wait_ge(B_ready, turn + START)
                        pe.wait_ge(hC_ready, turn + START)
                        spread(1 - k, turn + 1)
                        pe.wait_ge(hC_ready, turn + (1 + START))
                        add_up(k, False)
                end = b * NS + (NS - 2)
                pe.wait_ge(B_ready, end + START)
                pe.wait_ge(hC_ready, end + START)
                spread(1, end + 1)
                for k in range(2):
                    pe.wait_ge(hC_ready, end + (k + 1 + START))
                    add_up(k, False)
                pe.wait_ge(gated_ready, b + 1)
                for t in range(TB):
                    if t >= 2:
                        pe.wait_ge(added, b * TB + (t - 1))
                    for m in range(CC):
                        last = nc.tensor.matmul(B_ps[t % 2][:, 0:D], gated[:, m, t * P:(t + 1) * P], wout[:, m, :],
                                                start=(m == 0), stop=(m == CC - 1))
                    last.then_inc(out_ready, 1)
                sequence_end(pe, b)


def waves(nc, c, xa):
    EDGE = 2
    with Scope(nc, "wave") as s:
        wsi = s.sb("wsi", [P, DC, D])
        b_si = s.sb("bsi", [P, DC])
        gates = s.sb("gates", [P, 3, DC])
        alpha = s.sb("alpha", [P, DC])
        wso = s.sb("wso", [P, DC, D])
        b_so = s.sb("bso", [P, D])
        up = s.sb("up", [P, DC, T + 2 * EDGE])
        wide = lambda n: s.sb(n, [P, DC, T])
        turns, angle, sine, d1, d2, f, kdv, s1, heat, du = (
            wide(n) for n in ("turns", "angle", "sine", "d1", "d2", "f", "kdv", "s1", "heat", "du"))
        u_ps = [s.ps(f"u{k}", [P, T]) for k in range(DC)]
        out_ps = [s.ps(f"out{k}", [P, T]) for k in range(TB)]
        loaded = s.sem("loaded")
        ready0 = s.sem("ready0")
        based = s.sem("based")
        u_ready = s.sem("u_ready")
        inner_ready = s.sem("inner_ready")
        up_ready = s.sem("up_ready")
        angle_ready = s.sem("angle_ready")
        sine_ready = s.sem("sine_ready")
        kdv_ready = s.sem("kdv_ready")
        du_ready = s.sem("du_ready")
        out_ready = s.sem("out_ready")
        added = s.sem("added")
        vec = s.sem("vec")
        gps = s.sem("gps")
        passed = s.sem("passed")
        block = s.block()
        LOADS = 6 * 16
        START = 1
        at = lambda o: up[:, :, o:o + T]

        @block.sync
        def _(sp):
            for dst, src in ((wsi, "wsi"), (b_si, "bsi"), (gates, "gates"), (alpha, "alpha"), (wso, "wso")):
                sp.dma_start(dst[:], c.dram[f"wave_{src}"]).then_inc(loaded, 16)
            sp.dma_start(b_so[:], c.dram["wave_bso"].partition_broadcast(P)).then_inc(loaded, 16)

        @block.tensor
        def _(pe):
            pe.sem_inc(inner_ready, START)
            pe.sem_inc(du_ready, START)
            pe.sem_inc(sine_ready, START)
            pe.sem_inc(out_ready, START)
            pe.wait_ge(loaded, LOADS)
            with pe.Fori(0, B) as b:
                pe.wait_ge(inner_ready, b + START)
                for m in range(DC):
                    for k in range(DC):
                        last = nc.tensor.matmul(u_ps[m][:], wsi[:, k, m * P:(m + 1) * P], c.xnT[:, k, ds(b * T, T)],
                                                start=(k == 0), stop=(k == DC - 1))
                last.then_inc(u_ready, 1)
                pe.wait_ge(du_ready, b + (1 + START))
                for t in range(TB):
                    for k in range(DC):
                        last = nc.tensor.matmul(out_ps[t][:, 0:D], du[:, k, t * P:(t + 1) * P], wso[:, k, :],
                                                start=(k == 0), stop=(k == DC - 1))
                last.then_inc(out_ready, 1)

        @block.scalar
        def _(act):
            act.wait_ge(loaded, LOADS)
            with act.Fori(0, B) as b:
                act.wait_ge(u_ready, b + 1)
                act.wait_ge(du_ready, b + START)
                act.sem_inc(passed, 1)
                for m in range(DC):
                    last = nc.scalar.activation(up[:, m, EDGE:EDGE + T], u_ps[m][:], ACT.Identity, bias=b_si[:, m:m + 1])
                last.then_inc(inner_ready, 1)
                act.wait_ge(inner_ready, b + (1 + START))
                act.sem_inc(passed, 1)
                for to, edge in ((0, EDGE), (EDGE + T, EDGE + T - 1)):
                    last = nc.scalar.activation(up[:, :, to:to + EDGE], up[:, :, edge:edge + 1].broadcast_to([P, DC, EDGE]),
                                                ACT.Copy)
                last.then_inc(up_ready, 1)
                act.wait_ge(angle_ready, b + 1)
                nc.scalar.activation(sine[:], angle[:], ACT.Sin).then_inc(sine_ready, 1)

        @block.gpsimd
        def _(pool):
            pool.wait_ge(loaded, LOADS)
            nc.gpsimd.tensor_tensor(xa[:], xa[:], b_so[:].unsqueeze(1).broadcast_to([P, NT, D]), ALU.add).then_inc(based, 1)
            pool.wait_ge(based, 1)
            nc.gpsimd.tensor_tensor(c.x[:], c.x[:], xa[:], ALU.add).then_inc(based, 1)
            with pool.Fori(0, B) as b:
                chain = Chain(pool, gps, per=2)
                chain.start(b)
                pool.wait_ge(up_ready, b + 1)
                pool.sem_inc(passed, 1)
                nc.gpsimd.tensor_tensor(d1[:], at(3), at(1), ALU.subtract)
                chain.link(nc.gpsimd.tensor_scalar(f[:], at(2), -3.0, 1.0, ALU.mult, ALU.add))
                pool.wait_ge(du_ready, b + START)
                pool.sem_inc(passed, 1)
                chain.link(nc.gpsimd.tensor_tensor(kdv[:], f[:], d1[:], ALU.mult))
                nc.gpsimd.tensor_tensor(d2[:], at(4), at(0), ALU.subtract).then_inc(kdv_ready, 1)
                chain.close()

        @block.vector
        def _(dve):
            dve.wait_ge(loaded, LOADS)
            nc.vector.tensor_scalar(gates[:], gates[:], SOL, None, ALU.mult).then_inc(ready0, 1)
            dve.wait_ge(ready0, 1)
            dve.wait_ge(based, 2)
            with dve.Fori(0, B) as b:
                chain = Chain(dve, vec, per=9 + DC)
                chain.start(b)
                dve.wait_ge(up_ready, b + 1)
                dve.sem_inc(passed, 1)
                chain.link(nc.vector.tensor_scalar(turns[:], at(2), 1 / (2 * np.pi), TO_WHOLE, ALU.mult, ALU.add))
                chain.link(nc.vector.tensor_scalar(turns[:], turns[:], -TO_WHOLE, None, ALU.add))
                chain.link(nc.vector.scalar_tensor_tensor(out=angle[:], in0=turns[:], scalar=-TWO_PI_HIGH, in1=at(2),
                                                          op0=ALU.mult, op1=ALU.add))
                chain.link(nc.vector.scalar_tensor_tensor(out=angle[:], in0=turns[:], scalar=-TWO_PI_LOW, in1=angle[:],
                                                          op0=ALU.mult, op1=ALU.add))
                nc.vector.tensor_scalar(angle[:], angle[:], -PI, PI, ALU.max, ALU.min).then_inc(angle_ready, 1)
                chain.link(nc.vector.tensor_tensor(s1[:], at(3), at(1), ALU.add))
                nc.vector.scalar_tensor_tensor(out=s1[:], in0=at(2), scalar=-2.0, in1=s1[:], op0=ALU.mult, op1=ALU.add)
                for m in range(DC):
                    last = nc.vector.tensor_scalar(heat[:, m, :], up[:, m, EDGE:EDGE + T], alpha[:, m:m + 1], 1.0, ALU.mult, ALU.add)
                chain.link(last)
                chain.link(nc.vector.tensor_tensor(heat[:], heat[:], s1[:], ALU.mult))
                dve.wait_ge(kdv_ready, b + 1)
                chain.link(nc.vector.scalar_tensor_tensor(out=kdv[:], in0=d2[:], scalar=-0.5, in1=kdv[:], op0=ALU.mult, op1=ALU.add))
                dve.wait_ge(out_ready, b + START)
                dve.wait_ge(sine_ready, b + (1 + START))
                dve.sem_inc(passed, 1)
                for m in range(DC):
                    chain.link(nc.vector.tensor_scalar(sine[:, m, :], sine[:, m, :], gates[:, 0, m:m + 1], None, ALU.mult))
                for k, term in ((1, kdv), (2, heat)):
                    for m in range(DC):
                        last = nc.vector.scalar_tensor_tensor(out=du[:, m, :], in0=term[:, m, :], scalar=gates[:, k, m:m + 1],
                                                              in1=(sine if k == 1 else du)[:, m, :], op0=ALU.mult, op1=ALU.add)
                    if k == 1:
                        chain.link(last)
                last.then_inc(du_ready, 1)
                for t in range(TB):
                    row = c.x[:, ds(b * TB + t, 1), :].rearrange("p a d -> p (a d)")
                    dve.wait_ge(out_ready, b + (1 + START))
                    last = nc.vector.tensor_tensor(row, row, out_ps[t][:, 0:D], ALU.add)
                last.then_inc(added, 1)
                chain.close()


NE = 8
CAPACITY = -(-B * T * 5 // (NE * 4))


def lay_experts(a, rows, cols):
    p, f = np.arange(P)[:, None], np.arange(2 * B * T)[None, :]
    return {
        "moe_router": rows(a["L1_ffn_router_w"].T),
        "moe_w1": a["L1_ffn_W1"].reshape(NE, DC, P, DH).transpose(0, 2, 1, 3),
        "moe_b1": a["L1_ffn_b1"].reshape(NE, MH, P).transpose(2, 0, 1),
        "moe_w2": a["L1_ffn_W2"].reshape(NE, MH, P, D).transpose(0, 2, 1, 3),
        "moe_b2": a["L1_ffn_b2"].reshape(1, NE, D),
        "moe_before": (f - B * T < p).astype(np.float32),
        "moe_order": np.tile(np.arange(NE, 0, -1, dtype=np.float32), (P, 1)),
    }


def experts(nc, c):
    layernorm(nc, c, "moe_ln", c.x, c.xnT)
    NB = B * T // 512
    NT4 = 512 // P
    with Scope(nc, "moe_route") as s:
        router = s.sb("router", [P, DC, NE])
        order = s.sb("order", [P, NE])
        before = s.sb("before", [P, 2 * B * T])
        logits = s.sb("logits", [P, NT, NE])
        top = s.sb("top", [P, NT])
        is_top = s.sb("is_top", [P, NT, NE])
        mine = s.sb("mine", [P, 2, NT])
        wide = s.sb("wide", [P, 2, 2, 4, P])
        row = s.sb("row", [P, 2, B * T])
        rival = s.sb("rival", [P, B * T])
        hit = s.sb("hit", [P, B * T])
        place = s.sb("place", [P, NT, 2])
        keep = s.sb("keep", [P, NT])
        l_ps = s.ps("l_ps", [P, NT, NE])
        r_ps = [s.ps(f"r_ps{k}", [P, 512]) for k in range(4)]
        loaded = s.sem("loaded")
        l_ready = s.sem("l_ready")
        less_ready = s.sem("less_ready")
        exp_ready = s.sem("exp_ready")
        vec = s.sem("vec")
        vec_t = s.sem("vec_t")
        wide_ready = s.sem("wide_ready")
        turned = s.sem("turned")
        row_ready = s.sem("row_ready")
        block = s.block()

        @block.sync
        def _(sp):
            for dst, src in ((router, "router"), (order, "order"), (before, "before")):
                sp.dma_start(dst[:], c.dram[f"moe_{src}"]).then_inc(loaded, 16)

        @block.tensor
        def _(pe):
            pe.wait_ge(loaded, 48)
            for t in range(NT):
                for k in range(DC):
                    last = nc.tensor.matmul(l_ps[:, t, :], c.xnT[:, k, t * P:(t + 1) * P], router[:, k, :],
                                            start=(k == 0), stop=(k == DC - 1))
            last.then_inc(l_ready, 1)
            for g in range(NT // 4):
                pe.wait_ge(wide_ready, g + 1)
                if g >= 2:
                    pe.wait_ge(row_ready, g - 1)
                for e in range(2):
                    for t in range(4):
                        last = nc.tensor.transpose(r_ps[g % 2 * 2 + e][:, t * P:(t + 1) * P], wide[:, g % 2, e, t, :], c.ident[:])
                last.then_inc(turned, 1)

        @block.scalar
        def _(act):
            act.wait_ge(less_ready, 1)
            nc.scalar.activation(is_top[:], logits[:], ACT.Exp).then_inc(exp_ready, 1)
            for g in range(NT // 4):
                act.wait_ge(turned, g + 1)
                for e in range(2):
                    last = nc.scalar.activation(row[:, e, g * 512:(g + 1) * 512], r_ps[g % 2 * 2 + e][:], ACT.Copy)
                last.then_inc(row_ready, 1)

        @block.vector
        def _(dve):
            chain = Chain(dve, vec)
            over = lambda v: v.unsqueeze(2).broadcast_to([P, NT, NE])
            dve.wait_ge(loaded, 48)
            dve.wait_ge(l_ready, 1)
            chain.link(nc.vector.tensor_reduce(top[:], l_ps[:], AX, ALU.max))
            nc.vector.tensor_tensor(logits[:], l_ps[:], over(top[:]), ALU.subtract).then_inc(less_ready, 1)
            dve.wait_ge(exp_ready, 1)
            chain.link(nc.vector.tensor_reduce(top[:], is_top[:], AX, ALU.add))
            chain.link(nc.vector.reciprocal(mine[:, 1, :], top[:]))
            chain.link(nc.vector.scalar_tensor_tensor(out=is_top[:], in0=logits[:], scalar=0.0,
                                                      in1=order[:].unsqueeze(1).broadcast_to([P, NT, NE]),
                                                      op0=ALU.is_equal, op1=ALU.mult))
            chain.link(nc.vector.tensor_reduce(mine[:, 0, :], is_top[:], AX, ALU.max))
            for g in range(NT // 4):
                if g >= 2:
                    dve.wait_ge(turned, g - 1)
                for e in range(2):
                    last = nc.vector.tensor_copy(wide[:, g % 2, e], mine[:, e, g * 4:(g + 1) * 4].unsqueeze(2).broadcast_to([P, 4, P]))
                last.then_inc(wide_ready, 1)
            dve.wait_ge(row_ready, NT // 4)
            one = lambda v, t: v[:, ds(t, 1)]
            with dve.Fori(0, NT) as t:
                chain_t = Chain(dve, vec_t, per=3)
                chain_t.start(t)
                chain_t.link(nc.vector.scalar_tensor_tensor(out=rival[:], in0=row[:, 0, :], scalar=one(mine[:, 0, :], t),
                                                            in1=row[:, 1, :], op0=ALU.is_equal, op1=ALU.mult))
                chain_t.link(nc.vector.tensor_scalar(hit[:], rival[:], one(mine[:, 1, :], t), 0.0, ALU.is_gt, ALU.add,
                                                     accum_out=place[:, ds(t, 1), 0]))
                chain_t.link(nc.vector.scalar_tensor_tensor(out=hit[:], in0=rival[:], scalar=one(mine[:, 1, :], t),
                                                            in1=before[:, ds(t * -P + B * T, B * T)], op0=ALU.is_equal,
                                                            op1=ALU.mult, accum_out=place[:, ds(t, 1), 1]))
                chain_t.close()
            chain.link(nc.vector.tensor_tensor(keep[:], place[:, :, 0], place[:, :, 1], ALU.add))
            chain.link(nc.vector.tensor_scalar(keep[:], keep[:], float(CAPACITY), None, ALU.is_lt))
            chain.link(nc.vector.tensor_scalar(mine[:, 0, :], mine[:, 0, :], -1.0, float(NE), ALU.mult, ALU.add))
            chain.link(nc.vector.tensor_tensor(mine[:, 0, :], mine[:, 0, :], keep[:], ALU.mult))
            for e in range(NE):
                last = nc.vector.tensor_scalar(c.chosen[:, :, e], mine[:, 0, :], float(e), None, ALU.is_equal)

    with Scope(nc, "moe") as s:
        w1 = s.sb("w1", [P, 2, DC, DH])
        w2 = s.sb("w2", [P, 2, MH, D])
        b1 = s.sb("b1", [P, NE, MH])
        b2 = s.sb("b2", [1, NE, D])
        hid = [s.sb(f"hid{k}", [P, MH, 512]) for k in range(2)]
        mid = [s.ps(f"mid{k}", [P, 512]) for k in range(4)]
        low = [s.ps(f"low{k}", [P, 512]) for k in range(4)]
        loaded = s.sem("loaded")
        w_loaded = [s.sem(f"w_loaded{k}") for k in range(2)]
        mid_ready = s.sem("mid_ready")
        hid_ready = s.sem("hid_ready")
        out_ready = s.sem("out_ready")
        added = s.sem("added")
        passed = s.sem("passed")
        block = s.block()
        HT = NB * MH

        @block.sync
        def _(sp):
            sp.dma_start(b1[:], c.dram["moe_b1"]).then_inc(loaded, 16)
            sp.dma_start(b2[:], c.dram["moe_b2"]).then_inc(loaded, 16)
            with sp.Fori(0, NE // 2) as i:
                for k in range(2):
                    sp.wait_ge(out_ready, i * (2 * NT) + (k + 1) * NT)
                    sp.dma_start(w1[:, k], c.dram["moe_w1"][ds(i * 2 + k, 1)].rearrange("a p c m -> (a p) c m")).then_inc(w_loaded[k], 16)
                    sp.dma_start(w2[:, k], c.dram["moe_w2"][ds(i * 2 + k, 1)].rearrange("a p c m -> (a p) c m")).then_inc(w_loaded[k], 16)

        @block.scalar
        def _(act):
            act.wait_ge(loaded, 32)
            with act.Fori(0, NE // 2) as i:
                for k in range(2):
                    for n in range(HT):
                        tb, m = n // MH, n % MH
                        at = i * (2 * HT) + (k * HT + n + 1)
                        act.wait_ge(mid_ready, at)
                        act.sem_inc(passed, 1)
                        nc.scalar.activation(hid[tb % 2][:, m, :], mid[n % 4][:], ACT.Relu,
                                             bias=b1[:, ds(i * 2 + k, 1), m]).then_inc(hid_ready, 1)

        @block.vector
        def _(dve):
            with dve.Fori(0, NE // 2) as i:
                for k in range(2):
                    for t in range(NT):
                        dve.wait_ge(out_ready, i * (2 * NT) + (k * NT + t + 1 + 2 * NT))
                        nc.vector.scalar_tensor_tensor(out=c.x[:, t, :], in0=low[t % 4][:, 0:D],
                                                       scalar=c.chosen[:, t, ds(i * 2 + k, 1)], in1=c.x[:, t, :],
                                                       op0=ALU.mult, op1=ALU.add).then_inc(added, 1)

        @block.tensor
        def _(pe):
            pe.sem_inc(out_ready, 2 * NT)
            pe.sem_inc(hid_ready, 4)
            pe.sem_inc(added, 4)
            pe.wait_ge(loaded, 32)
            with pe.Fori(0, NE // 2) as i:
                for k in range(2):
                    pe.wait_ge(w_loaded[k], i * 32 + 32)
                    for tb in range(NB):
                        for m in range(MH):
                            n = tb * MH + m
                            pe.wait_ge(hid_ready, i * (2 * HT) + (k * HT + n + 1))
                            for d in range(DC):
                                last = nc.tensor.matmul(mid[n % 4][:], w1[:, k, d, m * P:(m + 1) * P],
                                                        c.xnT[:, d, tb * 512:(tb + 1) * 512], start=(d == 0), stop=(d == DC - 1))
                            last.then_inc(mid_ready, 1)
                        pe.wait_ge(hid_ready, i * (2 * HT) + (k * HT + (tb + 1) * MH + 4))
                        for t in range(NT4):
                            n = tb * NT4 + t
                            pe.wait_ge(added, i * (2 * NT) + (k * NT + n + 1))
                            pe.sem_inc(passed, 1)
                            nc.tensor.matmul(low[n % 4][:, 0:D], c.ones[0:1, :], b2[:, ds(i * 2 + k, 1), :].rearrange("p a d -> p (a d)"),
                                             start=True, stop=False)
                            for m in range(MH):
                                last = nc.tensor.matmul(low[n % 4][:, 0:D], hid[tb % 2][:, m, t * P:(t + 1) * P], w2[:, k, m, :],
                                                        start=False, stop=(m == MH - 1))
                            last.then_inc(out_ready, 1)


def store(nc, c):
    with Scope(nc, "store") as s:
        stored = s.sem("stored")
        block = s.block()

        @block.sync
        def _(sp):
            sp.dma_start(c.dram["out"], c.x[:]).then_inc(stored, 16)
            sp.wait_ge(stored, 16)


class Core:

    def __init__(self, dram):
        self.dram = dram


LAYERS = [gated_delta_net, masked_attention, ternary_mlp, selective_scan, full_attention, experts]


def program(nc, dram, layers=LAYERS):
    c = Core(dram)
    with ExitStack() as stack:
        c.x = stack.enter_context(nc.sbuf_tensor("x", [P, NT, D], F32))
        c.xnT = stack.enter_context(nc.sbuf_tensor("xnT", [P, DC, B * T], F32))
        c.ident = stack.enter_context(nc.sbuf_tensor("ident", [P, P], F32))
        c.ones = stack.enter_context(nc.sbuf_tensor("ones", [P, P], F32))
        c.eps = stack.enter_context(nc.sbuf_tensor("eps", [P, 1], F32))
        c.chosen = stack.enter_context(nc.sbuf_tensor("chosen", [P, NT, NE], F32))
        constants(nc, c)
        for layer in layers:
            layer(nc, c)
        store(nc, c)


def laid_out(inputs):
    a = {k: np.asarray(v) for k, v in inputs.items()}
    heads = lambda v, h: v.reshape(h, -1).T
    twice = lambda v: np.concatenate([v, v], 0)
    cols = lambda v: v.reshape(-1, P).T
    rows = lambda w: w.reshape(-1, P, w.shape[-1]).transpose(1, 0, 2)
    o = {
        "x": a["x"].reshape(NT, P, D).transpose(1, 0, 2),
        "ctxT": a["ctx_1024"].transpose(0, 2, 1).reshape(B, DC, P, S2).transpose(0, 2, 1, 3),
    }
    o.update(lay_gated_delta_net(a, rows, cols))
    o.update(lay_masked_attention(a, rows, cols))
    o.update(lay_ternary_mlp(a, rows, cols))
    o.update(lay_selective_scan(a, rows, cols))
    o.update(lay_full_attention(a, rows, cols))
    o.update(lay_experts(a, rows, cols))
    return {k: np.ascontiguousarray(v) for k, v in o.items()}


def kernel(**inputs):
    import concourse.bacc as bacc
    from concourse.bass_utils import run_bass_kernel_spmd

    nc = bacc.Bacc("TRN2", target_bir_lowering=False, num_devices=1)
    arrays = laid_out(inputs)
    dram = {k: nc.dram_tensor(f"in_{k}", v.shape, mybir.dt.from_np(v.dtype), kind="ExternalInput").ap()
            for k, v in arrays.items()}
    dram["out"] = nc.dram_tensor("out_0", [P, NT, D], F32, kind="ExternalOutput").ap()
    program(nc, dram)
    r = run_bass_kernel_spmd(nc, [{f"in_{k}": v for k, v in arrays.items()}], core_ids=[0])
    return r.results[0]["out_0"].transpose(1, 0, 2).reshape(B, T, D)
```

```python
from contextlib import ExitStack

import numpy as np

import concourse.bass as bass
from concourse import mybir

ALU = mybir.AluOpType
ACT = mybir.ActivationFunctionType
AX = mybir.AxisListType.X
F32 = mybir.dt.float32
F32R = mybir.dt.float32r
BF16 = mybir.dt.bfloat16
U8 = mybir.dt.uint8
I32 = mybir.dt.int32

P = 128
B, T, D = 4, 512, 256
DC = D // P
NT = B * T // P
TB = T // P
S2 = 1601
KT = -(-S2 // P)
SW = -(-S2 // 4)
LAST = S2 - (KT - 1) * P
NEG = -1.0e30
ds = bass.ds


class Scope:

    def __init__(self, nc, name):
        self.nc, self.name, self.stack, self.sems = nc, name, ExitStack(), []

    def __enter__(self):
        return self

    def __exit__(self, *failure):
        self.stack.close()
        if self.sems:
            self.nc.clear_and_free_semaphores(self.sems)
            self.nc.all_engine_barrier()

    def sb(self, name, shape, dt=F32):
        return self.stack.enter_context(self.nc.sbuf_tensor(f"{self.name}_{name}", shape, dt))

    def ps(self, name, shape, dt=F32):
        return self.stack.enter_context(self.nc.psum_tensor(f"{self.name}_{name}", shape, dt))

    def sem(self, name):
        self.sems.append(self.nc.alloc_semaphore(f"{self.name}_{name}"))
        return self.sems[-1]

    def block(self):
        return self.stack.enter_context(self.nc.Block())


class Chain:

    def __init__(self, eng, sem, per=0, base=0):
        self.eng, self.sem, self.per, self.n, self.turn, self.base = eng, sem, per, 0, 0, base

    def start(self, turn):
        assert self.n in (0, self.per), (self.n, self.per)
        self.turn, self.n = turn, 0

    def link(self, ins):
        self.n += 1
        ins.then_inc(self.sem, 1)
        self.eng.wait_ge(self.sem, self.turn * self.per + (self.base + self.n))

    def close(self):
        assert self.n == self.per, (self.n, self.per)


def constants(nc, c):
    with Scope(nc, "const") as s:
        made = s.sem("made")
        loaded = s.sem("loaded")
        block = s.block()

        @block.gpsimd
        def _(pool):
            nc.gpsimd.memset(c.ident[:], 0.0).then_inc(made, 1)
            nc.gpsimd.memset(c.ones[:], 1.0).then_inc(made, 1)
            nc.gpsimd.memset(c.eps[:], 1e-5).then_inc(made, 1)
            pool.wait_ge(made, 1)
            nc.gpsimd.affine_select(out=c.ident[:], in_=c.ident[:], compare_op=ALU.not_equal, fill=1.0,
                                    base=0, pattern=[[-1, P]], channel_multiplier=1).then_inc(made, 1)

        @block.sync
        def _(sp):
            sp.dma_start(c.x[:], c.dram["x"]).then_inc(loaded, 16)
            sp.wait_ge(loaded, 16)


def layernorm(nc, c, name, src, dst, gain=None, shift=None, keep=None):
    GROUPS = NT // 4
    FREE = 2
    with Scope(nc, name) as s:
        stats = s.sb("stats", [P, 2, 4, 6])
        mv = s.sb("mv", [P, 2, 4, 2])
        std = s.sb("std", [P, 2, 4])
        rstd = s.sb("rstd", [P, 2, 4])
        xn = s.sb("xn", [P, 2, 4, D])
        turned_ps = [s.ps(f"turned{k}", [P, DC, 512]) for k in range(2)]
        vec = s.sem("vec")
        stats_ready = s.sem("stats_ready")
        std_ready = s.sem("std_ready")
        xn_ready = s.sem("xn_ready")
        turned = s.sem("turned")
        copied = s.sem("copied")
        passed = s.sem("passed")
        block = s.block()

        @block.vector
        def _(dve):
            chain = Chain(dve, vec, per=6 if keep is not None else 4)
            with dve.Fori(0, GROUPS // 2) as i:
                chain.start(i)
                for k in range(2):
                    tile = [ds((i * 2 + k) * 4 + t, 1) for t in range(4)]
                    for t in range(4):
                        last = nc.vector.bn_stats(stats[:, k, t, :], src[:, tile[t], :])
                    chain.link(last)
                    dve.sem_inc(passed, 1)
                    for t in range(4):
                        last = nc.vector.bn_aggr(mv[:, k, t, :], stats[:, k, t, :])
                    last.then_inc(stats_ready, 1)
                    dve.wait_ge(std_ready, i * 2 + (k + 1))
                    chain.link(nc.vector.reciprocal(rstd[:, k, :], std[:, k, :]))
                    dve.wait_ge(turned, i * 2 + (k + FREE - 1))
                    for t in range(4):
                        last = nc.vector.tensor_scalar(xn[:, k, t, :], src[:, tile[t], :],
                                                       mv[:, k, t, 0:1], rstd[:, k, t:t + 1],
                                                       ALU.subtract, ALU.mult)
                    last.then_inc(xn_ready, 1)
                    if keep is not None:
                        for t in range(4):
                            last = nc.vector.tensor_scalar(keep[:, tile[t], :], src[:, tile[t], :],
                                                           mv[:, k, t, 0:1], rstd[:, k, t:t + 1],
                                                           ALU.subtract, ALU.mult)
                        chain.link(last)
                chain.close()

        @block.scalar
        def _(act):
            with act.Fori(0, GROUPS // 2) as i:
                for k in range(2):
                    act.wait_ge(stats_ready, i * 2 + (k + 1))
                    nc.scalar.activation(std[:, k, :], mv[:, k, :, 1], ACT.Sqrt, bias=c.eps[:]).then_inc(std_ready, 1)
                    act.wait_ge(turned, i * 2 + (k + 1 + FREE))
                    for d in range(DC):
                        out = dst[:, d, ds((i * 2 + k) * 512, 512)]
                        last = nc.scalar.activation(out, turned_ps[k][:, d, :], ACT.Identity,
                                                    bias=shift[:, d:d + 1] if shift is not None else 0.0,
                                                    scale=gain[:, d:d + 1] if gain is not None else 1.0)
                    last.then_inc(copied, 1)

        @block.tensor
        def _(pe):
            pe.sem_inc(turned, FREE)
            pe.sem_inc(copied, FREE)
            with pe.Fori(0, GROUPS // 2) as i:
                for k in range(2):
                    pe.wait_ge(xn_ready, i * 2 + (k + 1))
                    pe.wait_ge(copied, i * 2 + (k + FREE - 1))
                    for d in range(DC):
                        for t in range(4):
                            last = nc.tensor.transpose(turned_ps[k][:, d, t * P:(t + 1) * P],
                                                       xn[:, k, t, d * P:(d + 1) * P], c.ident[:])
                    last.then_inc(turned, 1)


HV, HK, DK = 16, 8, 64
LEVELS = 7
KOFF, VOFF = HK * DK, 2 * HK * DK
CONV = 4


def lay_gated_delta_net(a, rows, cols):
    p, f = np.arange(P)[:, None], np.arange(P)[None, :]
    levels = np.stack([(p >> s + 1 == f >> s + 1) & (p >> s & 1 == 1) & (f >> s & 1 == 0)
                       for s in range(LEVELS)], 1).astype(np.float32)
    return {
        "gdn_wqkv": rows(a["L0_attn_W_qkv"]),
        "gdn_wz": rows(a["L0_attn_W_z"]),
        "gdn_wba": rows(np.concatenate([a["L0_attn_W_b"], a["L0_attn_W_a"]], 1)),
        "gdn_wout": rows(a["L0_attn_W_out"]),
        "gdn_conv": a["L0_attn_conv_w"].reshape(-1, P, CONV).transpose(1, 0, 2),
        "gdn_dt_bias": a["L0_attn_dt_bias"],
        "gdn_A_log": a["L0_attn_A_log"],
        "gdn_norm": a["L0_attn_norm_w"],
        "gdn_levels": levels,
        "gdn_upto": (p <= f).astype(np.float32),
    }


def gated_delta_net(nc, c):
    layernorm(nc, c, "gdn_ln", c.x, c.xnT)
    NM = 2 * HK * DK // P + HV * DK // P
    HG = HV // 4
    NZ = HV * DK // 512
    with Scope(nc, "gdn") as s:
        wqkv = s.sb("wqkv", [P, DC, NM * P])
        wz = s.sb("wz", [P, DC, HV * DK])
        wba = s.sb("wba", [P, DC, 2 * HV])
        wout = s.sb("wout", [P, HV * DK // P, D])
        convw = s.sb("convw", [P, NM, CONV])
        dt_bias = s.sb("dt_bias", [P, HV])
        neg_a = s.sb("neg_a", [P, HV])
        norm_w = s.sb("norm_w", [P, DK])
        levels = s.sb("levels", [P, LEVELS, P])
        upto = s.sb("upto", [P, P])
        eps = s.sb("eps", [P, 1])
        xb = s.sb("xb", [P, DC, T])
        conv = s.sb("conv", [P, 2, T])
        act_ct = s.sb("act_ct", [P, 2, T])
        qkv = s.sb("qkv", [P, TB, NM * P])
        gate = s.sb("gate", [P, TB, HV * DK])
        o = s.sb("o", [P, TB, HV * DK])
        osq = qkv[:, 0:TB // 2, :].rearrange("p a (b n) -> p (a b) n", n=HV * DK)
        oT = qkv[:, TB // 2:TB, :].rearrange("p a (b n) -> p (a b) n", n=T)
        col = lambda n, h=HV: s.sb(n, [P, TB, h])
        beta, g, G, eG, eGl, eGend = (col(n) for n in ("beta", "g", "G", "eG", "eGl", "eGend"))
        u1, u2, u3 = (col(n) for n in ("u1", "u2", "u3"))
        k_in, k_out, q_in = (col(n) for n in ("k_in", "k_out", "q_in"))
        ss = col("ss")
        rn = col("rn")
        Kn, Qn = (s.sb(n, [P, 2, 2, DK]) for n in ("Kn", "Qn"))
        Kb, Kd, Qe, Vb = (s.sb(n, [P, 2, 4, DK]) for n in ("Kb", "Kd", "Qe", "Vb"))
        Ug = s.sb("Ug", [P, 2, 4, P])
        kqT = s.sb("kqT", [P, 6, P])
        dd = s.sb("dd", [P, 4, P])
        ad = s.sb("ad", [P, 4, P])
        E = s.sb("E", [P, 4, P])
        EU = s.sb("EU", [P, 4, P])
        Tm = s.sb("Tm", [P, 2, 2, P])
        PT = s.sb("PT", [P, 4, P])
        M = s.sb("M", [P, 4, LEVELS, P])
        XX = s.sb("XX", [P, 2, 2, 2, P])
        Y = s.sb("Y", [P, 4, P])
        Bm = s.sb("Bm", [P, 4, DK])
        U = s.sb("U", [P, 4, DK])
        S = s.sb("S", [P, 2, P])

        tps = s.ps("tps", [P, 8, P])
        wps = [s.ps(f"wps{k}", [P, 2, 2, P]) for k in range(2)]
        gps = s.ps("gps", [P, 4, P])
        kps = s.ps("kps", [P, 2, 2, P])
        yps = [s.ps(f"yps{k}", [P, 4, P]) for k in range(2)]
        proj = [tps[:, 0:4, :].rearrange("p a b -> p (a b)"), tps[:, 4:8, :].rearrange("p a b -> p (a b)")]
        zps = [gps[:].rearrange("p a b -> p (a b)"), kps[:].rearrange("p a b c -> p (a b c)")]
        trps = [w[:].rearrange("p a b c -> p (a b) c") for w in wps]
        ba_ps = yps[0][:, 0, :].rearrange("p (t h) -> p t h", t=TB)
        G_ps, end_ps = (yps[1][:, n, 0:TB * HV].rearrange("p (t h) -> p t h", t=TB) for n in range(2))
        m0_ps = wps[0][:]
        r_ps = gps[:, 0:2, :]
        u_ps = gps[:, 2:4, :].rearrange("p a (b d) -> p (a b) d", b=2)
        o_ps = kps[:, 0, :, :].rearrange("p a b -> p (a b)")
        s_ps = gps[:, 0:2, :]

        loaded = s.sem("loaded")
        ready0 = s.sem("ready0")
        xb_ready = s.sem("xb_ready")
        proj_ready = s.sem("proj_ready")
        conv_ready = s.sem("conv_ready")
        act_ready = s.sem("act_ready")
        tr_ready = s.sem("tr_ready")
        tr_copied = s.sem("tr_copied")
        z_ready = s.sem("z_ready")
        z_copied = s.sem("z_copied")
        ba_ready = s.sem("ba_ready")
        gate_sum = s.sem("gate_sum")
        softplus_ready = s.sem("softplus_ready")
        g_ready = s.sem("g_ready")
        Gsum_ready = s.sem("Gsum_ready")
        gl_ready = s.sem("gl_ready")
        exp_ready = s.sem("exp_ready")
        sq_ready = s.sem("sq_ready")
        ss_ready = s.sem("ss_ready")
        len_ready = s.sem("len_ready")
        vec_a = s.sem("vec_a")
        vec_t = s.sem("vec_t")
        vec_e = s.sem("vec_e")
        act_a = s.sem("act_a")
        act_t = s.sem("act_t")
        meet = s.sem("meet")
        prep_ready = s.sem("prep_ready")
        turned = s.sem("turned")
        kqT_ready = s.sem("kqT_ready")
        grow_ready = s.sem("grow_ready")
        kk_low = s.sem("kk_low")
        kk_ready = s.sem("kk_ready")
        dd_ready = s.sem("dd_ready")
        E_ready = s.sem("E_ready")
        EU_ready = s.sem("EU_ready")
        M_ready = s.sem("M_ready")
        PT_ready = s.sem("PT_ready")
        Tm_ready = s.sem("Tm_ready")
        m0_ready = s.sem("m0_ready")
        X0_ready = s.sem("X0_ready")
        y_ready = s.sem("y_ready")
        y_copied = s.sem("y_copied")
        w_ready = s.sem("w_ready")
        X_ready = s.sem("X_ready")
        r_ready = s.sem("r_ready")
        B_ready = s.sem("B_ready")
        u_ready = s.sem("u_ready")
        U_ready = s.sem("U_ready")
        o_ready = s.sem("o_ready")
        o_copied = s.sem("o_copied")
        s_ready = s.sem("s_ready")
        S_ready = s.sem("S_ready")
        osq_ready = s.sem("osq_ready")
        ovar_ready = s.sem("ovar_ready")
        ostd_ready = s.sem("ostd_ready")
        on_ready = s.sem("on_ready")
        oT_ready = s.sem("oT_ready")
        oT_copied = s.sem("oT_copied")
        out_ready = s.sem("out_ready")
        added = s.sem("added")
        passed = s.sem("passed")
        block = s.block()
        LOADS = 10 * 16
        WORKERS = 4
        STAGES = 3

        def stage_end(eng, b, stage):
            eng.drain().then_inc(meet, 1)
            eng.wait_ge(meet, b * (STAGES * WORKERS) + (stage + 1) * WORKERS)
            eng.sem_inc(passed, 1)

        @block.sync
        def _(sp):
            for dst, src in ((wqkv, "wqkv"), (convw, "conv"), (wz, "wz"), (wba, "wba"), (levels, "levels"),
                             (upto, "upto"), (wout, "wout")):
                sp.dma_start(dst[:], c.dram[f"gdn_{src}"]).then_inc(loaded, 16)
            for dst, src in ((dt_bias, "dt_bias"), (neg_a, "A_log"), (norm_w, "norm")):
                sp.dma_start(dst[:], c.dram[f"gdn_{src}"].partition_broadcast(P)).then_inc(loaded, 16)

        @block.gpsimd
        def _(pool):
            nc.gpsimd.memset(eps[:], 1e-6).then_inc(ready0, 1)
            pool.wait_ge(loaded, LOADS)
            with pool.Fori(0, B) as b:
                pool.wait_ge(z_copied, b * (TB * NZ) + TB * NZ)
                for t in range(TB):
                    zt = gate[:, t, :].rearrange("p (h d) -> p h d", d=DK)
                    nc.gpsimd.tensor_tensor(zt, zt, norm_w[:].unsqueeze(1).broadcast_to([P, HV, DK]), ALU.mult)
                stage_end(pool, b, 0)
                with pool.Fori(0, HG) as hg:
                    for ch in range(TB):
                        pool.wait_ge(E_ready, (b * HG + hg) * TB + (ch + 1))
                        nc.gpsimd.tensor_tensor(EU[:], E[:], upto[:].unsqueeze(1).broadcast_to([P, 4, P]),
                                                ALU.mult).then_inc(EU_ready, 1)
                stage_end(pool, b, 1)
                stage_end(pool, b, 2)

        @block.scalar
        def _(act):
            act.wait_ge(loaded, LOADS)
            act.wait_ge(ready0, 1)
            nc.scalar.activation(neg_a[:], neg_a[:], ACT.Exp).then_inc(ready0, 1)
            with act.Fori(0, B) as b:
                chain = Chain(act, act_a, per=2)
                chain.start(b)
                nc.scalar.activation(xb[:], c.xnT[:, :, ds(b * T, T)], ACT.Copy).then_inc(xb_ready, 1)

                def turn_copy(m):
                    act.wait_ge(tr_ready, b * NM + (m + 1))
                    nc.scalar.activation(qkv[:, :, m * P:(m + 1) * P], trps[m % 2], ACT.Copy).then_inc(tr_copied, 1)

                for m in range(NM):
                    act.wait_ge(conv_ready, b * NM + (m + 1))
                    if m >= 2:
                        act.wait_ge(tr_ready, b * NM + (m - 1))
                    nc.scalar.activation(act_ct[:, m % 2, :], conv[:, m % 2, :], ACT.Silu).then_inc(act_ready, 1)
                    if m >= 1:
                        turn_copy(m - 1)
                turn_copy(NM - 1)
                for n in range(TB * NZ):
                    act.wait_ge(z_ready, b * (TB * NZ) + (n + 1))
                    nc.scalar.activation(gate[:, n // NZ, (n % NZ) * 512:(n % NZ + 1) * 512], zps[n % 2],
                                         ACT.Silu).then_inc(z_copied, 1)
                act.wait_ge(gate_sum, b + 1)
                nc.scalar.activation(u1[:], u1[:], ACT.Exp, scale=-1.0)
                chain.link(nc.scalar.activation(u3[:], u2[:], ACT.Abs))
                chain.link(nc.scalar.activation(u3[:], u3[:], ACT.Exp, scale=-1.0))
                nc.scalar.activation(u3[:], u3[:], ACT.Ln, bias=1.0).then_inc(softplus_ready, 1)
                act.wait_ge(gl_ready, b + 1)
                nc.scalar.activation(eG[:], G[:], ACT.Exp)
                nc.scalar.activation(eGend[:], eGend[:], ACT.Exp)
                nc.scalar.activation(eGl[:], u1[:], ACT.Exp).then_inc(exp_ready, 1)
                nc.scalar.activation(o[:], qkv[:, :, 0:VOFF], ACT.Square).then_inc(sq_ready, 1)
                act.wait_ge(ss_ready, b + 1)
                nc.scalar.activation(ss[:], ss[:], ACT.Sqrt, bias=eps[:]).then_inc(len_ready, 1)
                chain.close()
                stage_end(act, b, 0)
                with act.Fori(0, HG) as hg:
                    turn = b * HG + hg
                    chain = Chain(act, act_t, per=TB)
                    chain.start(turn)
                    for ch in range(TB):
                        act.wait_ge(turned, turn * TB + (ch + 1))
                        nc.scalar.activation(kqT[:], tps[:, 0:6, :], ACT.Copy).then_inc(kqT_ready, 1)
                        act.wait_ge(dd_ready, turn * TB + (ch + 1))
                        chain.link(nc.scalar.activation(ad[:], dd[:], ACT.Abs))
                        nc.scalar.activation(E[:], ad[:], ACT.Exp, scale=-1.0).then_inc(E_ready, 1)
                        for lv in range(1, LEVELS):
                            for half in range(2):
                                act.wait_ge(y_ready, turn * (TB * 12) + (ch * 12 + (lv - 1) * 2 + half + 1))
                                nc.scalar.activation(Y[:, 2 * half:2 * half + 2, :], yps[half][:, 0:2, :], ACT.Copy).then_inc(y_copied, 1)
                        act.wait_ge(u_ready, turn * TB + (ch + 1))
                        nc.scalar.activation(U[:], u_ps, ACT.Copy).then_inc(U_ready, 1)
                        act.wait_ge(o_ready, turn * TB + (ch + 1))
                        nc.scalar.activation(o[:, ch, ds(hg * (4 * DK), 4 * DK)], o_ps, ACT.Copy).then_inc(o_copied, 1)
                    chain.close()
                stage_end(act, b, 1)
                nc.scalar.activation(osq, o[:], ACT.Square).then_inc(osq_ready, 1)
                act.wait_ge(ovar_ready, b + 1)
                nc.scalar.activation(ss[:], ss[:], ACT.Sqrt, bias=eps[:], scale=1.0 / DK).then_inc(ostd_ready, 1)
                for m in range(HV * DK // P):
                    act.wait_ge(oT_ready, b * (HV * DK // P) + (m + 1))
                    nc.scalar.activation(oT[:, m, :], proj[m % 2], ACT.Copy).then_inc(oT_copied, 1)
                stage_end(act, b, 2)

        @block.vector
        def _(dve):
            dve.wait_ge(loaded, LOADS)
            dve.wait_ge(ready0, 2)
            nc.vector.tensor_scalar(neg_a[:], neg_a[:], -1.0, None, ALU.mult).then_inc(ready0, 1)
            dve.wait_ge(ready0, 3)
            with dve.Fori(0, B) as b:
                chain = Chain(dve, vec_a, per=NM * 3 + 7)
                chain.start(b)
                for m in range(NM):
                    dve.wait_ge(proj_ready, b * NM + (m + 1))
                    if m >= 2:
                        dve.wait_ge(act_ready, b * NM + (m - 1))
                    y, x = conv[:, m % 2, :], proj[m % 2]
                    chain.link(nc.vector.tensor_scalar(y, x, convw[:, m, CONV - 1:CONV], None, ALU.mult))
                    for back in range(1, CONV):
                        last = nc.vector.scalar_tensor_tensor(
                            out=y[:, back:], in0=x[:, :T - back], scalar=convw[:, m, CONV - 1 - back:CONV - back],
                            in1=y[:, back:], op0=ALU.mult, op1=ALU.add)
                        if back < CONV - 1:
                            chain.link(last)
                    last.then_inc(conv_ready, 1)
                heads = lambda v: v.unsqueeze(1).broadcast_to([P, TB, HV])
                dve.wait_ge(ba_ready, b + 1)
                nc.vector.tensor_copy(u1[:], ba_ps[:, :, 0:HV])
                nc.vector.tensor_tensor(u2[:], ba_ps[:, :, HV:2 * HV], heads(dt_bias[:]), ALU.add).then_inc(gate_sum, 1)
                dve.wait_ge(softplus_ready, b + 1)
                chain.link(nc.vector.tensor_scalar(u1[:], u1[:], 1.0, None, ALU.add))
                chain.link(nc.vector.reciprocal(beta[:], u1[:]))
                chain.link(nc.vector.scalar_tensor_tensor(out=u3[:], in0=u2[:], scalar=0.0, in1=u3[:],
                                                          op0=ALU.max, op1=ALU.add))
                nc.vector.tensor_tensor(g[:], u3[:], heads(neg_a[:]), ALU.mult).then_inc(g_ready, 1)
                dve.wait_ge(Gsum_ready, b + 1)
                nc.vector.tensor_copy(G[:], G_ps)
                chain.link(nc.vector.tensor_copy(eGend[:], end_ps))
                nc.vector.tensor_tensor(u1[:], eGend[:], G[:], ALU.subtract).then_inc(gl_ready, 1)
                dve.wait_ge(sq_ready, b + 1)
                nc.vector.tensor_reduce(ss[:].rearrange("p t h -> p (t h)"),
                                        o[:].rearrange("p t (h d) -> p (t h) d", d=DK), AX, ALU.add).then_inc(ss_ready, 1)
                dve.wait_ge(len_ready, b + 1)
                chain.link(nc.vector.reciprocal(rn[:], ss[:]))
                rq, rk = rn[:, :, 0:HK], rn[:, :, HK:2 * HK]
                chain.link(nc.vector.tensor_scalar(rq, rq, float(DK) ** -0.5, None, ALU.mult))
                dve.wait_ge(exp_ready, b + 1)
                both = lambda v: v.unsqueeze(3).broadcast_to([P, TB, HK, 2])
                split = lambda v: v.rearrange("p t (h r) -> p t h r", r=2)
                chain.link(nc.vector.tensor_tensor(k_in[:], beta[:], eG[:], ALU.mult))
                nc.vector.tensor_tensor(split(k_in[:]), split(k_in[:]), both(rk), ALU.mult)
                nc.vector.tensor_tensor(split(k_out[:]), split(eGl[:]), both(rk), ALU.mult)
                nc.vector.tensor_tensor(split(q_in[:]), split(eG[:]), both(rq), ALU.mult)
                chain.close()
                stage_end(dve, b, 0)
                with dve.Fori(0, HG) as hg:
                    turn = b * HG + hg
                    chain = Chain(dve, vec_t, per=1)
                    chain.start(turn)

                    def prep(ch):
                        k = ch % 2
                        q = qkv[:, ch, ds(hg * P, P)].rearrange("p (h d) -> p h d", d=DK)
                        kk = qkv[:, ch, ds(hg * P + KOFF, P)].rearrange("p (h d) -> p h d", d=DK)
                        v = qkv[:, ch, ds(hg * (2 * P) + VOFF, 2 * P)].rearrange("p (h d) -> p h d", d=DK)
                        key = lambda w, at: w[:, ch, ds(hg * 2 + at, 2)].unsqueeze(2).broadcast_to([P, 2, DK])
                        four = lambda w, n: w[:, ch, ds(hg * 4, 4)].unsqueeze(2).broadcast_to([P, 4, n])
                        twice = lambda w: w.unsqueeze(2).broadcast_to([P, 2, 2, DK])
                        value = lambda w: w[:, ch, ds(hg * 4, 4)].rearrange(
                            "p (h r) -> p h r", r=2).unsqueeze(3).broadcast_to([P, 2, 2, DK])
                        by_key = lambda w: w[:, k].rearrange("p (h r) d -> p h r d", r=2)
                        nc.vector.tensor_tensor(Kn[:, k], kk, key(rn, HK), ALU.mult)
                        nc.vector.tensor_tensor(Qn[:, k], q, key(rn, 0), ALU.mult)
                        nc.vector.tensor_tensor(by_key(Kb), twice(kk), value(k_in), ALU.mult)
                        nc.vector.tensor_tensor(by_key(Kd), twice(kk), value(k_out), ALU.mult)
                        nc.vector.tensor_tensor(by_key(Qe), twice(q), value(q_in), ALU.mult)
                        nc.vector.tensor_tensor(Vb[:, k], v, four(beta, DK), ALU.mult)
                        nc.vector.tensor_tensor(Ug[:, k], upto[:].unsqueeze(1).broadcast_to([P, 4, P]), four(g, P),
                                                ALU.mult).then_inc(prep_ready, 1)

                    dve.wait_ge(S_ready, turn * TB + 1)
                    chain.link(nc.vector.memset(S[:], 0.0))
                    prep(0)
                    for ch in range(TB):
                        at = turn * TB + (ch + 1)
                        dve.wait_ge(grow_ready, at)
                        nc.vector.tensor_tensor(dd[:], gps[:], G[:, ch, ds(hg * 4, 4)].unsqueeze(2).broadcast_to([P, 4, P]),
                                                ALU.subtract).then_inc(dd_ready, 1)
                        kqT_ps = kps[:, :, 1, :].unsqueeze(2).broadcast_to([P, 2, 2, P])
                        by_key = lambda w: w[:].rearrange("p (h r) t -> p h r t", r=2)
                        dve.wait_ge(kk_ready, at)
                        for h in range(4):
                            last = nc.vector.scalar_tensor_tensor(
                                out=M[:, h], in0=kps[:, h // 2, 0, :].unsqueeze(1).broadcast_to([P, LEVELS, P]),
                                scalar=beta[:, ch, ds(hg * 4 + h, 1)], in1=levels[:], op0=ALU.mult, op1=ALU.mult)
                        last.then_inc(M_ready, 1)
                        one = c.ident[:].unsqueeze(1).unsqueeze(1).broadcast_to([P, 2, 2, P])
                        halves = lambda w: w.rearrange("p (a h) t -> p a h t", a=2)
                        dve.wait_ge(M_ready, at)
                        nc.vector.tensor_tensor(XX[:, :, 1], one, halves(M[:, :, 0, :]), ALU.subtract)
                        dve.wait_ge(m0_ready, at)
                        nc.vector.tensor_tensor(XX[:, :, 0], one, m0_ps, ALU.subtract).then_inc(X0_ready, 1)
                        for lv in range(1, LEVELS):
                            for half in range(2):
                                dve.wait_ge(w_ready, turn * (TB * 12) + (ch * 12 + (lv - 1) * 2 + half + 1))
                                n = 2 if lv < LEVELS - 1 else 1
                                nc.vector.tensor_tensor(XX[:, half, 0:n], XX[:, half, 0:n], wps[half][:, 0:n],
                                                        ALU.subtract).then_inc(X_ready, 1)
                            if lv == 1:
                                dve.wait_ge(EU_ready, at)
                                nc.vector.tensor_tensor(by_key(PT), kqT_ps, by_key(EU), ALU.mult).then_inc(PT_ready, 1)
                            if lv == 3 and ch + 1 < TB:
                                prep(ch + 1)
                        dve.wait_ge(X_ready, turn * (TB * 12) + (ch + 1) * 12)
                        nc.vector.tensor_tensor(Tm[:], XX[:, :, 0], E[:].rearrange("p (a h) t -> p a h t", a=2),
                                                ALU.mult).then_inc(Tm_ready, 1)
                        dve.wait_ge(r_ready, at)
                        nc.vector.tensor_tensor(Bm[:], Vb[:, ch % 2], r_ps.rearrange("p a (b d) -> p (a b) d", d=DK),
                                                ALU.subtract).then_inc(B_ready, 1)
                        dve.wait_ge(s_ready, at)
                        for h in range(4):
                            rows, cs = slice(DK * (h % 2), DK * (h % 2) + DK), slice(DK * (h % 2), DK * (h % 2) + DK)
                            last = nc.vector.scalar_tensor_tensor(
                                out=S[rows, h // 2, cs], in0=S[rows, h // 2, cs],
                                scalar=eGend[rows, ch, ds(hg * 4 + h, 1)], in1=s_ps[rows, h // 2, cs],
                                op0=ALU.mult, op1=ALU.add)
                        last.then_inc(S_ready, 1)
                    chain.close()
                stage_end(dve, b, 1)
                dve.wait_ge(osq_ready, b + 1)
                nc.vector.tensor_reduce(ss[:].rearrange("p t h -> p (t h)"),
                                        osq.rearrange("p t (h d) -> p (t h) d", d=DK), AX,
                                        ALU.add).then_inc(ovar_ready, 1)
                dve.wait_ge(ostd_ready, b + 1)
                chain = Chain(dve, vec_e, per=2)
                chain.start(b)
                chain.link(nc.vector.reciprocal(rn[:], ss[:]))
                oh = o[:].rearrange("p t (h d) -> p (t h) d", d=DK)
                chain.link(nc.vector.tensor_tensor(oh, oh, rn[:].rearrange("p t h -> p (t h)").unsqueeze(2).broadcast_to(
                    [P, TB * HV, DK]), ALU.mult))
                nc.vector.tensor_tensor(o[:], o[:], gate[:], ALU.mult).then_inc(on_ready, 1)
                chain.close()
                for t in range(TB):
                    dve.wait_ge(out_ready, b * TB + (t + 1))
                    row = c.x[:, ds(b * TB + t, 1), :].rearrange("p a d -> p (a d)")
                    nc.vector.tensor_tensor(row, row, zps[t % 2][:, 0:D], ALU.add).then_inc(added, 1)
                stage_end(dve, b, 2)

        @block.tensor
        def _(pe):
            pe.wait_ge(loaded, LOADS)
            pe.sem_inc(S_ready, 1)
            pe.sem_inc(o_copied, 1)
            with pe.Fori(0, B) as b:
                pe.wait_ge(xb_ready, b + 1)

                def turn_tile(m):
                    pe.wait_ge(act_ready, b * NM + (m + 1))
                    if m >= 2:
                        pe.wait_ge(tr_copied, b * NM + (m - 1))
                    for t in range(TB):
                        last = nc.tensor.transpose(trps[m % 2][:, t, :], act_ct[:, m % 2, t * P:(t + 1) * P], c.ident[:])
                    last.then_inc(tr_ready, 1)

                for m in range(NM):
                    if m >= 2:
                        pe.wait_ge(conv_ready, b * NM + (m - 1))
                    for k in range(DC):
                        last = nc.tensor.matmul(proj[m % 2], wqkv[:, k, m * P:(m + 1) * P], xb[:, k, :],
                                                start=(k == 0), stop=(k == DC - 1))
                    last.then_inc(proj_ready, 1)
                    if m >= 2:
                        turn_tile(m - 2)
                turn_tile(NM - 2)
                turn_tile(NM - 1)
                for t in range(TB):
                    for k in range(DC):
                        last = nc.tensor.matmul(ba_ps[:, t, :], xb[:, k, t * P:(t + 1) * P], wba[:, k, :],
                                                start=(k == 0), stop=(k == DC - 1))
                last.then_inc(ba_ready, 1)
                for n in range(TB * NZ):
                    t, half = n // NZ, n % NZ
                    if n >= 2:
                        pe.wait_ge(z_copied, b * (TB * NZ) + (n - 1))
                    for k in range(DC):
                        last = nc.tensor.matmul(zps[n % 2], xb[:, k, t * P:(t + 1) * P],
                                                wz[:, k, half * 512:(half + 1) * 512],
                                                start=(k == 0), stop=(k == DC - 1))
                    last.then_inc(z_ready, 1)
                pe.wait_ge(g_ready, b + 1)
                nc.tensor.matmul(G_ps, upto[:], g[:], start=True, stop=True)
                nc.tensor.matmul(end_ps, c.ones[:], g[:], start=True, stop=True).then_inc(Gsum_ready, 1)
                stage_end(pe, b, 0)
                with pe.Fori(0, HG) as hg:
                    turn = b * HG + hg
                    for ch in range(TB):
                        k = ch % 2
                        at = turn * TB + (ch + 1)
                        pe.wait_ge(prep_ready, at)
                        two = lambda w: w.rearrange("p h d -> p (h d)")
                        for n, w in enumerate((Kn[:, k], Qn[:, k], Kb[:, k, 0:2], Kb[:, k, 2:4], Qe[:, k, 0:2],
                                               Qe[:, k, 2:4])):
                            last = nc.tensor.transpose(tps[:, n, :], two(w), c.ident[:])
                        last.then_inc(turned, 1)
                        pe.wait_ge(S_ready, at)
                        nc.tensor.matmul(gps[:], c.ones[:], Ug[:, k], start=True, stop=True).then_inc(grow_ready, 1)
                        pe.wait_ge(kqT_ready, at)
                        pe.wait_ge(o_copied, at)
                        low, high = slice(0, DK), slice(DK, 2 * DK)
                        nc.tensor.matmul(kps[:, 0], kqT[low, 0, :], kqT[low, 0:2, :], start=True,
                                         stop=True).then_inc(kk_low, 1)
                        pe.wait_ge(kk_low, at)
                        nc.tensor.matmul(kps[:, 1], kqT[high, 0, :], kqT[high, 0:2, :], start=True,
                                         stop=True).then_inc(kk_ready, 1)
                        pe.wait_ge(M_ready, at)
                        for h in range(4):
                            last = nc.tensor.transpose(m0_ps[:, h // 2, h % 2, :], M[:, h, 0, :], c.ident[:])
                        last.then_inc(m0_ready, 1)
                        pe.wait_ge(X0_ready, at)
                        for lv in range(1, LEVELS):
                            step = ch * 12 + (lv - 1) * 2
                            for half in range(2):
                                if lv > 1:
                                    pe.wait_ge(X_ready, turn * (TB * 12) + (step - 2 + half + 1))
                                for e in range(2):
                                    h = 2 * half + e
                                    last = nc.tensor.matmul(yps[half][:, e, :], M[:, h, lv, :], XX[:, half, 0, e, :],
                                                            start=True, stop=True)
                                last.then_inc(y_ready, 1)
                            for half in range(2):
                                pe.wait_ge(y_copied, turn * (TB * 12) + (step + half + 1))
                                for e in range(2):
                                    h = 2 * half + e
                                    last = nc.tensor.matmul(wps[half][:, 0, e, :], XX[:, half, 1, e, :], Y[:, h, :],
                                                            start=True, stop=True)
                                    if lv < LEVELS - 1:
                                        last = nc.tensor.matmul(wps[half][:, 1, e, :], Y[:, h, :], XX[:, half, 1, e, :],
                                                                start=True, stop=True)
                                last.then_inc(w_ready, 1)
                        for e in range(2):
                            last = nc.tensor.matmul(r_ps[:, e, :], kqT[:, 2 + e, :], S[:, e, :], start=True, stop=True)
                        last.then_inc(r_ready, 1)
                        pe.wait_ge(Tm_ready, at)
                        pe.wait_ge(B_ready, at)
                        for h in range(4):
                            last = nc.tensor.matmul(u_ps[:, h, :], Tm[:, h // 2, h % 2, :], Bm[:, h, :],
                                                    start=True, stop=True)
                        last.then_inc(u_ready, 1)
                        pe.wait_ge(U_ready, at)
                        pe.wait_ge(PT_ready, at)
                        for e in range(2):
                            nc.tensor.matmul(o_ps[:, e * P:(e + 1) * P], kqT[:, 4 + e, :], S[:, e, :], start=True,
                                             stop=False, skip_group_check=True)
                            for h in (2 * e, 2 * e + 1):
                                last = nc.tensor.matmul(o_ps[:, h * DK:(h + 1) * DK], PT[:, h, :], U[:, h, :], start=False,
                                                        stop=True, skip_group_check=True)
                        last.then_inc(o_ready, 1)
                        for e in range(2):
                            last = nc.tensor.matmul(s_ps[:, e, :], Kd[:, k, 2 * e:2 * e + 2], U[:, 2 * e:2 * e + 2],
                                                    start=True, stop=True)
                        last.then_inc(s_ready, 1)
                stage_end(pe, b, 1)
                pe.wait_ge(on_ready, b + 1)
                for m in range(HV * DK // P):
                    if m >= 2:
                        pe.wait_ge(oT_copied, b * (HV * DK // P) + (m - 1))
                    for t in range(TB):
                        last = nc.tensor.transpose(proj[m % 2][:, t * P:(t + 1) * P], o[:, t, m * P:(m + 1) * P], c.ident[:])
                    last.then_inc(oT_ready, 1)
                pe.wait_ge(oT_copied, b * (HV * DK // P) + HV * DK // P)
                for t in range(TB):
                    if t >= 2:
                        pe.wait_ge(added, b * TB + (t - 1))
                    for m in range(HV * DK // P):
                        last = nc.tensor.matmul(zps[t % 2][:, 0:D], oT[:, m, t * P:(t + 1) * P], wout[:, m, :],
                                                start=(m == 0), stop=(m == HV * DK // P - 1))
                    last.then_inc(out_ready, 1)
                stage_end(pe, b, 2)


HPG = 4
SP = 4 * SW
KW = 64


def lay_attention(name, a, rows, wq, bq, wk, bk, wv, bv, wo, bo, heads):
    d = wv.shape[1] // heads

    def twice(w):
        w = w.reshape(*w.shape[:-1], -1, KW)
        return np.concatenate([w, w], -1)

    n = wq.shape[1] // KW
    stacks = lambda w: rows(twice(w).reshape(D, n * P)).reshape(P, DC, n, P).transpose(2, 0, 1, 3)
    p = np.arange(P)[:, None]
    return {
        f"{name}_wqk": np.stack([stacks(wq), stacks(wk)], 2),
        f"{name}_bqk": np.stack([twice(bq).T, twice(bk).T], 1),
        f"{name}_member": (p % KW // d == np.arange(HPG)).astype(np.float32),
        f"{name}_wv": rows(wv),
        f"{name}_bv": bv,
        f"{name}_wo": np.concatenate([wo.reshape(heads, d, D).transpose(1, 0, 2)] * 2, 0),
        f"{name}_bo": bo,
    }


def lay_masked_attention(a, rows, cols):
    g = lambda n: a["L0_xattn_" + n]
    o = lay_attention("xa0", a, rows, g("Wq"), g("bq"), g("Wk"), g("bk"), g("Wv"), g("bv"), g("Wo"), g("bo"), 16)
    bytes_ = np.pad(a["mask_BxSxS2_bk1"].view(np.uint8).reshape(B, TB, P, S2), [(0, 0)] * 3 + [(0, SP - S2)],
                    constant_values=1)
    o["mask"] = bytes_.view(np.int32)
    return o


def lay_full_attention(a, rows, cols):
    g = lambda n: a["L1_xattn_" + n]
    return lay_attention("xa1", a, rows, g("W_q").T, g("b_q"), g("W_k").T, g("b_k"), g("W_v").T, g("b_v"),
                         g("W_o").T, g("b_o"), 16)


def masked_attention(nc, c):
    attention(nc, c, "xa0", heads=16, dk=64, masked=True)


def full_attention(nc, c):
    attention(nc, c, "xa1", heads=16, dk=16, masked=False)


def attention(nc, c, name, heads, dk, masked):
    layernorm(nc, c, f"{name}_ln", c.x, c.xnT)
    wide_heads = dk == KW
    NG = heads // HPG
    VW = 256
    MV = 2 * dk
    UN = HPG * TB
    PAIRS = UN // 2
    SCALE = float(dk) ** -0.5
    KC = [(n * 512, min(512, S2 - n * 512)) for n in range(-(-S2 // 512))]
    SWW = SW + SW % 2
    WIDE = 3 * SW + SWW
    G4 = [(g, min(g + 4, KT)) for g in range(0, KT, 4)]
    GN = len(G4)
    NPT = 1 if wide_heads else 2
    NP = 1 + len(KC)
    with Scope(nc, name) as s:
        wv = s.sb("wv", [P, DC, heads * dk])
        wo = s.sb("wo", [MV, heads, D])
        bqk = s.sb("bqk", [P, 2, heads * dk // KW])
        bv = s.sb("bv", [P, heads * dk])
        bo = s.sb("bo", [P, D])
        ctxT = s.sb("ctxT", [P, DC, S2])
        wqk = s.sb("wqk", [P, 2, DC, P])
        Vf = s.sb("Vf", [P, KT, VW])
        V = s.sb("V", [P, KT, HPG, 2, dk], F32R)
        Q = s.sb("Q", [P, 2, 2, T], F32R)
        K = s.sb("K", [P, 2 if wide_heads else 1, WIDE], F32R)
        prob = s.sb("prob", [P, 2, SP])
        PT = s.sb("PT", [P, NPT, 2, KT, 2, P], F32R)
        mx = s.sb("mx", [P, 2])
        neg = s.sb("neg", [P, 2])
        total = s.sb("total", [P, 2])
        rtotal = s.sb("rtotal", [P, 2])
        diag = s.sb("diag", [P, 2, 2, P])
        share = s.sb("share", [MV, 2 * P])
        attT = s.sb("attT", [MV, HPG, T])
        if masked:
            mask8 = s.sb("mask8", [P, TB, SW], I32)
        mask = s.sb("mask", [P, TB if masked else 1, SP], BF16)
        if not wide_heads:
            member = s.sb("member", [P, HPG])
            qf = s.sb("qf", [P, T])
        sps = s.ps("sps", [P, 4, 512])
        tps = [s.ps(f"tps{k}", [P, 4, P]) for k in range(2)]
        pv = s.ps("pv", [P, 512])
        proj = s.ps("proj", [P, 512])
        flat = [t[:].rearrange("p a b -> p (a b)") for t in tps]
        proj_banks = [proj[:]] if wide_heads else [proj[:], *flat]

        loaded = s.sem("loaded")
        pad_ready = s.sem("pad_ready")
        ctx_loaded = s.sem("ctx_loaded")
        mask_loaded = s.sem("mask_loaded")
        mask_ready = s.sem("mask_ready")
        w_loaded = s.sem("w_loaded")
        v_ready = s.sem("v_ready")
        v_copied = s.sem("v_copied")
        v_hi = s.sem("v_hi")
        v_lo = s.sem("v_lo")
        proj_ready = s.sem("proj_ready")
        proj_hi = s.sem("proj_hi")
        proj_lo = s.sem("proj_lo")
        q_hi = s.sem("q_hi")
        q_lo = s.sem("q_lo")
        s_ready = s.sem("s_ready")
        max_ready = s.sem("max_ready")
        neg_ready = s.sem("neg_ready")
        p_ready = s.sem("p_ready")
        t_ready = s.sem("t_ready")
        t_hi = s.sem("t_hi")
        t_lo = s.sem("t_lo")
        inv_ready = s.sem("inv_ready")
        diag_ready = s.sem("diag_ready")
        pv_ready = s.sem("pv_ready")
        share_ready = s.sem("share_ready")
        att_ready = s.sem("att_ready")
        out_ready = s.sem("out_ready")
        added = s.sem("added")
        based = s.sem("based")
        passed = s.sem("passed")
        block = s.block()
        LOADS = (5 if wide_heads else 6) * 16
        OUTS = 2 * HPG if wide_heads else 2
        PADS = 2 if masked else 4
        START = 1
        FREE = 1
        VN = NG if wide_heads else 1
        SN = NG * HPG if wide_heads else NG

        def seen(eng):
            eng.sem_inc(passed, 1)

        def keys(kt):
            return P if kt < KT - 1 else LAST

        def chunk(n):
            return (0, T) if n == 0 else KC[n - 1]

        NEXT = {(0, "B"): 0, (1, "A"): 1, (1, "B"): 2, (2, "B"): 3, (2, "C"): 4} if wide_heads else {}
        OUT = {(3, "A"): 0, (3, "B"): 1} if wide_heads else {}

        @block.sync
        def _(sp):
            for dst, src in ((bqk, "bqk"), (wv, "wv"), (wo, "wo")) + (() if wide_heads else ((member, "member"),)):
                sp.dma_start(dst[:], c.dram[f"{name}_{src}"]).then_inc(loaded, 16)
            for dst, src in ((bv, "bv"), (bo, "bo")):
                sp.dma_start(dst[:], c.dram[f"{name}_{src}"].partition_broadcast(P)).then_inc(loaded, 16)
            with sp.Fori(0, B) as b:
                sp.wait_ge(proj_ready, b * (SN * NP) + FREE)
                sp.dma_start(ctxT[:], c.dram["ctxT"][ds(b, 1)].rearrange("a p c s -> (a p) c s")).then_inc(ctx_loaded, 16)
                if masked:
                    sp.wait_ge(mask_ready, b + FREE)
                    sp.dma_start(mask8[:], c.dram["mask"][ds(b, 1)].rearrange("a t p s -> (a p) t s")).then_inc(mask_loaded, 16)
                with sp.Fori(0, SN) as h:
                    sp.wait_ge(proj_ready, (b * SN + h) * NP + FREE)
                    sp.dma_start(wqk[:], c.dram[f"{name}_wqk"][ds(h, 1)].rearrange("a p e c m -> (a p) e c m")
                                 ).then_inc(w_loaded, 16)

        @block.scalar
        def _(act):
            act.wait_ge(loaded, LOADS)
            with act.Fori(0, B) as b:
                with act.Fori(0, NG) as gr:
                    group = b * NG + gr

                    def high(hh, n):
                        stack, col = (group * HPG + hh, gr * HPG + hh) if wide_heads else (group, gr)
                        act.wait_ge(proj_ready, stack * NP + (n + 1 + FREE))
                        seen(act)
                        k0, w = chunk(n)
                        bank = proj_banks[n % len(proj_banks)]
                        dst = K[:, hh % 2, k0:k0 + w] if n else Q[:, hh % 2, 0, :] if wide_heads else qf[:]
                        nc.scalar.activation(dst, bank[:, 0:w], ACT.Identity, bias=bqk[:, min(n, 1), ds(col, 1)]
                                             ).then_inc(proj_hi, 1)

                    def head_rows(hh):
                        nc.scalar.activation(Q[:, hh % 2, 0, :], qf[:], ACT.Copy, scale=member[:, hh:hh + 1]).then_inc(q_hi, 1)

                    def exps(u):
                        e = u % 2
                        act.wait_ge(neg_ready, group * UN + (u + 1))
                        nc.scalar.activation(prob[:, e, :], prob[:, e, :], ACT.Exp, bias=neg[:, e:e + 1], scale=SCALE,
                                             accum_out=total[:, e:e + 1]).then_inc(p_ready, 1)

                    def turned_high(u, g):
                        k0, k1 = G4[g]
                        act.wait_ge(t_ready, (group * UN + u) * GN + (g + 1))
                        if u >= 2 * NPT and u % 2 == 0 and g == 0:
                            act.wait_ge(pv_ready, group * PAIRS + (u // 2 + 1 - NPT))
                        n = keys(k1 - 1) if k1 - k0 == 1 else P
                        nc.scalar.activation(PT[0:n, u // 2 % NPT, 0, k0:k1, u % 2, :], tps[g % 2][0:n, 0:k1 - k0, :], ACT.Copy
                                             ).then_inc(t_hi, 1)

                    def spread_share(pair):
                        act.wait_ge(pv_ready, group * PAIRS + (pair + 1))
                        nc.scalar.activation(share[:], pv[0:MV, 2 * P:4 * P], ACT.Copy).then_inc(share_ready, 1)

                    for n in range(NP):
                        high(0, n)
                    if not wide_heads:
                        act.wait_ge(proj_hi, group * NP + 1)
                        head_rows(0)
                    act.wait_ge(v_copied, (group if wide_heads else b) * KT + KT)
                    cols = slice(0, VW) if wide_heads else ds(gr * (HPG * dk), HPG * dk)
                    seen(act)
                    nc.scalar.activation(V[:, :, :, 0, :], Vf[:, :, cols].rearrange("p k (h d) -> p k h d", d=dk), ACT.Copy
                                         ).then_inc(v_hi, 1)
                    exps(0)
                    for u in range(UN):
                        hh, q = divmod(u, TB)
                        def beside(place):
                            if hh + 1 < HPG and (q, place) in NEXT:
                                high(hh + 1, NEXT[q, place])

                        behind = u % 2 == 0 and u >= 2 * NPT
                        if behind and not wide_heads:
                            spread_share(u // 2 - 2)
                        if wide_heads and behind:
                            exps(u + 1)
                        beside("A")
                        turned_high(u, 0)
                        turned_high(u, 1)
                        if u + 1 < UN and not (wide_heads and behind):
                            exps(u + 1)
                        beside("B")
                        turned_high(u, 2)
                        turned_high(u, 3)
                        beside("C")
                        if behind and wide_heads:
                            spread_share(u // 2 - 1)
                        if not wide_heads and hh + 1 < HPG and q == 0:
                            head_rows(hh + 1)
                    for pair in range(PAIRS - NPT, PAIRS):
                        spread_share(pair)

        @block.vector
        def _(dve):
            nc.vector.memset(K[:].bitcast(F32), 0.0).then_inc(pad_ready, 1)
            nc.vector.memset(Vf[:, KT - 1, :], 0.0).then_inc(pad_ready, 1)
            if not masked:
                nc.vector.memset(mask[:], 0.0).then_inc(pad_ready, 1)
                dve.wait_ge(pad_ready, 3)
                nc.vector.memset(mask[:, 0, S2:], NEG).then_inc(pad_ready, 1)
            dve.wait_ge(pad_ready, PADS)
            dve.wait_ge(loaded, LOADS)
            with dve.Fori(0, B) as b:
                xb = c.x[:, ds(b * TB, TB), :]
                nc.vector.tensor_tensor(xb, xb, bo[:].unsqueeze(1).broadcast_to([P, TB, D]), ALU.add).then_inc(based, 1)
                dve.wait_ge(based, b + 1)
                seen(dve)
                if masked:
                    dve.wait_ge(mask_loaded, b * 16 + 16)
                    nc.vector.tensor_scalar(mask[:], mask8[:].bitcast(U8), NEG, None, ALU.mult
                                            ).then_inc(mask_ready, 1)
                    dve.wait_ge(mask_ready, b + (1 + FREE))
                    seen(dve)

                def copy_values(kt, turn, col):
                    n = keys(kt)
                    dve.wait_ge(v_ready, turn * KT + (kt + 1))
                    nc.vector.tensor_tensor(Vf[0:n, kt, :], flat[kt % 2][0:n, 0:VW], bv[0:n, ds(col, VW)], ALU.add
                                            ).then_inc(v_copied, 1)

                if not wide_heads:
                    for kt in range(KT):
                        copy_values(kt, b, 0)
                with dve.Fori(0, NG) as gr:
                    group = b * NG + gr

                    def low(hh, n):
                        stack, col = (group * HPG + hh, gr * HPG + hh) if wide_heads else (group, gr)
                        k0, w = chunk(n)
                        bank = proj_banks[n % len(proj_banks)]
                        dve.wait_ge(proj_hi, stack * NP + (n + 1))
                        if n == 0 and not wide_heads:
                            seen(dve)
                            dve.sem_inc(proj_lo, 1)
                            return
                        if n == 0:
                            rows, hi, lo = slice(0, P), Q[:, hh % 2, 0, :], Q[:, hh % 2, 1, :]
                        else:
                            rows = slice(P // 2, P)
                            hi = lo = K[rows, hh % 2, k0:k0 + w]
                        nc.vector.scalar_tensor_tensor(out=lo, in0=bank[rows, 0:w], scalar=bqk[rows, min(n, 1), ds(col, 1)],
                                                       in1=hi.bitcast(F32), op0=ALU.add, op1=ALU.subtract
                                                       ).then_inc(proj_lo, 1)

                    def head_rows(hh):
                        dve.wait_ge(q_hi, group * HPG + (hh + 1))
                        nc.vector.scalar_tensor_tensor(out=Q[:, hh % 2, 1, :], in0=qf[:], scalar=member[:, hh:hh + 1],
                                                       in1=Q[:, hh % 2, 0, :].bitcast(F32), op0=ALU.mult, op1=ALU.subtract
                                                       ).then_inc(q_lo, 1)

                    def row_max(u):
                        e = u % 2
                        dve.wait_ge(s_ready, group * UN + (u + 1))
                        seen(dve)
                        parts = lambda v: v.rearrange("p (n k) -> p n k", k=SW)
                        nc.vector.tensor_tensor_reduce(parts(prob[:, e, :]), sps[:, :, 0:SW], parts(mask[:, u % TB if masked else 0, :]),
                                                       1.0, -3.0e38, ALU.add, ALU.max, mx[:, e:e + 1]).then_inc(max_ready, 1)
                        dve.wait_ge(max_ready, group * UN + (u + 1))
                        nc.vector.tensor_scalar(neg[:, e:e + 1], mx[:, e:e + 1], -SCALE, None, ALU.mult).then_inc(neg_ready, 1)

                    def turned_low(u, g):
                        k0, k1 = G4[g]
                        dve.wait_ge(t_hi, (group * UN + u) * GN + (g + 1))
                        n = keys(k1 - 1) if k1 - k0 == 1 else P
                        nc.vector.tensor_tensor(PT[0:n, u // 2 % NPT, 1, k0:k1, u % 2, :], tps[g % 2][0:n, 0:k1 - k0, :],
                                                PT[0:n, u // 2 % NPT, 0, k0:k1, u % 2, :].bitcast(F32), ALU.subtract).then_inc(t_lo, 1)

                    def shares(u):
                        e = u % 2
                        dve.wait_ge(p_ready, group * UN + (u + 1))
                        nc.vector.reciprocal(rtotal[:, e:e + 1], total[:, e:e + 1]).then_inc(inv_ready, 1)
                        dve.wait_ge(inv_ready, group * UN + (u + 1))
                        nc.vector.tensor_scalar(diag[:, u // 2 % 2, e, :], c.ident[:], rtotal[:, e:e + 1], None, ALU.mult
                                                ).then_inc(diag_ready, 1)

                    def scale_output(pair):
                        hh, half = divmod(pair, 2)
                        dve.wait_ge(share_ready, group * PAIRS + (pair + 1))
                        nc.vector.tensor_tensor(attT[:, hh, half * 2 * P:(half + 1) * 2 * P], pv[0:MV, 0:2 * P], share[:],
                                                ALU.mult).then_inc(att_ready, 1)

                    def add_output(turn, half):
                        rows = c.x[:, ds(b * TB + half * (TB // 2), TB // 2), :]
                        dve.wait_ge(out_ready, turn + 1)
                        nc.vector.tensor_tensor(rows, rows, proj[:].rearrange("p (t d) -> p t d", d=D), ALU.add
                                                ).then_inc(added, 1)

                    if wide_heads:
                        done = 0
                        for n in range(NP):
                            low(0, n)
                            upto = KT * (n + 1) // NP
                            for kt in range(done, upto):
                                copy_values(kt, group, gr * VW)
                            done = upto
                    else:
                        for n in range(NP):
                            low(0, n)
                        head_rows(0)
                    row_max(0)
                    dve.wait_ge(v_hi, group + 1)
                    cols = slice(0, VW) if wide_heads else ds(gr * (HPG * dk), HPG * dk)
                    nc.vector.tensor_tensor(V[:, :, :, 1, :], Vf[:, :, cols].rearrange("p k (h d) -> p k h d", d=dk),
                                            V[:, :, :, 0, :].bitcast(F32), ALU.subtract).then_inc(v_lo, 1)
                    for u in range(UN):
                        hh, q = divmod(u, TB)
                        def beside(place):
                            if hh + 1 < HPG and (q, place) in NEXT:
                                low(hh + 1, NEXT[q, place])
                            if hh >= 1 and (q, place) in OUT:
                                add_output(group * OUTS + (hh - 1) * 2 + OUT[q, place], OUT[q, place])

                        behind = u % 2 == 0 and u >= 2 * NPT
                        if behind and not wide_heads:
                            scale_output(u // 2 - 2)
                        if u + 1 < UN:
                            row_max(u + 1)
                        shares(u)
                        beside("A")
                        turned_low(u, 0)
                        turned_low(u, 1)
                        beside("B")
                        turned_low(u, 2)
                        turned_low(u, 3)
                        beside("C")
                        if behind and wide_heads:
                            scale_output(u // 2 - 1)
                        if not wide_heads and hh + 1 < HPG and q == 0:
                            head_rows(hh + 1)
                    for pair in range(PAIRS - NPT, PAIRS):
                        scale_output(pair)
                    for half in range(2):
                        add_output(group * OUTS + OUTS - 2 + half, half)

        @block.tensor
        def _(pe):
            for sem in (proj_ready, mask_ready):
                pe.sem_inc(sem, FREE)
            pe.sem_inc(added, START)
            pe.wait_ge(loaded, LOADS)
            pe.wait_ge(pad_ready, PADS)

            with pe.Fori(0, B) as b:
                pe.wait_ge(ctx_loaded, b * 16 + 16)
                seen(pe)

                def values(kt, turn, col):
                    if kt >= 2:
                        pe.wait_ge(v_copied, turn * KT + (kt - 1))
                    n = keys(kt)
                    for k in range(DC):
                        last = nc.tensor.matmul(flat[kt % 2][0:n, 0:VW], ctxT[:, k, kt * P:kt * P + n],
                                                wv[:, k, ds(col, VW)], start=(k == 0), stop=(k == DC - 1))
                    last.then_inc(v_ready, 1)

                if not wide_heads:
                    for kt in range(KT):
                        values(kt, b, 0)
                    pe.wait_ge(v_copied, b * KT + KT)
                    seen(pe)
                with pe.Fori(0, NG) as gr:
                    group = b * NG + gr

                    def project(hh, n):
                        stack = group * HPG + hh if wide_heads else group
                        if n == 0:
                            pe.wait_ge(w_loaded, stack * 16 + 16)
                            if hh >= 3:
                                pe.wait_ge(added, group * OUTS + (hh - 2) * 2 + START)
                        elif n >= len(proj_banks):
                            pe.wait_ge(proj_lo, stack * NP + (n + 1 - len(proj_banks)))
                        seen(pe)
                        k0, w = chunk(n)
                        for k in range(DC):
                            rhs = c.xnT[:, k, ds(b * T, T)] if n == 0 else ctxT[:, k, k0:k0 + w]
                            last = nc.tensor.matmul(proj_banks[n % len(proj_banks)][:, 0:w], wqk[:, min(n, 1), k, :], rhs,
                                                    start=(k == 0), stop=(k == DC - 1))
                        last.then_inc(proj_ready, 1)

                    def scores(u):
                        hh, q = divmod(u, TB)
                        kb = hh % 2 if wide_heads else 0
                        if q == 0:
                            stack = group * HPG + hh if wide_heads else group
                            if wide_heads or hh == 0:
                                pe.wait_ge(proj_lo, stack * NP + NP)
                            if not wide_heads:
                                pe.wait_ge(q_lo, group * HPG + (hh + 1))
                        if u >= 1:
                            pe.wait_ge(max_ready, group * UN + u)
                        for n in range(4):
                            for e in range(2):
                                last = nc.tensor.matmul(sps[:, n, 0:SWW], Q[:, hh % 2, e, q * P:(q + 1) * P],
                                                        K[:, kb, n * SW:n * SW + SWW], start=(e == 0), stop=(e == 1))
                        last.then_inc(s_ready, 1)

                    def turn(u, g):
                        k0, k1 = G4[g]
                        if g == 0:
                            pe.wait_ge(p_ready, group * UN + (u + 1))
                        if u >= 1 or g >= 2:
                            pe.wait_ge(t_lo, (group * UN + u) * GN + (g - 1))
                        for kt in range(k0, k1):
                            n = keys(kt)
                            last = nc.tensor.transpose(tps[g % 2][0:n, kt - k0, :], prob[:, u % 2, kt * P:kt * P + n], c.ident[:])
                        last.then_inc(t_ready, 1)

                    def output(pair, kts):
                        hh = pair // 2
                        if kts[0] == 0:
                            pe.wait_ge(t_lo, (group * UN + 2 * pair + 2) * GN)
                            pe.wait_ge(diag_ready, group * UN + (2 * pair + 2))
                            if pair == 0:
                                pe.wait_ge(v_lo, group + 1)
                            else:
                                pe.wait_ge(att_ready, group * PAIRS + pair)
                        for kt in kts:
                            n = keys(kt)
                            for part in range(2):
                                nc.tensor.matmul(pv[0:MV, 0:2 * P], V[0:n, kt, hh].rearrange("p e d -> p (e d)"),
                                                 PT[0:n, pair % NPT, part, kt].rearrange("p a q -> p (a q)"),
                                                 start=(kt == 0 and part == 0), stop=(kt == KT - 1 and part == 1))
                        if kts[-1] == KT - 1:
                            nc.tensor.matmul(pv[0:MV, 2 * P:4 * P], c.ones[:, 0:MV],
                                             diag[:, pair % 2].rearrange("p a q -> p (a q)"),
                                             start=True, stop=True).then_inc(pv_ready, 1)

                    def out_product(turn, half, members):
                        pe.wait_ge(added, turn + START)
                        pe.wait_ge(att_ready, group * PAIRS + 2 * members[-1] + 2)
                        seen(pe)
                        for t in range(TB // 2):
                            at = half * (TB // 2) + t
                            for hh in members:
                                last = nc.tensor.matmul(proj[:, t * D:(t + 1) * D], attT[:, hh, at * P:(at + 1) * P],
                                                        wo[:, ds(gr * HPG + hh, 1), :].rearrange("p a d -> p (a d)"),
                                                        start=(hh == members[0]), stop=(hh == members[-1]))
                        last.then_inc(out_ready, 1)

                    done = 0
                    for n in range(NP):
                        project(0, n)
                        if wide_heads:
                            upto = KT * (n + 1) // NP
                            for kt in range(done, upto):
                                values(kt, group, gr * VW)
                            done = upto
                    if wide_heads:
                        pe.wait_ge(v_copied, group * KT + KT)
                    scores(0)
                    for u in range(UN):
                        hh, q = divmod(u, TB)
                        def beside(place):
                            if wide_heads and place == "A" and q % 2 == 0 and u >= 2:
                                output(u // 2 - 1, range(KT))
                            if not wide_heads and place != "C" and u >= 2:
                                n = u % 2 * 2 + (place == "B")
                                output(u // 2 - 1, range(KT * n // 4, KT * (n + 1) // 4))
                            if hh + 1 < HPG and (q, place) in NEXT:
                                project(hh + 1, NEXT[q, place])
                            if hh >= 1 and (q, place) in OUT:
                                out_product(group * OUTS + (hh - 1) * 2 + OUT[q, place], OUT[q, place], [hh - 1])

                        if u + 1 < UN:
                            scores(u + 1)
                        beside("A")
                        turn(u, 0)
                        turn(u, 1)
                        beside("B")
                        turn(u, 2)
                        turn(u, 3)
                        beside("C")
                    output(PAIRS - 1, range(KT))
                    for half in range(2):
                        out_product(group * OUTS + OUTS - 2 + half, half, [HPG - 1] if wide_heads else list(range(HPG)))
                    pe.wait_ge(added, group * OUTS + OUTS + START)
                    seen(pe)


DH = 1024
MH = DH // P


def lay_ternary_mlp(a, rows, cols):
    g = lambda n: a["L0_ffn_" + n]
    o = {f"ffn_{n}": rows(g(n + "_w").T) for n in ("w1", "w2", "h1", "h2", "w3")}
    o.update({f"ffn_{n}_s": cols(g(n + "_s")) for n in ("w1", "w2", "h1", "h2")})
    o["ffn_w3_s"] = g("w3_s")
    return o


def ternary_mlp(nc, c):
    layernorm(nc, c, "ffn_ln", c.x, c.xnT)
    NB = B * T // 512
    NT4 = 512 // P
    with Scope(nc, "ffn") as s:
        names = ("w1", "w2", "h1", "h2", "w3")
        w = {n: s.sb(n, list(c.dram[f"ffn_{n}"].shape)) for n in names}
        sc = {n: s.sb(n + "_s", [P, MH]) for n in names[:4]}
        w3_s = s.sb("w3_s", [P, D])
        gate = s.sb("gate", [P, 2, 512])
        hid = [s.sb(f"hid{k}", [P, MH, 512]) for k in range(3)]
        scaled = s.sb("scaled", [P, 2, D])
        up = [s.ps(f"up{k}", [P, 512]) for k in range(2)]
        lin = [s.ps(f"lin{k}", [P, 512]) for k in range(2)]
        mid = [s.ps(f"mid{k}", [P, 512]) for k in range(2)]
        low = [s.ps(f"low{k}", [P, 512]) for k in range(2)]
        loaded = {n: s.sem(n + "_loaded") for n in names}
        scales = s.sem("scales")
        up_ready = s.sem("up_ready")
        gate_ready = s.sem("gate_ready")
        hid_ready = s.sem("hid_ready")
        mid_ready = [s.sem(f"mid_ready{k}") for k in range(2)]
        act_ready = [s.sem(f"act_ready{k}") for k in range(2)]
        out_ready = s.sem("out_ready")
        scaled_ready = s.sem("scaled_ready")
        added = s.sem("added")
        block = s.block()
        SCALES = 5 * 16

        @block.sync
        def _(sp):
            for n in ("w1", "w2", "h1", "h2"):
                sp.dma_start(sc[n][:], c.dram[f"ffn_{n}_s"]).then_inc(scales, 16)
            sp.dma_start(w3_s[:], c.dram["ffn_w3_s"].partition_broadcast(P)).then_inc(scales, 16)
            for n in names:
                sp.dma_start(w[n][:], c.dram[f"ffn_{n}"]).then_inc(loaded[n], 16)

        @block.scalar
        def _(act):
            act.wait_ge(scales, SCALES)
            with act.Fori(0, NB) as i:
                for m in range(MH):
                    act.wait_ge(up_ready, i * MH + (m + 1))
                    if m >= 2:
                        act.wait_ge(hid_ready, i * MH + (m - 1))
                    nc.scalar.activation(gate[:, m % 2, :], up[m % 2][:], ACT.Silu, scale=sc["w1"][:, m:m + 1]
                                         ).then_inc(gate_ready, 1)
                for k, n in enumerate(("h1", "h2")):
                    for m in range(MH):
                        act.wait_ge(mid_ready[k], i * MH + (m + 1))
                        nc.scalar.activation(hid[1 + k][:, m, :], mid[m % 2][:], ACT.Gelu, scale=sc[n][:, m:m + 1]
                                             ).then_inc(act_ready[k], 1)

        @block.vector
        def _(dve):
            dve.wait_ge(scales, SCALES)
            with dve.Fori(0, NB) as i:
                for m in range(MH):
                    dve.wait_ge(gate_ready, i * MH + (m + 1))
                    nc.vector.scalar_tensor_tensor(out=hid[0][:, m, :], in0=lin[m % 2][:], scalar=sc["w2"][:, m:m + 1],
                                                   in1=gate[:, m % 2, :], op0=ALU.mult, op1=ALU.mult
                                                   ).then_inc(hid_ready, 1)
                for t in range(NT4):
                    row = c.x[:, ds(i * NT4 + t, 1), :].rearrange("p a d -> p (a d)")
                    dve.wait_ge(out_ready, i * NT4 + (t + 1))
                    nc.vector.tensor_tensor(scaled[:, t % 2, :], low[t % 2][:, 0:D], w3_s[:], ALU.mult
                                            ).then_inc(scaled_ready, 1)
                    dve.wait_ge(scaled_ready, i * NT4 + (t + 1))
                    nc.vector.tensor_tensor(row, row, scaled[:, t % 2, :], ALU.add).then_inc(added, 1)

        @block.tensor
        def _(pe):
            for n in names:
                pe.wait_ge(loaded[n], 16)
            with pe.Fori(0, NB) as i:
                for m in range(MH):
                    if m >= 2:
                        pe.wait_ge(hid_ready, i * MH + (m - 1))
                    for dst, n in ((lin, "w2"), (up, "w1")):
                        for k in range(DC):
                            last = nc.tensor.matmul(dst[m % 2][:], w[n][:, k, m * P:(m + 1) * P], c.xnT[:, k, ds(i * 512, 512)],
                                                    start=(k == 0), stop=(k == DC - 1))
                    last.then_inc(up_ready, 1)
                for e, n in enumerate(("h1", "h2")):
                    pe.wait_ge(hid_ready if e == 0 else act_ready[0], i * MH + MH)
                    for m in range(MH):
                        if e == 1 and m < 2:
                            pass
                        elif m >= 2:
                            pe.wait_ge(act_ready[e], i * MH + (m - 1))
                        for k in range(MH):
                            last = nc.tensor.matmul(mid[m % 2][:], w[n][:, k, m * P:(m + 1) * P], hid[e][:, k, :],
                                                    start=(k == 0), stop=(k == MH - 1))
                        last.then_inc(mid_ready[e], 1)
                pe.wait_ge(act_ready[1], i * MH + MH)
                for t in range(NT4):
                    if t >= 2:
                        pe.wait_ge(added, i * NT4 + (t - 1))
                    for k in range(MH):
                        last = nc.tensor.matmul(low[t % 2][:, 0:D], hid[2][:, k, t * P:(t + 1) * P], w["w3"][:, k, :],
                                                start=(k == 0), stop=(k == MH - 1))
                    last.then_inc(out_ready, 1)


CH = 2 * D
CC = CH // P
NS, RANK = 16, D // 16
DBC = RANK + 2 * NS
LOW = 64
SOL = 0.1
TWO_PI_HIGH = 6.28125
TWO_PI_LOW = 2 * np.pi - TWO_PI_HIGH
TO_WHOLE = 1.5 * 2.0 ** 23
PI = 3.1415925


def lay_selective_scan(a, rows, cols):
    g = lambda n: a["L1_attn_" + n]
    gap = np.zeros((CH, LOW - DBC), np.float32)
    pick = np.zeros((LOW + DBC, NS, 2, P), np.float32)
    for n in range(NS):
        for e in range(2):
            row = RANK + e * NS + n
            pick[[row, LOW + row], n, e] = 1
    per_head = lambda v: cols(np.repeat(v, D // v.shape[0]))
    return {
        "scan_ln": np.stack([cols(g(n)) for n in ("ln1_g", "ln1_b", "ln2_g", "ln2_b")], 1),
        "scan_win": rows(g("W_in")), "scan_bin": cols(g("b_in")),
        "scan_conv": g("conv_w").reshape(CC, P, CONV).transpose(1, 0, 2), "scan_conv_b": cols(g("conv_b")),
        "scan_wxp": rows(np.concatenate([g("W_xp"), gap, g("W_xp")], 1)),
        "scan_wdt": g("W_dt"), "scan_bdt": cols(g("b_dt")),
        "scan_A_log": g("A_log").reshape(CC, P, NS).transpose(1, 0, 2),
        "scan_skip": cols(g("D_skip")),
        "scan_wout": rows(g("W_out")), "scan_bout": g("b_out"),
        "scan_pick": pick,
        "wave_wsi": rows(g("W_si")), "wave_bsi": cols(g("b_si")),
        "wave_gates": np.stack([per_head(g("gates")[:, k]) for k in range(3)], 1),
        "wave_alpha": per_head(g("alpha")),
        "wave_wso": rows(g("W_so")), "wave_bso": g("b_so"),
    }


def selective_scan(nc, c):
    with Scope(nc, "ss") as s:
        ln = s.sb("ln", [P, 4, DC])
        xa = s.sb("xa", [P, NT, D])
        load_norms(nc, c, ln)
        layernorm(nc, c, "ss_ln0", c.x, c.xnT, keep=xa)
        layernorm(nc, c, "ss_ln1", xa, c.xnT, gain=ln[:, 0, :], shift=ln[:, 1, :])
        scan_channels(nc, c, xa)
        layernorm(nc, c, "ss_ln2", xa, c.xnT, gain=ln[:, 2, :], shift=ln[:, 3, :])
        waves(nc, c, xa)


def load_norms(nc, c, ln):
    with Scope(nc, "ss_norms") as s:
        loaded = s.sem("loaded")
        block = s.block()

        @block.sync
        def _(sp):
            sp.dma_start(ln[:], c.dram["scan_ln"]).then_inc(loaded, 16)
            sp.wait_ge(loaded, 16)


def scan_channels(nc, c, xa):
    with Scope(nc, "scan") as s:
        win = s.sb("win", [P, DC, 2 * CH])
        b_in = s.sb("bin", [P, 2 * CC])
        convw = s.sb("convw", [P, CC, CONV])
        conv_b = s.sb("conv_b", [P, CC])
        wxp = s.sb("wxp", [P, CC, LOW + DBC])
        wdt = s.sb("wdt", [RANK, CH])
        b_dt = s.sb("bdt", [P, CC])
        neg_a = s.sb("neg_a", [P, CC, NS])
        skip = s.sb("skip", [P, CC])
        wout = s.sb("wout", [P, CC, D])
        b_out = s.sb("bout", [P, D])
        pick = s.sb("pick", [LOW + DBC, NS, 2, P])
        xp = s.sb("xp", [P, 2, T])
        conv = s.sb("conv", [P, 2, T])
        xc = s.sb("xc", [P, CC, T])
        zs = s.sb("zs", [P, CC, T])
        whole = s.sb("whole", [LOW + DBC, T], F32R)
        parts = s.sb("parts", [LOW + DBC, T], F32R)
        low_rank = s.sb("low_rank", [RANK, T])
        v = s.sb("v", [P, CC, T])
        dt = s.sb("dt", [P, CC, T])
        dtx = s.sb("dtx", [P, CC, T])
        picked = s.sb("picked", [LOW + DBC, 2, 2, P], F32R)
        Bs = s.sb("Bs", [P, 2, T])
        dA = s.sb("dA", [P, 2, CC, T])
        dBx = s.sb("dBx", [P, 2, CC, T])
        h = s.sb("h", [P, CC, T])
        hC = s.sb("hC", [P, 2, CC, T])
        e1, e2 = dA[:, 0], dBx[:, 0]
        gated = dBx[:, 1]
        y_ps = [s.ps(f"y{k}", [P, T]) for k in range(CC)]
        B_ps = [s.ps(f"B{k}", [P, T]) for k in range(2)]
        C_ps = [s.ps(f"C{k}", [P, T]) for k in range(2)]

        loaded = s.sem("loaded")
        ready0 = s.sem("ready0")
        proj_ready = s.sem("proj_ready")
        xp_ready = s.sem("xp_ready")
        conv_ready = s.sem("conv_ready")
        xc_ready = s.sem("xc_ready")
        z_ready = s.sem("z_ready")
        dbc_ready = s.sem("dbc_ready")
        whole_ready = s.sem("whole_ready")
        parts_ready = s.sem("parts_ready")
        rank_ready = s.sem("rank_ready")
        step_ready = s.sem("step_ready")
        v_ready = s.sem("v_ready")
        w_ready = s.sem("w_ready")
        log_ready = s.sem("log_ready")
        exp_ready = s.sem("exp_ready")
        dt_ready = s.sem("dt_ready")
        dtx_ready = s.sem("dtx_ready")
        skip_ready = s.sem("skip_ready")
        zero_ready = s.sem("zero_ready")
        pick_ready = s.sem("pick_ready")
        bc_ready = s.sem("bc_ready")
        B_ready = s.sem("B_ready")
        dA_ready = s.sem("dA_ready")
        dBx_ready = s.sem("dBx_ready")
        scanned = s.sem("scanned")
        hC_ready = s.sem("hC_ready")
        summed = s.sem("summed")
        gated_ready = s.sem("gated_ready")
        out_ready = s.sem("out_ready")
        added = s.sem("added")
        vec = s.sem("vec")
        act_a = s.sem("act_a")
        meet = s.sem("meet")
        passed = s.sem("passed")
        block = s.block()
        LOADS = 12 * 16
        WORKERS = 4
        START = 1
        FREE = 2

        def sequence_end(eng, b):
            eng.drain().then_inc(meet, 1)
            eng.wait_ge(meet, b * WORKERS + WORKERS)
            eng.sem_inc(passed, 1)

        @block.sync
        def _(sp):
            for dst, src in ((win, "win"), (b_in, "bin"), (convw, "conv"), (conv_b, "conv_b"), (wxp, "wxp"), (wdt, "wdt"),
                             (b_dt, "bdt"), (neg_a, "A_log"), (skip, "skip"), (wout, "wout"), (pick, "pick")):
                sp.dma_start(dst[:], c.dram[f"scan_{src}"]).then_inc(loaded, 16)
            sp.dma_start(b_out[:], c.dram["scan_bout"].partition_broadcast(P)).then_inc(loaded, 16)

        @block.gpsimd
        def _(pool):
            pool.wait_ge(loaded, LOADS)
            nc.gpsimd.tensor_tensor(xa[:], xa[:], b_out[:].unsqueeze(1).broadcast_to([P, NT, D]), ALU.add
                                    ).then_inc(ready0, 1)
            with pool.Fori(0, B) as b:
                pool.wait_ge(dt_ready, b + 1)
                pool.sem_inc(passed, 1)
                for k in range(2):
                    last = nc.gpsimd.memset(dA[:, k, :, 0:1], 0.0)
                last.then_inc(zero_ready, 1)
                pool.wait_ge(dtx_ready, b + 1)
                pool.sem_inc(passed, 1)
                with pool.Fori(0, NS // 2) as i:
                    for k in range(2):
                        turn = b * NS + i * 2
                        pool.wait_ge(B_ready, turn + (k + 1 + START))
                        pool.wait_ge(scanned, turn + (k + FREE - 1))
                        nc.gpsimd.tensor_tensor(dBx[:, k], dtx[:], Bs[:, k, :].unsqueeze(1).broadcast_to([P, CC, T]),
                                                ALU.mult).then_inc(dBx_ready, 1)
                sequence_end(pool, b)

        @block.scalar
        def _(act):
            act.wait_ge(loaded, LOADS)
            nc.scalar.activation(neg_a[:], neg_a[:], ACT.Exp).then_inc(ready0, 1)
            with act.Fori(0, B) as b:
                chain = Chain(act, act_a, per=1)
                chain.start(b)
                for m in range(CC):
                    act.wait_ge(proj_ready, b * (2 * CC) + (m + 1))
                    if m >= 2:
                        act.wait_ge(conv_ready, b * CC + (m - 1))
                    nc.scalar.activation(xp[:, m % 2, :], y_ps[m][:], ACT.Identity, bias=b_in[:, m:m + 1]
                                         ).then_inc(xp_ready, 1)
                    if m >= 1:
                        act.wait_ge(conv_ready, b * CC + m)
                        nc.scalar.activation(xc[:, m - 1, :], conv[:, (m - 1) % 2, :], ACT.Silu, bias=conv_b[:, m - 1:m]
                                             ).then_inc(xc_ready, 1)
                act.wait_ge(conv_ready, b * CC + CC)
                nc.scalar.activation(xc[:, CC - 1, :], conv[:, (CC - 1) % 2, :], ACT.Silu, bias=conv_b[:, CC - 1:CC]
                                     ).then_inc(xc_ready, 1)
                for m in range(CC):
                    act.wait_ge(proj_ready, b * (2 * CC) + (CC + m + 1))
                    nc.scalar.activation(zs[:, m, :], y_ps[m][:], ACT.Silu, bias=b_in[:, CC + m:CC + m + 1]
                                         ).then_inc(z_ready, 1)
                act.wait_ge(dbc_ready, b + 1)
                nc.scalar.activation(low_rank[:], B_ps[0][0:RANK, :], ACT.Copy).then_inc(rank_ready, 1)
                nc.scalar.activation(whole[:], B_ps[0][0:LOW + DBC, :], ACT.Copy).then_inc(whole_ready, 1)
                for m in range(CC):
                    act.wait_ge(step_ready, b * CC + (m + 1))
                    last = nc.scalar.activation(v[:, m, :], y_ps[m][:], ACT.Identity, bias=b_dt[:, m:m + 1])
                last.then_inc(v_ready, 1)
                act.wait_ge(v_ready, b + 1)
                chain.link(nc.scalar.activation(e1, v[:], ACT.Abs))
                nc.scalar.activation(e1, e1, ACT.Exp, scale=-1.0).then_inc(exp_ready, 1)
                act.wait_ge(w_ready, b + 1)
                nc.scalar.activation(dt[:], e2, ACT.Ln).then_inc(log_ready, 1)
                chain.close()

                def pick_rows(k, n, sync):
                    if sync is not None:
                        act.wait_ge(bc_ready, sync + START)
                    nc.scalar.activation(picked[:, k], pick[:, ds(n, 1)].rearrange("p a e q -> p (a e) q"), ACT.Copy
                                         ).then_inc(pick_ready, 1)

                def spread_and_decay(k, n, turn):
                    act.wait_ge(bc_ready, turn + (1 + START))
                    act.wait_ge(dBx_ready, turn + (FREE - 1))
                    nc.scalar.activation(Bs[:, k, :], B_ps[k][:], ACT.Copy).then_inc(B_ready, 1)
                    act.wait_ge(scanned, turn + (FREE - 1))
                    act.sem_inc(passed, 1)
                    for m in range(CC):
                        last = nc.scalar.activation(dA[:, k, m, 1:], dt[:, m, 1:], ACT.Exp, scale=neg_a[:, m, ds(n, 1)])
                    last.then_inc(dA_ready, 1)

                pick_rows(0, 0, None)
                act.wait_ge(dt_ready, b + 1)
                act.sem_inc(passed, 1)
                with act.Fori(0, NS // 2 - 1) as i:
                    for k in range(2):
                        turn = b * NS + i * 2 + k
                        pick_rows(1 - k, i * 2 + (k + 1), turn)
                        spread_and_decay(k, i * 2 + k, turn)
                pick_rows(1, NS - 1, b * NS + (NS - 2))
                for k in range(2):
                    spread_and_decay(k, NS - 2 + k, b * NS + (NS - 2 + k))
                sequence_end(act, b)

        @block.vector
        def _(dve):
            dve.sem_inc(scanned, FREE)
            dve.wait_ge(loaded, LOADS)
            dve.wait_ge(ready0, 2)
            nc.vector.tensor_scalar(neg_a[:], neg_a[:], -1.0, None, ALU.mult).then_inc(ready0, 1)
            dve.wait_ge(ready0, 3)
            with dve.Fori(0, B) as b:
                chain = Chain(dve, vec, per=CC * (CONV - 1) + 2)
                chain.start(b)
                for m in range(CC):
                    dve.wait_ge(xp_ready, b * CC + (m + 1))
                    if m >= 2:
                        dve.wait_ge(xc_ready, b * CC + (m - 1))
                    y, x = conv[:, m % 2, :], xp[:, m % 2, :]
                    chain.link(nc.vector.tensor_scalar(y, x, convw[:, m, CONV - 1:CONV], None, ALU.mult))
                    for back in range(1, CONV):
                        last = nc.vector.scalar_tensor_tensor(
                            out=y[:, back:], in0=x[:, :T - back], scalar=convw[:, m, CONV - 1 - back:CONV - back],
                            in1=y[:, back:], op0=ALU.mult, op1=ALU.add)
                        if back < CONV - 1:
                            chain.link(last)
                    last.then_inc(conv_ready, 1)
                dve.wait_ge(whole_ready, b + 1)
                nc.vector.tensor_copy(parts[0:LOW, :], whole[0:LOW, :])
                nc.vector.tensor_tensor(parts[LOW:, :], B_ps[0][LOW:LOW + DBC, :], whole[LOW:, :].bitcast(F32), ALU.subtract
                                        ).then_inc(parts_ready, 1)
                for m in range(CC):
                    last = nc.vector.tensor_scalar(hC[:, 1, m, :], xc[:, m, :], skip[:, m:m + 1], None, ALU.mult)
                last.then_inc(skip_ready, 1)
                dve.wait_ge(exp_ready, b + 1)
                nc.vector.tensor_scalar(e2, e1, 1.0, None, ALU.add).then_inc(w_ready, 1)
                dve.wait_ge(w_ready, b + 1)
                chain.link(nc.vector.scalar_tensor_tensor(out=e1, in0=e2, scalar=1.0, in1=e1, op0=ALU.subtract,
                                                          op1=ALU.subtract))
                chain.link(nc.vector.scalar_tensor_tensor(out=e1, in0=v[:], scalar=0.0, in1=e1, op0=ALU.max,
                                                          op1=ALU.subtract))
                dve.wait_ge(log_ready, b + 1)
                nc.vector.tensor_tensor(dt[:], dt[:], e1, ALU.add).then_inc(dt_ready, 1)
                dve.wait_ge(dt_ready, b + 1)
                nc.vector.tensor_tensor(dtx[:], dt[:], xc[:], ALU.mult).then_inc(dtx_ready, 1)
                dve.wait_ge(zero_ready, b + 1)
                dve.sem_inc(passed, 1)
                flat = lambda v: v.rearrange("p c t -> p (c t)")
                with dve.Fori(0, NS // 2) as i:
                    for k in range(2):
                        turn = b * NS + i * 2
                        dve.wait_ge(dA_ready, turn + (k + 1))
                        dve.wait_ge(dBx_ready, turn + (k + FREE + 1))
                        dve.wait_ge(hC_ready, turn + (k + START))
                        nc.vector.tensor_tensor_scan(flat(h[:]), flat(dA[:, k]), flat(dBx[:, k]), 0.0, ALU.mult, ALU.add
                                                     ).then_inc(scanned, 1)
                        dve.wait_ge(scanned, turn + (k + 1 + FREE))
                        dve.wait_ge(summed, b * (NS + 1) + i * 2 + (k + START))
                        nc.vector.tensor_tensor(hC[:, k], h[:], C_ps[k][:].unsqueeze(1).broadcast_to([P, CC, T]), ALU.mult
                                                ).then_inc(hC_ready, 1)
                dve.wait_ge(summed, b * (NS + 1) + (NS + 1 + START))
                for m in range(CC):
                    last = nc.vector.tensor_tensor(gated[:, m, :], y_ps[m][:], zs[:, m, :], ALU.mult)
                last.then_inc(gated_ready, 1)
                for t in range(TB):
                    row = xa[:, ds(b * TB + t, 1), :].rearrange("p a d -> p (a d)")
                    dve.wait_ge(out_ready, b * TB + (t + 1))
                    nc.vector.tensor_tensor(row, row, B_ps[t % 2][:, 0:D], ALU.add).then_inc(added, 1)
                chain.close()
                sequence_end(dve, b)

        @block.tensor
        def _(pe):
            pe.sem_inc(dBx_ready, FREE)
            for sem in (B_ready, hC_ready, bc_ready, summed):
                pe.sem_inc(sem, START)
            pe.wait_ge(loaded, LOADS)
            with pe.Fori(0, B) as b:
                for m in range(2 * CC):
                    if m >= CC:
                        pe.wait_ge(xp_ready, b * CC + (m - CC + 1))
                    for k in range(DC):
                        last = nc.tensor.matmul(y_ps[m % CC][:], win[:, k, m * P:(m + 1) * P], c.xnT[:, k, ds(b * T, T)],
                                                start=(k == 0), stop=(k == DC - 1))
                    last.then_inc(proj_ready, 1)
                pe.wait_ge(xc_ready, b * CC + CC)
                for m in range(CC):
                    last = nc.tensor.matmul(B_ps[0][0:LOW + DBC, :], wxp[:, m, :], xc[:, m, :], start=(m == 0),
                                            stop=(m == CC - 1))
                last.then_inc(dbc_ready, 1)
                pe.wait_ge(rank_ready, b + 1)
                pe.wait_ge(z_ready, b * CC + CC)
                for m in range(CC):
                    nc.tensor.matmul(y_ps[m][:], wdt[:, m * P:(m + 1) * P], low_rank[:], start=True, stop=True
                                     ).then_inc(step_ready, 1)

                def spread(k, turn):
                    pe.wait_ge(pick_ready, turn + 1)
                    for e, dst in enumerate((B_ps, C_ps)):
                        last = nc.tensor.matmul(dst[k][:], picked[:, k, e, :], parts[:], start=True, stop=True)
                    last.then_inc(bc_ready, 1)

                def add_up(k, first):
                    for m in range(CC):
                        last = nc.tensor.matmul(y_ps[m][:], c.ident[:], hC[:, k, m, :], start=first, stop=True,
                                                skip_group_check=True)
                    last.then_inc(summed, 1)

                pe.wait_ge(parts_ready, b + 1)
                spread(0, b * NS)
                pe.wait_ge(v_ready, b + 1)
                pe.wait_ge(skip_ready, b + 1)
                add_up(1, True)
                with pe.Fori(0, NS // 2 - 1) as i:
                    for k in range(2):
                        turn = b * NS + i * 2 + k
                        pe.wait_ge(B_ready, turn + START)
                        pe.wait_ge(hC_ready, turn + START)
                        spread(1 - k, turn + 1)
                        pe.wait_ge(hC_ready, turn + (1 + START))
                        add_up(k, False)
                end = b * NS + (NS - 2)
                pe.wait_ge(B_ready, end + START)
                pe.wait_ge(hC_ready, end + START)
                spread(1, end + 1)
                for k in range(2):
                    pe.wait_ge(hC_ready, end + (k + 1 + START))
                    add_up(k, False)
                pe.wait_ge(gated_ready, b + 1)
                for t in range(TB):
                    if t >= 2:
                        pe.wait_ge(added, b * TB + (t - 1))
                    for m in range(CC):
                        last = nc.tensor.matmul(B_ps[t % 2][:, 0:D], gated[:, m, t * P:(t + 1) * P], wout[:, m, :],
                                                start=(m == 0), stop=(m == CC - 1))
                    last.then_inc(out_ready, 1)
                sequence_end(pe, b)


def waves(nc, c, xa):
    EDGE = 2
    with Scope(nc, "wave") as s:
        wsi = s.sb("wsi", [P, DC, D])
        b_si = s.sb("bsi", [P, DC])
        gates = s.sb("gates", [P, 3, DC])
        alpha = s.sb("alpha", [P, DC])
        wso = s.sb("wso", [P, DC, D])
        b_so = s.sb("bso", [P, D])
        up = s.sb("up", [P, DC, T + 2 * EDGE])
        wide = lambda n: s.sb(n, [P, DC, T])
        turns, angle, sine, d1, d2, f, kdv, s1, heat, du = (
            wide(n) for n in ("turns", "angle", "sine", "d1", "d2", "f", "kdv", "s1", "heat", "du"))
        u_ps = [s.ps(f"u{k}", [P, T]) for k in range(DC)]
        out_ps = [s.ps(f"out{k}", [P, T]) for k in range(TB)]
        loaded = s.sem("loaded")
        ready0 = s.sem("ready0")
        based = s.sem("based")
        u_ready = s.sem("u_ready")
        inner_ready = s.sem("inner_ready")
        up_ready = s.sem("up_ready")
        angle_ready = s.sem("angle_ready")
        sine_ready = s.sem("sine_ready")
        kdv_ready = s.sem("kdv_ready")
        du_ready = s.sem("du_ready")
        out_ready = s.sem("out_ready")
        added = s.sem("added")
        vec = s.sem("vec")
        gps = s.sem("gps")
        passed = s.sem("passed")
        block = s.block()
        LOADS = 6 * 16
        START = 1
        at = lambda o: up[:, :, o:o + T]

        @block.sync
        def _(sp):
            for dst, src in ((wsi, "wsi"), (b_si, "bsi"), (gates, "gates"), (alpha, "alpha"), (wso, "wso")):
                sp.dma_start(dst[:], c.dram[f"wave_{src}"]).then_inc(loaded, 16)
            sp.dma_start(b_so[:], c.dram["wave_bso"].partition_broadcast(P)).then_inc(loaded, 16)

        @block.tensor
        def _(pe):
            pe.sem_inc(inner_ready, START)
            pe.sem_inc(du_ready, START)
            pe.sem_inc(sine_ready, START)
            pe.sem_inc(out_ready, START)
            pe.wait_ge(loaded, LOADS)
            with pe.Fori(0, B) as b:
                pe.wait_ge(inner_ready, b + START)
                for m in range(DC):
                    for k in range(DC):
                        last = nc.tensor.matmul(u_ps[m][:], wsi[:, k, m * P:(m + 1) * P], c.xnT[:, k, ds(b * T, T)],
                                                start=(k == 0), stop=(k == DC - 1))
                last.then_inc(u_ready, 1)
                pe.wait_ge(du_ready, b + (1 + START))
                for t in range(TB):
                    for k in range(DC):
                        last = nc.tensor.matmul(out_ps[t][:, 0:D], du[:, k, t * P:(t + 1) * P], wso[:, k, :],
                                                start=(k == 0), stop=(k == DC - 1))
                last.then_inc(out_ready, 1)

        @block.scalar
        def _(act):
            act.wait_ge(loaded, LOADS)
            with act.Fori(0, B) as b:
                act.wait_ge(u_ready, b + 1)
                act.wait_ge(du_ready, b + START)
                act.sem_inc(passed, 1)
                for m in range(DC):
                    last = nc.scalar.activation(up[:, m, EDGE:EDGE + T], u_ps[m][:], ACT.Identity, bias=b_si[:, m:m + 1])
                last.then_inc(inner_ready, 1)
                act.wait_ge(inner_ready, b + (1 + START))
                act.sem_inc(passed, 1)
                for to, edge in ((0, EDGE), (EDGE + T, EDGE + T - 1)):
                    last = nc.scalar.activation(up[:, :, to:to + EDGE], up[:, :, edge:edge + 1].broadcast_to([P, DC, EDGE]),
                                                ACT.Copy)
                last.then_inc(up_ready, 1)
                act.wait_ge(angle_ready, b + 1)
                nc.scalar.activation(sine[:], angle[:], ACT.Sin).then_inc(sine_ready, 1)

        @block.gpsimd
        def _(pool):
            pool.wait_ge(loaded, LOADS)
            nc.gpsimd.tensor_tensor(xa[:], xa[:], b_so[:].unsqueeze(1).broadcast_to([P, NT, D]), ALU.add).then_inc(based, 1)
            pool.wait_ge(based, 1)
            nc.gpsimd.tensor_tensor(c.x[:], c.x[:], xa[:], ALU.add).then_inc(based, 1)
            with pool.Fori(0, B) as b:
                chain = Chain(pool, gps, per=2)
                chain.start(b)
                pool.wait_ge(up_ready, b + 1)
                pool.sem_inc(passed, 1)
                nc.gpsimd.tensor_tensor(d1[:], at(3), at(1), ALU.subtract)
                chain.link(nc.gpsimd.tensor_scalar(f[:], at(2), -3.0, 1.0, ALU.mult, ALU.add))
                pool.wait_ge(du_ready, b + START)
                pool.sem_inc(passed, 1)
                chain.link(nc.gpsimd.tensor_tensor(kdv[:], f[:], d1[:], ALU.mult))
                nc.gpsimd.tensor_tensor(d2[:], at(4), at(0), ALU.subtract).then_inc(kdv_ready, 1)
                chain.close()

        @block.vector
        def _(dve):
            dve.wait_ge(loaded, LOADS)
            nc.vector.tensor_scalar(gates[:], gates[:], SOL, None, ALU.mult).then_inc(ready0, 1)
            dve.wait_ge(ready0, 1)
            dve.wait_ge(based, 2)
            with dve.Fori(0, B) as b:
                chain = Chain(dve, vec, per=9 + DC)
                chain.start(b)
                dve.wait_ge(up_ready, b + 1)
                dve.sem_inc(passed, 1)
                chain.link(nc.vector.tensor_scalar(turns[:], at(2), 1 / (2 * np.pi), TO_WHOLE, ALU.mult, ALU.add))
                chain.link(nc.vector.tensor_scalar(turns[:], turns[:], -TO_WHOLE, None, ALU.add))
                chain.link(nc.vector.scalar_tensor_tensor(out=angle[:], in0=turns[:], scalar=-TWO_PI_HIGH, in1=at(2),
                                                          op0=ALU.mult, op1=ALU.add))
                chain.link(nc.vector.scalar_tensor_tensor(out=angle[:], in0=turns[:], scalar=-TWO_PI_LOW, in1=angle[:],
                                                          op0=ALU.mult, op1=ALU.add))
                nc.vector.tensor_scalar(angle[:], angle[:], -PI, PI, ALU.max, ALU.min).then_inc(angle_ready, 1)
                chain.link(nc.vector.tensor_tensor(s1[:], at(3), at(1), ALU.add))
                nc.vector.scalar_tensor_tensor(out=s1[:], in0=at(2), scalar=-2.0, in1=s1[:], op0=ALU.mult, op1=ALU.add)
                for m in range(DC):
                    last = nc.vector.tensor_scalar(heat[:, m, :], up[:, m, EDGE:EDGE + T], alpha[:, m:m + 1], 1.0, ALU.mult, ALU.add)
                chain.link(last)
                chain.link(nc.vector.tensor_tensor(heat[:], heat[:], s1[:], ALU.mult))
                dve.wait_ge(kdv_ready, b + 1)
                chain.link(nc.vector.scalar_tensor_tensor(out=kdv[:], in0=d2[:], scalar=-0.5, in1=kdv[:], op0=ALU.mult, op1=ALU.add))
                dve.wait_ge(out_ready, b + START)
                dve.wait_ge(sine_ready, b + (1 + START))
                dve.sem_inc(passed, 1)
                for m in range(DC):
                    chain.link(nc.vector.tensor_scalar(sine[:, m, :], sine[:, m, :], gates[:, 0, m:m + 1], None, ALU.mult))
                for k, term in ((1, kdv), (2, heat)):
                    for m in range(DC):
                        last = nc.vector.scalar_tensor_tensor(out=du[:, m, :], in0=term[:, m, :], scalar=gates[:, k, m:m + 1],
                                                              in1=(sine if k == 1 else du)[:, m, :], op0=ALU.mult, op1=ALU.add)
                    if k == 1:
                        chain.link(last)
                last.then_inc(du_ready, 1)
                for t in range(TB):
                    row = c.x[:, ds(b * TB + t, 1), :].rearrange("p a d -> p (a d)")
                    dve.wait_ge(out_ready, b + (1 + START))
                    last = nc.vector.tensor_tensor(row, row, out_ps[t][:, 0:D], ALU.add)
                last.then_inc(added, 1)
                chain.close()


NE = 8
CAPACITY = -(-B * T * 5 // (NE * 4))


def lay_experts(a, rows, cols):
    p, f = np.arange(P)[:, None], np.arange(2 * B * T)[None, :]
    return {
        "moe_router": rows(a["L1_ffn_router_w"].T),
        "moe_w1": a["L1_ffn_W1"].reshape(NE, DC, P, DH).transpose(0, 2, 1, 3),
        "moe_b1": a["L1_ffn_b1"].reshape(NE, MH, P).transpose(2, 0, 1),
        "moe_w2": a["L1_ffn_W2"].reshape(NE, MH, P, D).transpose(0, 2, 1, 3),
        "moe_b2": a["L1_ffn_b2"].reshape(1, NE, D),
        "moe_before": (f - B * T < p).astype(np.float32),
        "moe_order": np.tile(np.arange(NE, 0, -1, dtype=np.float32), (P, 1)),
    }


def experts(nc, c):
    layernorm(nc, c, "moe_ln", c.x, c.xnT)
    NB = B * T // 512
    NT4 = 512 // P
    with Scope(nc, "moe_route") as s:
        router = s.sb("router", [P, DC, NE])
        order = s.sb("order", [P, NE])
        before = s.sb("before", [P, 2 * B * T])
        logits = s.sb("logits", [P, NT, NE])
        top = s.sb("top", [P, NT])
        is_top = s.sb("is_top", [P, NT, NE])
        mine = s.sb("mine", [P, 2, NT])
        wide = s.sb("wide", [P, 2, 2, 4, P])
        row = s.sb("row", [P, 2, B * T])
        rival = s.sb("rival", [P, B * T])
        hit = s.sb("hit", [P, B * T])
        place = s.sb("place", [P, NT, 2])
        keep = s.sb("keep", [P, NT])
        l_ps = s.ps("l_ps", [P, NT, NE])
        r_ps = [s.ps(f"r_ps{k}", [P, 512]) for k in range(4)]
        loaded = s.sem("loaded")
        l_ready = s.sem("l_ready")
        less_ready = s.sem("less_ready")
        exp_ready = s.sem("exp_ready")
        vec = s.sem("vec")
        vec_t = s.sem("vec_t")
        wide_ready = s.sem("wide_ready")
        turned = s.sem("turned")
        row_ready = s.sem("row_ready")
        block = s.block()

        @block.sync
        def _(sp):
            for dst, src in ((router, "router"), (order, "order"), (before, "before")):
                sp.dma_start(dst[:], c.dram[f"moe_{src}"]).then_inc(loaded, 16)

        @block.tensor
        def _(pe):
            pe.wait_ge(loaded, 48)
            for t in range(NT):
                for k in range(DC):
                    last = nc.tensor.matmul(l_ps[:, t, :], c.xnT[:, k, t * P:(t + 1) * P], router[:, k, :],
                                            start=(k == 0), stop=(k == DC - 1))
            last.then_inc(l_ready, 1)
            for g in range(NT // 4):
                pe.wait_ge(wide_ready, g + 1)
                if g >= 2:
                    pe.wait_ge(row_ready, g - 1)
                for e in range(2):
                    for t in range(4):
                        last = nc.tensor.transpose(r_ps[g % 2 * 2 + e][:, t * P:(t + 1) * P], wide[:, g % 2, e, t, :], c.ident[:])
                last.then_inc(turned, 1)

        @block.scalar
        def _(act):
            act.wait_ge(less_ready, 1)
            nc.scalar.activation(is_top[:], logits[:], ACT.Exp).then_inc(exp_ready, 1)
            for g in range(NT // 4):
                act.wait_ge(turned, g + 1)
                for e in range(2):
                    last = nc.scalar.activation(row[:, e, g * 512:(g + 1) * 512], r_ps[g % 2 * 2 + e][:], ACT.Copy)
                last.then_inc(row_ready, 1)

        @block.vector
        def _(dve):
            chain = Chain(dve, vec)
            over = lambda v: v.unsqueeze(2).broadcast_to([P, NT, NE])
            dve.wait_ge(loaded, 48)
            dve.wait_ge(l_ready, 1)
            chain.link(nc.vector.tensor_reduce(top[:], l_ps[:], AX, ALU.max))
            nc.vector.tensor_tensor(logits[:], l_ps[:], over(top[:]), ALU.subtract).then_inc(less_ready, 1)
            dve.wait_ge(exp_ready, 1)
            chain.link(nc.vector.tensor_reduce(top[:], is_top[:], AX, ALU.add))
            chain.link(nc.vector.reciprocal(mine[:, 1, :], top[:]))
            chain.link(nc.vector.scalar_tensor_tensor(out=is_top[:], in0=logits[:], scalar=0.0,
                                                      in1=order[:].unsqueeze(1).broadcast_to([P, NT, NE]),
                                                      op0=ALU.is_equal, op1=ALU.mult))
            chain.link(nc.vector.tensor_reduce(mine[:, 0, :], is_top[:], AX, ALU.max))
            for g in range(NT // 4):
                if g >= 2:
                    dve.wait_ge(turned, g - 1)
                for e in range(2):
                    last = nc.vector.tensor_copy(wide[:, g % 2, e], mine[:, e, g * 4:(g + 1) * 4].unsqueeze(2).broadcast_to([P, 4, P]))
                last.then_inc(wide_ready, 1)
            dve.wait_ge(row_ready, NT // 4)
            one = lambda v, t: v[:, ds(t, 1)]
            with dve.Fori(0, NT) as t:
                chain_t = Chain(dve, vec_t, per=3)
                chain_t.start(t)
                chain_t.link(nc.vector.scalar_tensor_tensor(out=rival[:], in0=row[:, 0, :], scalar=one(mine[:, 0, :], t),
                                                            in1=row[:, 1, :], op0=ALU.is_equal, op1=ALU.mult))
                chain_t.link(nc.vector.tensor_scalar(hit[:], rival[:], one(mine[:, 1, :], t), 0.0, ALU.is_gt, ALU.add,
                                                     accum_out=place[:, ds(t, 1), 0]))
                chain_t.link(nc.vector.scalar_tensor_tensor(out=hit[:], in0=rival[:], scalar=one(mine[:, 1, :], t),
                                                            in1=before[:, ds(t * -P + B * T, B * T)], op0=ALU.is_equal,
                                                            op1=ALU.mult, accum_out=place[:, ds(t, 1), 1]))
                chain_t.close()
            chain.link(nc.vector.tensor_tensor(keep[:], place[:, :, 0], place[:, :, 1], ALU.add))
            chain.link(nc.vector.tensor_scalar(keep[:], keep[:], float(CAPACITY), None, ALU.is_lt))
            chain.link(nc.vector.tensor_scalar(mine[:, 0, :], mine[:, 0, :], -1.0, float(NE), ALU.mult, ALU.add))
            chain.link(nc.vector.tensor_tensor(mine[:, 0, :], mine[:, 0, :], keep[:], ALU.mult))
            for e in range(NE):
                last = nc.vector.tensor_scalar(c.chosen[:, :, e], mine[:, 0, :], float(e), None, ALU.is_equal)

    with Scope(nc, "moe") as s:
        w1 = s.sb("w1", [P, 2, DC, DH])
        w2 = s.sb("w2", [P, 2, MH, D])
        b1 = s.sb("b1", [P, NE, MH])
        b2 = s.sb("b2", [1, NE, D])
        hid = [s.sb(f"hid{k}", [P, MH, 512]) for k in range(2)]
        mid = [s.ps(f"mid{k}", [P, 512]) for k in range(4)]
        low = [s.ps(f"low{k}", [P, 512]) for k in range(4)]
        loaded = s.sem("loaded")
        w_loaded = [s.sem(f"w_loaded{k}") for k in range(2)]
        mid_ready = s.sem("mid_ready")
        hid_ready = s.sem("hid_ready")
        out_ready = s.sem("out_ready")
        added = s.sem("added")
        passed = s.sem("passed")
        block = s.block()
        HT = NB * MH

        @block.sync
        def _(sp):
            sp.dma_start(b1[:], c.dram["moe_b1"]).then_inc(loaded, 16)
            sp.dma_start(b2[:], c.dram["moe_b2"]).then_inc(loaded, 16)
            with sp.Fori(0, NE // 2) as i:
                for k in range(2):
                    sp.wait_ge(out_ready, i * (2 * NT) + (k + 1) * NT)
                    sp.dma_start(w1[:, k], c.dram["moe_w1"][ds(i * 2 + k, 1)].rearrange("a p c m -> (a p) c m")).then_inc(w_loaded[k], 16)
                    sp.dma_start(w2[:, k], c.dram["moe_w2"][ds(i * 2 + k, 1)].rearrange("a p c m -> (a p) c m")).then_inc(w_loaded[k], 16)

        @block.scalar
        def _(act):
            act.wait_ge(loaded, 32)
            with act.Fori(0, NE // 2) as i:
                for k in range(2):
                    for n in range(HT):
                        tb, m = n // MH, n % MH
                        at = i * (2 * HT) + (k * HT + n + 1)
                        act.wait_ge(mid_ready, at)
                        act.sem_inc(passed, 1)
                        nc.scalar.activation(hid[tb % 2][:, m, :], mid[n % 4][:], ACT.Relu,
                                             bias=b1[:, ds(i * 2 + k, 1), m]).then_inc(hid_ready, 1)

        @block.vector
        def _(dve):
            with dve.Fori(0, NE // 2) as i:
                for k in range(2):
                    for t in range(NT):
                        dve.wait_ge(out_ready, i * (2 * NT) + (k * NT + t + 1 + 2 * NT))
                        nc.vector.scalar_tensor_tensor(out=c.x[:, t, :], in0=low[t % 4][:, 0:D],
                                                       scalar=c.chosen[:, t, ds(i * 2 + k, 1)], in1=c.x[:, t, :],
                                                       op0=ALU.mult, op1=ALU.add).then_inc(added, 1)

        @block.tensor
        def _(pe):
            pe.sem_inc(out_ready, 2 * NT)
            pe.sem_inc(hid_ready, 4)
            pe.sem_inc(added, 4)
            pe.wait_ge(loaded, 32)
            with pe.Fori(0, NE // 2) as i:
                for k in range(2):
                    pe.wait_ge(w_loaded[k], i * 32 + 32)
                    for tb in range(NB):
                        for m in range(MH):
                            n = tb * MH + m
                            pe.wait_ge(hid_ready, i * (2 * HT) + (k * HT + n + 1))
                            for d in range(DC):
                                last = nc.tensor.matmul(mid[n % 4][:], w1[:, k, d, m * P:(m + 1) * P],
                                                        c.xnT[:, d, tb * 512:(tb + 1) * 512], start=(d == 0), stop=(d == DC - 1))
                            last.then_inc(mid_ready, 1)
                        pe.wait_ge(hid_ready, i * (2 * HT) + (k * HT + (tb + 1) * MH + 4))
                        for t in range(NT4):
                            n = tb * NT4 + t
                            pe.wait_ge(added, i * (2 * NT) + (k * NT + n + 1))
                            pe.sem_inc(passed, 1)
                            nc.tensor.matmul(low[n % 4][:, 0:D], c.ones[0:1, :], b2[:, ds(i * 2 + k, 1), :].rearrange("p a d -> p (a d)"),
                                             start=True, stop=False)
                            for m in range(MH):
                                last = nc.tensor.matmul(low[n % 4][:, 0:D], hid[tb % 2][:, m, t * P:(t + 1) * P], w2[:, k, m, :],
                                                        start=False, stop=(m == MH - 1))
                            last.then_inc(out_ready, 1)


def store(nc, c):
    with Scope(nc, "store") as s:
        stored = s.sem("stored")
        block = s.block()

        @block.sync
        def _(sp):
            sp.dma_start(c.dram["out"], c.x[:]).then_inc(stored, 16)
            sp.wait_ge(stored, 16)


class Core:

    def __init__(self, dram):
        self.dram = dram


LAYERS = [gated_delta_net, masked_attention, ternary_mlp, selective_scan, full_attention, experts]


def program(nc, dram, layers=LAYERS):
    c = Core(dram)
    with ExitStack() as stack:
        c.x = stack.enter_context(nc.sbuf_tensor("x", [P, NT, D], F32))
        c.xnT = stack.enter_context(nc.sbuf_tensor("xnT", [P, DC, B * T], F32))
        c.ident = stack.enter_context(nc.sbuf_tensor("ident", [P, P], F32))
        c.ones = stack.enter_context(nc.sbuf_tensor("ones", [P, P], F32))
        c.eps = stack.enter_context(nc.sbuf_tensor("eps", [P, 1], F32))
        c.chosen = stack.enter_context(nc.sbuf_tensor("chosen", [P, NT, NE], F32))
        constants(nc, c)
        for layer in layers:
            layer(nc, c)
        store(nc, c)


def laid_out(inputs):
    a = {k: np.asarray(v) for k, v in inputs.items()}
    heads = lambda v, h: v.reshape(h, -1).T
    twice = lambda v: np.concatenate([v, v], 0)
    cols = lambda v: v.reshape(-1, P).T
    rows = lambda w: w.reshape(-1, P, w.shape[-1]).transpose(1, 0, 2)
    o = {
        "x": a["x"].reshape(NT, P, D).transpose(1, 0, 2),
        "ctxT": a["ctx_1024"].transpose(0, 2, 1).reshape(B, DC, P, S2).transpose(0, 2, 1, 3),
    }
    o.update(lay_gated_delta_net(a, rows, cols))
    o.update(lay_masked_attention(a, rows, cols))
    o.update(lay_ternary_mlp(a, rows, cols))
    o.update(lay_selective_scan(a, rows, cols))
    o.update(lay_full_attention(a, rows, cols))
    o.update(lay_experts(a, rows, cols))
    return {k: np.ascontiguousarray(v) for k, v in o.items()}


def kernel(**inputs):
    import concourse.bacc as bacc
    from concourse.bass_utils import run_bass_kernel_spmd

    nc = bacc.Bacc("TRN2", target_bir_lowering=False, num_devices=1)
    arrays = laid_out(inputs)
    dram = {k: nc.dram_tensor(f"in_{k}", v.shape, mybir.dt.from_np(v.dtype), kind="ExternalInput").ap()
            for k, v in arrays.items()}
    dram["out"] = nc.dram_tensor("out_0", [P, NT, D], F32, kind="ExternalOutput").ap()
    program(nc, dram)
    r = run_bass_kernel_spmd(nc, [{f"in_{k}": v for k, v in arrays.items()}], core_ids=[0])
    return r.results[0]["out_0"].transpose(1, 0, 2).reshape(B, T, D)
```

```python
from contextlib import ExitStack

import numpy as np

import concourse.bass as bass
from concourse import mybir

ALU = mybir.AluOpType
ACT = mybir.ActivationFunctionType
AX = mybir.AxisListType.X
F32 = mybir.dt.float32
F32R = mybir.dt.float32r
BF16 = mybir.dt.bfloat16
U8 = mybir.dt.uint8
I32 = mybir.dt.int32

P = 128
B, T, D = 4, 512, 256
DC = D // P
NT = B * T // P
TB = T // P
S2 = 1601
KT = -(-S2 // P)
SW = -(-S2 // 4)
LAST = S2 - (KT - 1) * P
NEG = -1.0e30
ds = bass.ds


class Scope:

    def __init__(self, nc, name):
        self.nc, self.name, self.stack, self.sems = nc, name, ExitStack(), []

    def __enter__(self):
        return self

    def __exit__(self, *failure):
        self.stack.close()
        if self.sems:
            self.nc.clear_and_free_semaphores(self.sems)
            self.nc.all_engine_barrier()

    def sb(self, name, shape, dt=F32):
        return self.stack.enter_context(self.nc.sbuf_tensor(f"{self.name}_{name}", shape, dt))

    def ps(self, name, shape, dt=F32):
        return self.stack.enter_context(self.nc.psum_tensor(f"{self.name}_{name}", shape, dt))

    def sem(self, name):
        self.sems.append(self.nc.alloc_semaphore(f"{self.name}_{name}"))
        return self.sems[-1]

    def block(self):
        return self.stack.enter_context(self.nc.Block())


class Chain:

    def __init__(self, eng, sem, per=0, base=0):
        self.eng, self.sem, self.per, self.n, self.turn, self.base = eng, sem, per, 0, 0, base

    def start(self, turn):
        assert self.n in (0, self.per), (self.n, self.per)
        self.turn, self.n = turn, 0

    def link(self, ins):
        self.n += 1
        ins.then_inc(self.sem, 1)
        self.eng.wait_ge(self.sem, self.turn * self.per + (self.base + self.n))

    def close(self):
        assert self.n == self.per, (self.n, self.per)


def constants(nc, c):
    with Scope(nc, "const") as s:
        made = s.sem("made")
        loaded = s.sem("loaded")
        block = s.block()

        @block.gpsimd
        def _(pool):
            nc.gpsimd.memset(c.ident[:], 0.0).then_inc(made, 1)
            nc.gpsimd.memset(c.ones[:], 1.0).then_inc(made, 1)
            nc.gpsimd.memset(c.eps[:], 1e-5).then_inc(made, 1)
            pool.wait_ge(made, 1)
            nc.gpsimd.affine_select(out=c.ident[:], in_=c.ident[:], compare_op=ALU.not_equal, fill=1.0,
                                    base=0, pattern=[[-1, P]], channel_multiplier=1).then_inc(made, 1)

        @block.sync
        def _(sp):
            sp.dma_start(c.x[:], c.dram["x"]).then_inc(loaded, 16)
            sp.wait_ge(loaded, 16)


def layernorm(nc, c, name, src, dst, gain=None, shift=None, keep=None):
    GROUPS = NT // 4
    with Scope(nc, name) as s:
        stats = s.sb("stats", [P, NT, 6])
        mv = s.sb("mv", [P, NT, 2])
        std = s.sb("std", [P, NT])
        rstd = s.sb("rstd", [P, NT])
        xn = s.sb("xn", [P, 2, 4, D])
        turned_ps = [s.ps(f"turned{k}", [P, DC, 512]) for k in range(2)]
        vec = s.sem("vec")
        stats_ready = s.sem("stats_ready")
        std_ready = s.sem("std_ready")
        xn_ready = s.sem("xn_ready")
        turned = s.sem("turned")
        copied = s.sem("copied")
        block = s.block()

        def rows(t):
            return keep[:, t, :] if keep is not None else xn[:, t // 4 % 2, t % 4, :]

        @block.vector
        def _(dve):
            chain = Chain(dve, vec)
            for t in range(NT):
                last = nc.vector.bn_stats(stats[:, t, :], src[:, t, :])
            chain.link(last)
            for t in range(NT):
                last = nc.vector.bn_aggr(mv[:, t, :], stats[:, t, :])
            last.then_inc(stats_ready, 1)
            dve.wait_ge(std_ready, 1)
            chain.link(nc.vector.reciprocal(rstd[:], std[:]))
            for g in range(GROUPS):
                if g >= 2 and keep is None:
                    dve.wait_ge(turned, g - 1)
                for t in range(4 * g, 4 * g + 4):
                    last = nc.vector.tensor_scalar(rows(t), src[:, t, :], mv[:, t, 0:1], rstd[:, t:t + 1],
                                                   ALU.subtract, ALU.mult)
                last.then_inc(xn_ready, 1)

        @block.scalar
        def _(act):
            act.wait_ge(stats_ready, 1)
            nc.scalar.activation(std[:], mv[:, :, 1], ACT.Sqrt, bias=c.eps[:]).then_inc(std_ready, 1)
            for g in range(GROUPS):
                act.wait_ge(turned, g + 1)
                for d in range(DC):
                    last = nc.scalar.activation(dst[:, d, g * 512:(g + 1) * 512], turned_ps[g % 2][:, d, :], ACT.Identity,
                                                bias=shift[:, d:d + 1] if shift is not None else 0.0,
                                                scale=gain[:, d:d + 1] if gain is not None else 1.0)
                last.then_inc(copied, 1)

        @block.tensor
        def _(pe):
            for g in range(GROUPS):
                pe.wait_ge(xn_ready, g + 1)
                if g >= 2:
                    pe.wait_ge(copied, g - 1)
                for d in range(DC):
                    for t in range(4):
                        last = nc.tensor.transpose(turned_ps[g % 2][:, d, t * P:(t + 1) * P],
                                                   rows(4 * g + t)[:, d * P:(d + 1) * P], c.ident[:])
                last.then_inc(turned, 1)


HV, HK, DK = 16, 8, 64
LEVELS = 7
KOFF, VOFF = HK * DK, 2 * HK * DK
CONV = 4


def lay_gated_delta_net(a, rows, cols):
    p, f = np.arange(P)[:, None], np.arange(P)[None, :]
    levels = np.stack([(p >> s + 1 == f >> s + 1) & (p >> s & 1 == 1) & (f >> s & 1 == 0)
                       for s in range(LEVELS)], 1).astype(np.float32)
    return {
        "gdn_wqkv": rows(a["L0_attn_W_qkv"]),
        "gdn_wz": rows(a["L0_attn_W_z"]),
        "gdn_wba": rows(np.concatenate([a["L0_attn_W_b"], a["L0_attn_W_a"]], 1)),
        "gdn_wout": rows(a["L0_attn_W_out"]),
        "gdn_conv": a["L0_attn_conv_w"].reshape(-1, P, CONV).transpose(1, 0, 2),
        "gdn_dt_bias": a["L0_attn_dt_bias"],
        "gdn_A_log": a["L0_attn_A_log"],
        "gdn_norm": a["L0_attn_norm_w"],
        "gdn_levels": levels,
        "gdn_upto": (p <= f).astype(np.float32),
    }


def gated_delta_net(nc, c):
    layernorm(nc, c, "gdn_ln", c.x, c.xnT)
    NM = 2 * HK * DK // P + HV * DK // P
    HG = HV // 4
    NZ = HV * DK // 512
    with Scope(nc, "gdn") as s:
        wqkv = s.sb("wqkv", [P, DC, NM * P])
        wz = s.sb("wz", [P, DC, HV * DK])
        wba = s.sb("wba", [P, DC, 2 * HV])
        wout = s.sb("wout", [P, HV * DK // P, D])
        convw = s.sb("convw", [P, NM, CONV])
        dt_bias = s.sb("dt_bias", [P, HV])
        neg_a = s.sb("neg_a", [P, HV])
        norm_w = s.sb("norm_w", [P, DK])
        levels = s.sb("levels", [P, LEVELS, P])
        upto = s.sb("upto", [P, P])
        eps = s.sb("eps", [P, 1])
        shared = s.sb("shared", [P, 4 * LEVELS * P])
        span = lambda n: shared[:, n * 2 * T:(n + 1) * 2 * T].rearrange("p (a t) -> p a t", t=T)
        xb, conv, act_ct = (span(n) for n in range(3))
        qkv = s.sb("qkv", [P, TB, NM * P])
        gate = s.sb("gate", [P, TB, HV * DK])
        o = s.sb("o", [P, TB, HV * DK])
        oT = qkv[:, TB // 2:TB, :].rearrange("p a (b n) -> p (a b) n", n=T)
        osq = s.sb("osq", [P, 4, DK])
        col = lambda n, h=HV: s.sb(n, [P, TB, h])
        beta, g, G, eG, eGl, eGend = (col(n) for n in ("beta", "g", "G", "eG", "eGl", "eGend"))
        u1, u2, u3 = (col(n) for n in ("u1", "u2", "u3"))
        k_in, k_out, q_in = (col(n) for n in ("k_in", "k_out", "q_in"))
        ss = col("ss")
        rn = col("rn")
        Kn, Qn = (s.sb(n, [P, 2, DK]) for n in ("Kn", "Qn"))
        Kb, Qe = (s.sb(n, [P, 4, DK]) for n in ("Kb", "Qe"))
        Kd, Vb = (s.sb(n, [P, 2, 4, DK]) for n in ("Kd", "Vb"))
        Ug = s.sb("Ug", [P, 4, P])
        kqT = s.sb("kqT", [P, 2, 6, P])
        E = s.sb("E", [P, 2, 4, P])
        EU = s.sb("EU", [P, 4, P])
        Tm = s.sb("Tm", [P, 2, 2, P])
        PT = s.sb("PT", [P, 2, 4, P])
        Ms = [s.sb("M", [P, 4, LEVELS, P])[:], shared[:].rearrange("p (h l t) -> p h l t", h=4, l=LEVELS)]
        XX = s.sb("XX", [P, 2, 2, 2, 2, P])
        Y = s.sb("Y", [P, 4, P])
        Bm = s.sb("Bm", [P, 4, DK])
        U = s.sb("U", [P, 4, DK])
        S = s.sb("S", [P, 2, P])

        tps = s.ps("tps", [P, 8, P])
        wps = [s.ps(f"wps{k}", [P, 2, 2, P]) for k in range(2)]
        gps = s.ps("gps", [P, 4, P])
        kps = s.ps("kps", [P, 2, 2, P])
        yps = [s.ps(f"yps{k}", [P, 4, P]) for k in range(2)]
        proj = [tps[:, 0:4, :].rearrange("p a b -> p (a b)"), tps[:, 4:8, :].rearrange("p a b -> p (a b)")]
        zps = [gps[:].rearrange("p a b -> p (a b)"), kps[:].rearrange("p a b c -> p (a b c)")]
        trps = [w[:].rearrange("p a b c -> p (a b) c") for w in wps]
        ba_ps = yps[0][:, 0, :].rearrange("p (t h) -> p t h", t=TB)
        G_ps, end_ps = (yps[1][:, n, 0:TB * HV].rearrange("p (t h) -> p t h", t=TB) for n in range(2))
        m0_ps = tps[:, 0:4, :].rearrange("p (a h) t -> p a h t", a=2)
        r_ps = gps[:, 0:2, :]
        u_ps = gps[:, 2:4, :].rearrange("p a (b d) -> p (a b) d", b=2)
        o_ps = kps[:, 0, :, :].rearrange("p a b -> p (a b)")
        s_ps = gps[:, 0:2, :]

        loaded = s.sem("loaded")
        ready0 = s.sem("ready0")
        xb_ready = s.sem("xb_ready")
        proj_ready = s.sem("proj_ready")
        tap_ready = s.sem("tap_ready")
        conv_ready = s.sem("conv_ready")
        act_ready = s.sem("act_ready")
        tr_ready = s.sem("tr_ready")
        tr_copied = s.sem("tr_copied")
        z_ready = s.sem("z_ready")
        z_copied = s.sem("z_copied")
        ba_ready = s.sem("ba_ready")
        gate_sum = s.sem("gate_sum")
        softplus_ready = s.sem("softplus_ready")
        g_ready = s.sem("g_ready")
        Gsum_ready = s.sem("Gsum_ready")
        gl_ready = s.sem("gl_ready")
        exp_ready = s.sem("exp_ready")
        sq_ready = s.sem("sq_ready")
        ss_ready = s.sem("ss_ready")
        len_ready = s.sem("len_ready")
        vec_a = s.sem("vec_a")
        vec_t = s.sem("vec_t")
        vec_e = s.sem("vec_e")
        act_a = s.sem("act_a")
        act_t = s.sem("act_t")
        meet = s.sem("meet")
        prep_ready = s.sem("prep_ready")
        turned = s.sem("turned")
        kqT_ready = s.sem("kqT_ready")
        grow_ready = s.sem("grow_ready")
        kk_low = s.sem("kk_low")
        kk_ready = s.sem("kk_ready")
        dd_ready = s.sem("dd_ready")
        E_ready = s.sem("E_ready")
        EU_ready = s.sem("EU_ready")
        M_ready = s.sem("M_ready")
        PT_ready = s.sem("PT_ready")
        Tm_ready = s.sem("Tm_ready")
        m0_ready = s.sem("m0_ready")
        X0_ready = s.sem("X0_ready")
        y_ready = s.sem("y_ready")
        y_copied = s.sem("y_copied")
        w_ready = s.sem("w_ready")
        X_ready = s.sem("X_ready")
        r_ready = s.sem("r_ready")
        B_ready = s.sem("B_ready")
        u_ready = s.sem("u_ready")
        U_ready = s.sem("U_ready")
        o_ready = s.sem("o_ready")
        o_copied = s.sem("o_copied")
        s_ready = s.sem("s_ready")
        S_ready = s.sem("S_ready")
        pool_t = s.sem("pool_t")
        ostd_ready = s.sem("ostd_ready")
        on_ready = s.sem("on_ready")
        oT_ready = s.sem("oT_ready")
        oT_copied = s.sem("oT_copied")
        out_ready = s.sem("out_ready")
        added = s.sem("added")
        passed = s.sem("passed")
        block = s.block()
        LOADS = 10 * 16
        WORKERS = 4
        STAGES = 3
        OG = HV * DK // P

        PREP, TURN, DECAY, GRAM, FIRST = 1, 2, 3, 3, 5

        def seen(eng):
            eng.sem_inc(passed, 1)

        def following(hg, ch, last):
            return (hg, ch + 1) if ch + 1 < TB else None if last else (hg + 1, 0)

        def by_heads(eng, group):
            with eng.Fori(0, HG - 1) as hg:
                group(hg, False)
            group(HG - 1, True)

        def stage_end(eng, b, stage):
            eng.drain().then_inc(meet, 1)
            eng.wait_ge(meet, b * (STAGES * WORKERS) + (stage + 1) * WORKERS)
            eng.sem_inc(passed, 1)

        @block.sync
        def _(sp):
            for dst, src in ((wqkv, "wqkv"), (convw, "conv"), (wz, "wz"), (wba, "wba"), (levels, "levels"),
                             (upto, "upto"), (wout, "wout")):
                sp.dma_start(dst[:], c.dram[f"gdn_{src}"]).then_inc(loaded, 16)
            for dst, src in ((dt_bias, "dt_bias"), (neg_a, "A_log"), (norm_w, "norm")):
                sp.dma_start(dst[:], c.dram[f"gdn_{src}"].partition_broadcast(P)).then_inc(loaded, 16)

        @block.gpsimd
        def _(pool):
            nc.gpsimd.memset(eps[:], 1e-6).then_inc(ready0, 1)
            pool.wait_ge(loaded, LOADS)
            with pool.Fori(0, B) as b:
                pool.wait_ge(z_copied, b * (TB * NZ) + TB * NZ)
                for t in range(TB):
                    zt = gate[:, t, :].rearrange("p (h d) -> p h d", d=DK)
                    nc.gpsimd.tensor_tensor(zt, zt, norm_w[:].unsqueeze(1).broadcast_to([P, HV, DK]), ALU.mult)
                stage_end(pool, b, 0)

                def upper(hg, ch):
                    pool.wait_ge(E_ready, (b * HG + hg) * TB + (ch + 1))
                    nc.gpsimd.tensor_tensor(EU[:], E[:, ch % 2], upto[:].unsqueeze(1).broadcast_to([P, 4, P]),
                                            ALU.mult).then_inc(EU_ready, 1)

                def gated(hg, ch):
                    at = (b * HG + hg) * TB + ch
                    chain = Chain(pool, pool_t, per=int(np.log2(DK)) + 1)
                    chain.start(at)
                    pool.wait_ge(o_copied, at + 2)
                    seen(pool)
                    out, z = (w[:, ch, ds(hg * (4 * DK), 4 * DK)] for w in (o, gate))
                    mine = out.rearrange("p (h d) -> p h d", d=DK)
                    chain.link(nc.gpsimd.tensor_tensor(osq[:], mine, mine, ALU.mult))
                    seen(pool)
                    nc.gpsimd.tensor_tensor(out, out, z, ALU.mult)
                    w = DK // 2
                    while w > 1:
                        chain.link(nc.gpsimd.tensor_tensor(osq[:, :, 0:w], osq[:, :, 0:w], osq[:, :, w:2 * w], ALU.add))
                        w //= 2
                    seen(pool)
                    chain.link(nc.gpsimd.tensor_tensor(ss[:, ch, ds(hg * 4, 4)].unsqueeze(2), osq[:, :, 0:1], osq[:, :, 1:2], ALU.add))
                    seen(pool)
                    chain.close()

                def group(hg, last_heads):
                    for ch in range(TB):
                        if following(hg, ch, last_heads):
                            upper(*following(hg, ch, last_heads))
                        gated(hg, ch)

                upper(0, 0)
                by_heads(pool, group)
                stage_end(pool, b, 1)
                stage_end(pool, b, 2)

        @block.scalar
        def _(act):
            act.wait_ge(loaded, LOADS)
            act.wait_ge(ready0, 1)
            nc.scalar.activation(neg_a[:], neg_a[:], ACT.Exp).then_inc(ready0, 1)
            with act.Fori(0, B) as b:
                chain = Chain(act, act_a, per=2)
                chain.start(b)
                nc.scalar.activation(xb, c.xnT[:, :, ds(b * T, T)], ACT.Copy).then_inc(xb_ready, 1)

                def turn_copy(m):
                    act.wait_ge(tr_ready, b * NM + (m + 1))
                    nc.scalar.activation(qkv[:, :, m * P:(m + 1) * P], trps[m % 2], ACT.Copy).then_inc(tr_copied, 1)

                def last_tap(m):
                    act.wait_ge(proj_ready, b * NM + (m + 1))
                    if m >= 2:
                        act.wait_ge(act_ready, b * NM + (m - 1))
                    nc.scalar.activation(conv[:, m % 2, :], proj[m % 2], ACT.Copy, scale=convw[:, m, CONV - 1:CONV]
                                         ).then_inc(tap_ready, 1)

                last_tap(0)
                for m in range(NM):
                    if m + 1 < NM:
                        last_tap(m + 1)
                    act.wait_ge(conv_ready, b * NM + (m + 1))
                    if m >= 2:
                        act.wait_ge(tr_ready, b * NM + (m - 1))
                    nc.scalar.activation(act_ct[:, m % 2, :], conv[:, m % 2, :], ACT.Silu).then_inc(act_ready, 1)
                    if m >= 1:
                        turn_copy(m - 1)
                turn_copy(NM - 1)
                for n in range(TB * NZ):
                    act.wait_ge(z_ready, b * (TB * NZ) + (n + 1))
                    nc.scalar.activation(gate[:, n // NZ, (n % NZ) * 512:(n % NZ + 1) * 512], zps[n % 2],
                                         ACT.Silu).then_inc(z_copied, 1)
                act.wait_ge(gate_sum, b + 1)
                nc.scalar.activation(u1[:], u1[:], ACT.Exp, scale=-1.0)
                chain.link(nc.scalar.activation(u3[:], u2[:], ACT.Abs))
                chain.link(nc.scalar.activation(u3[:], u3[:], ACT.Exp, scale=-1.0))
                nc.scalar.activation(u3[:], u3[:], ACT.Ln, bias=1.0).then_inc(softplus_ready, 1)
                act.wait_ge(gl_ready, b + 1)
                nc.scalar.activation(eG[:], G[:], ACT.Exp)
                nc.scalar.activation(eGend[:], eGend[:], ACT.Exp)
                nc.scalar.activation(eGl[:], u1[:], ACT.Exp).then_inc(exp_ready, 1)
                nc.scalar.activation(o[:], qkv[:, :, 0:VOFF], ACT.Square).then_inc(sq_ready, 1)
                act.wait_ge(ss_ready, b + 1)
                nc.scalar.activation(ss[:], ss[:], ACT.Sqrt, bias=eps[:]).then_inc(len_ready, 1)
                chain.close()
                stage_end(act, b, 0)

                def copy_turned(hg, ch):
                    act.wait_ge(turned, (b * HG + hg) * TB + (ch + 1))
                    nc.scalar.activation(kqT[:, ch % 2], tps[:, 0:6, :], ACT.Copy).then_inc(kqT_ready, 1)

                def decays(hg, ch):
                    at = (b * HG + hg) * TB + (ch + 1)
                    act.wait_ge(dd_ready, at)
                    nc.scalar.activation(E[:, ch % 2], E[:, ch % 2], ACT.Abs).then_inc(act_t, 1)
                    act.wait_ge(act_t, at)
                    nc.scalar.activation(E[:, ch % 2], E[:, ch % 2], ACT.Exp, scale=-1.0).then_inc(E_ready, 1)

                def group(hg, last_heads):
                    turn = b * HG + hg
                    for ch in range(TB):
                        for lv in range(1, LEVELS):
                            for half in range(2):
                                act.wait_ge(y_ready, turn * (TB * 12) + (ch * 12 + (lv - 1) * 2 + half + 1))
                                nc.scalar.activation(Y[:, 2 * half:2 * half + 2, :], yps[half][:, 0:2, :], ACT.Copy).then_inc(y_copied, 1)
                            if following(hg, ch, last_heads) and lv == TURN:
                                copy_turned(*following(hg, ch, last_heads))
                            if following(hg, ch, last_heads) and lv == DECAY:
                                decays(*following(hg, ch, last_heads))
                        act.wait_ge(u_ready, turn * TB + (ch + 1))
                        nc.scalar.activation(U[:], u_ps, ACT.Copy).then_inc(U_ready, 1)
                        act.wait_ge(o_ready, turn * TB + (ch + 1))
                        nc.scalar.activation(o[:, ch, ds(hg * (4 * DK), 4 * DK)], o_ps, ACT.Copy).then_inc(o_copied, 1)

                copy_turned(0, 0)
                decays(0, 0)
                by_heads(act, group)
                stage_end(act, b, 1)
                nc.scalar.activation(ss[:], ss[:], ACT.Sqrt, bias=eps[:], scale=1.0 / DK).then_inc(ostd_ready, 1)
                for n in range(OG):
                    half, m = n // (OG // 2), n % (OG // 2) * 2
                    act.wait_ge(oT_ready, b * OG + (n + 1))
                    nc.scalar.activation(oT[:, m:m + 2, half * (T // 2):(half + 1) * (T // 2)],
                                         proj[n % 2].rearrange("p (m t) -> p m t", m=2), ACT.Copy).then_inc(oT_copied, 1)
                stage_end(act, b, 2)

        @block.vector
        def _(dve):
            dve.wait_ge(loaded, LOADS)
            dve.wait_ge(ready0, 2)
            nc.vector.tensor_scalar(neg_a[:], neg_a[:], -1.0, None, ALU.mult).then_inc(ready0, 1)
            dve.wait_ge(ready0, 3)
            nc.vector.memset(S[:], 0.0).then_inc(S_ready, 1)
            with dve.Fori(0, B) as b:
                chain = Chain(dve, vec_a, per=NM * (CONV - 2) + 7)
                chain.start(b)
                for m in range(NM):
                    dve.wait_ge(tap_ready, b * NM + (m + 1))
                    y, x = conv[:, m % 2, :], proj[m % 2]
                    for back in range(1, CONV):
                        last = nc.vector.scalar_tensor_tensor(
                            out=y[:, back:], in0=x[:, :T - back], scalar=convw[:, m, CONV - 1 - back:CONV - back],
                            in1=y[:, back:], op0=ALU.mult, op1=ALU.add)
                        if back < CONV - 1:
                            chain.link(last)
                    last.then_inc(conv_ready, 1)
                heads = lambda v: v.unsqueeze(1).broadcast_to([P, TB, HV])
                dve.wait_ge(ba_ready, b + 1)
                nc.vector.tensor_copy(u1[:], ba_ps[:, :, 0:HV])
                nc.vector.tensor_tensor(u2[:], ba_ps[:, :, HV:2 * HV], heads(dt_bias[:]), ALU.add).then_inc(gate_sum, 1)
                dve.wait_ge(softplus_ready, b + 1)
                chain.link(nc.vector.tensor_scalar(u1[:], u1[:], 1.0, None, ALU.add))
                chain.link(nc.vector.reciprocal(beta[:], u1[:]))
                chain.link(nc.vector.scalar_tensor_tensor(out=u3[:], in0=u2[:], scalar=0.0, in1=u3[:],
                                                          op0=ALU.max, op1=ALU.add))
                nc.vector.tensor_tensor(g[:], u3[:], heads(neg_a[:]), ALU.mult).then_inc(g_ready, 1)
                dve.wait_ge(Gsum_ready, b + 1)
                nc.vector.tensor_copy(G[:], G_ps)
                chain.link(nc.vector.tensor_copy(eGend[:], end_ps))
                nc.vector.tensor_tensor(u1[:], eGend[:], G[:], ALU.subtract).then_inc(gl_ready, 1)
                dve.wait_ge(sq_ready, b + 1)
                nc.vector.tensor_reduce(ss[:].rearrange("p t h -> p (t h)"),
                                        o[:].rearrange("p t (h d) -> p (t h) d", d=DK), AX, ALU.add).then_inc(ss_ready, 1)
                dve.wait_ge(len_ready, b + 1)
                chain.link(nc.vector.reciprocal(rn[:], ss[:]))
                rq, rk = rn[:, :, 0:HK], rn[:, :, HK:2 * HK]
                chain.link(nc.vector.tensor_scalar(rq, rq, float(DK) ** -0.5, None, ALU.mult))
                dve.wait_ge(exp_ready, b + 1)
                both = lambda v: v.unsqueeze(3).broadcast_to([P, TB, HK, 2])
                split = lambda v: v.rearrange("p t (h r) -> p t h r", r=2)
                chain.link(nc.vector.tensor_tensor(k_in[:], beta[:], eG[:], ALU.mult))
                nc.vector.tensor_tensor(split(k_in[:]), split(k_in[:]), both(rk), ALU.mult)
                nc.vector.tensor_tensor(split(k_out[:]), split(eGl[:]), both(rk), ALU.mult)
                nc.vector.tensor_tensor(split(q_in[:]), split(eG[:]), both(rq), ALU.mult)
                chain.close()
                stage_end(dve, b, 0)
                def prep(hg, ch):
                    k = ch % 2
                    q = qkv[:, ch, ds(hg * P, P)].rearrange("p (h d) -> p h d", d=DK)
                    kk = qkv[:, ch, ds(hg * P + KOFF, P)].rearrange("p (h d) -> p h d", d=DK)
                    v = qkv[:, ch, ds(hg * (2 * P) + VOFF, 2 * P)].rearrange("p (h d) -> p h d", d=DK)
                    key = lambda w, at: w[:, ch, ds(hg * 2 + at, 2)].unsqueeze(2).broadcast_to([P, 2, DK])
                    four = lambda w, n: w[:, ch, ds(hg * 4, 4)].unsqueeze(2).broadcast_to([P, 4, n])
                    twice = lambda w: w.unsqueeze(2).broadcast_to([P, 2, 2, DK])
                    value = lambda w: w[:, ch, ds(hg * 4, 4)].rearrange(
                        "p (h r) -> p h r", r=2).unsqueeze(3).broadcast_to([P, 2, 2, DK])
                    by_key = lambda w: w.rearrange("p (h r) d -> p h r d", r=2)
                    nc.vector.tensor_tensor(Kn[:], kk, key(rn, HK), ALU.mult)
                    nc.vector.tensor_tensor(Qn[:], q, key(rn, 0), ALU.mult)
                    nc.vector.tensor_tensor(by_key(Kb[:]), twice(kk), value(k_in), ALU.mult)
                    nc.vector.tensor_tensor(by_key(Kd[:, k]), twice(kk), value(k_out), ALU.mult)
                    nc.vector.tensor_tensor(by_key(Qe[:]), twice(q), value(q_in), ALU.mult)
                    nc.vector.tensor_tensor(Vb[:, k], v, four(beta, DK), ALU.mult)
                    nc.vector.tensor_tensor(Ug[:], upto[:].unsqueeze(1).broadcast_to([P, 4, P]), four(g, P),
                                            ALU.mult).then_inc(prep_ready, 1)

                by_key4 = lambda w: w.rearrange("p (h r) t -> p h r t", r=2)
                one = c.ident[:].unsqueeze(1).unsqueeze(1).broadcast_to([P, 2, 2, P])

                def log_decays(hg, ch):
                    dve.wait_ge(grow_ready, (b * HG + hg) * TB + (ch + 1))
                    nc.vector.tensor_tensor(E[:, ch % 2], gps[:], G[:, ch, ds(hg * 4, 4)].unsqueeze(2).broadcast_to([P, 4, P]),
                                            ALU.subtract).then_inc(dd_ready, 1)

                def lower(hg, ch, members):
                    dve.wait_ge(kk_ready, (b * HG + hg) * TB + (ch + 1))
                    seen(dve)
                    for h in members:
                        nc.vector.scalar_tensor_tensor(
                            out=Ms[ch % 2][:, h], in0=kps[:, h // 2, 0, :].unsqueeze(1).broadcast_to([P, LEVELS, P]),
                            scalar=beta[:, ch, ds(hg * 4 + h, 1)], in1=levels[:], op0=ALU.mult, op1=ALU.mult
                            ).then_inc(M_ready, 1)

                def blocks(hg, ch):
                    dve.wait_ge(M_ready, (b * HG + hg) * (TB * 4) + (ch + 1) * 4)
                    nc.vector.tensor_tensor(XX[:, ch % 2, :, 1], one,
                                            Ms[ch % 2][:, :, 0, :].rearrange("p (a h) t -> p a h t", a=2), ALU.subtract)
                    dve.wait_ge(m0_ready, (b * HG + hg) * TB + (ch + 1))
                    nc.vector.tensor_tensor(XX[:, ch % 2, :, 0], one, m0_ps, ALU.subtract).then_inc(X0_ready, 1)

                def inner(hg, ch):
                    dve.wait_ge(EU_ready, (b * HG + hg) * TB + (ch + 1))
                    nc.vector.tensor_tensor(by_key4(PT[:, ch % 2]), kps[:, :, 1, :].unsqueeze(2).broadcast_to([P, 2, 2, P]),
                                            by_key4(EU[:]), ALU.mult).then_inc(PT_ready, 1)

                def group(hg, last_heads):
                    turn = b * HG + hg
                    for ch in range(TB):
                        at = turn * TB + (ch + 1)
                        X = XX[:, ch % 2]
                        for lv in range(1, LEVELS):
                            nxt = following(hg, ch, last_heads)
                            if nxt and lv == PREP:
                                prep(*nxt)
                            for half in range(2):
                                dve.wait_ge(w_ready, turn * (TB * 12) + (ch * 12 + (lv - 1) * 2 + half + 1))
                                n = 2 if lv < LEVELS - 1 else 1
                                nc.vector.tensor_tensor(X[:, half, 0:n], X[:, half, 0:n], wps[half][:, 0:n],
                                                        ALU.subtract).then_inc(X_ready, 1)
                            if nxt:
                                if lv == TURN:
                                    log_decays(*nxt)
                                if lv == GRAM:
                                    lower(*nxt, (0, 1))
                                if lv == GRAM + 1:
                                    lower(*nxt, (2, 3))
                                if lv == FIRST:
                                    blocks(*nxt)
                                    inner(*nxt)
                        dve.wait_ge(X_ready, turn * (TB * 12) + (ch + 1) * 12)
                        nc.vector.tensor_tensor(Tm[:], X[:, :, 0], E[:, ch % 2].rearrange("p (a h) t -> p a h t", a=2),
                                                ALU.mult).then_inc(Tm_ready, 1)
                        dve.wait_ge(r_ready, at)
                        nc.vector.tensor_tensor(Bm[:], Vb[:, ch % 2], r_ps.rearrange("p a (b d) -> p (a b) d", d=DK),
                                                ALU.subtract).then_inc(B_ready, 1)
                        if ch == TB - 1:
                            dve.wait_ge(o_ready, at)
                            seen(dve)
                            nc.vector.memset(S[:], 0.0).then_inc(S_ready, 1)
                        else:
                            dve.wait_ge(s_ready, turn * (TB - 1) + (ch + 1))
                            for h in range(4):
                                rows, cs = slice(DK * (h % 2), DK * (h % 2) + DK), slice(DK * (h % 2), DK * (h % 2) + DK)
                                last = nc.vector.scalar_tensor_tensor(
                                    out=S[rows, h // 2, cs], in0=S[rows, h // 2, cs],
                                    scalar=eGend[rows, ch, ds(hg * 4 + h, 1)], in1=s_ps[rows, h // 2, cs],
                                    op0=ALU.mult, op1=ALU.add)
                            last.then_inc(S_ready, 1)

                prep(0, 0)
                log_decays(0, 0)
                lower(0, 0, range(4))
                blocks(0, 0)
                inner(0, 0)
                by_heads(dve, group)
                stage_end(dve, b, 1)
                dve.wait_ge(ostd_ready, b + 1)
                chain = Chain(dve, vec_e, per=1)
                chain.start(b)
                chain.link(nc.vector.reciprocal(rn[:], ss[:]))
                for half in range(2):
                    tiles = slice(half * (TB // 2), (half + 1) * (TB // 2))
                    oh = o[:, tiles, :].rearrange("p t (h d) -> p (t h) d", d=DK)
                    nc.vector.tensor_tensor(oh, oh, rn[:, tiles, :].rearrange("p t h -> p (t h)").unsqueeze(2).broadcast_to(
                        [P, TB // 2 * HV, DK]), ALU.mult).then_inc(on_ready, 1)
                chain.close()
                for t in range(TB):
                    dve.wait_ge(out_ready, b * TB + (t + 1))
                    row = c.x[:, ds(b * TB + t, 1), :].rearrange("p a d -> p (a d)")
                    nc.vector.tensor_tensor(row, row, zps[t % 2][:, 0:D], ALU.add).then_inc(added, 1)
                stage_end(dve, b, 2)

        @block.tensor
        def _(pe):
            pe.wait_ge(loaded, LOADS)
            pe.sem_inc(o_copied, 1)
            with pe.Fori(0, B) as b:
                pe.wait_ge(xb_ready, b + 1)

                def turn_tile(m):
                    pe.wait_ge(act_ready, b * NM + (m + 1))
                    if m >= 2:
                        pe.wait_ge(tr_copied, b * NM + (m - 1))
                    for t in range(TB):
                        last = nc.tensor.transpose(trps[m % 2][:, t, :], act_ct[:, m % 2, t * P:(t + 1) * P], c.ident[:])
                    last.then_inc(tr_ready, 1)

                for m in range(NM):
                    if m >= 2:
                        pe.wait_ge(conv_ready, b * NM + (m - 1))
                    for k in range(DC):
                        last = nc.tensor.matmul(proj[m % 2], wqkv[:, k, m * P:(m + 1) * P], xb[:, k, :],
                                                start=(k == 0), stop=(k == DC - 1))
                    last.then_inc(proj_ready, 1)
                    if m >= 2:
                        turn_tile(m - 2)
                turn_tile(NM - 2)
                turn_tile(NM - 1)
                for t in range(TB):
                    for k in range(DC):
                        last = nc.tensor.matmul(ba_ps[:, t, :], xb[:, k, t * P:(t + 1) * P], wba[:, k, :],
                                                start=(k == 0), stop=(k == DC - 1))
                last.then_inc(ba_ready, 1)
                for n in range(TB * NZ):
                    t, half = n // NZ, n % NZ
                    if n >= 2:
                        pe.wait_ge(z_copied, b * (TB * NZ) + (n - 1))
                    for k in range(DC):
                        last = nc.tensor.matmul(zps[n % 2], xb[:, k, t * P:(t + 1) * P],
                                                wz[:, k, half * 512:(half + 1) * 512],
                                                start=(k == 0), stop=(k == DC - 1))
                    last.then_inc(z_ready, 1)
                pe.wait_ge(g_ready, b + 1)
                nc.tensor.matmul(G_ps, upto[:], g[:], start=True, stop=True)
                nc.tensor.matmul(end_ps, c.ones[:], g[:], start=True, stop=True).then_inc(Gsum_ready, 1)
                stage_end(pe, b, 0)

                def turn_keys(hg, ch, first=False):
                    at = (b * HG + hg) * TB + (ch + 1)
                    k = ch % 2
                    pe.wait_ge(prep_ready, at)
                    if not first:
                        pe.wait_ge(X0_ready, at - 1)
                    two = lambda w: w.rearrange("p h d -> p (h d)")
                    for n, w in enumerate((Kn[:], Qn[:], Kb[:, 0:2], Kb[:, 2:4], Qe[:, 0:2], Qe[:, 2:4])):
                        last = nc.tensor.transpose(tps[:, n, :], two(w), c.ident[:])
                    last.then_inc(turned, 1)
                    pe.wait_ge(S_ready, at if first else at - 1)
                    nc.tensor.matmul(gps[:], c.ones[:], Ug[:], start=True, stop=True).then_inc(grow_ready, 1)

                def gram(hg, ch, first=False):
                    at = (b * HG + hg) * TB + (ch + 1)
                    T_ = kqT[:, ch % 2]
                    pe.wait_ge(kqT_ready, at)
                    pe.wait_ge(o_copied, at if first else at - 1)
                    low, high = slice(0, DK), slice(DK, 2 * DK)
                    nc.tensor.matmul(kps[:, 0], T_[low, 0, :], T_[low, 0:2, :], start=True, stop=True).then_inc(kk_low, 1)
                    pe.wait_ge(kk_low, at)
                    nc.tensor.matmul(kps[:, 1], T_[high, 0, :], T_[high, 0:2, :], start=True, stop=True).then_inc(kk_ready, 1)

                def turn_first(hg, ch, first=False):
                    pe.wait_ge(M_ready, (b * HG + hg) * (TB * 4) + (ch + 1) * 4)
                    pe.wait_ge(kqT_ready, (b * HG + hg) * TB + (ch + 1))
                    for h in range(4):
                        last = nc.tensor.transpose(m0_ps[:, h // 2, h % 2, :], Ms[ch % 2][:, h, 0, :], c.ident[:])
                    last.then_inc(m0_ready, 1)

                def group(hg, last_heads):
                    turn = b * HG + hg
                    for ch in range(TB):
                        k = ch % 2
                        at = turn * TB + (ch + 1)
                        M, X = Ms[k], XX[:, k]
                        pe.wait_ge(X0_ready, at)
                        for lv in range(1, LEVELS):
                            step = ch * 12 + (lv - 1) * 2
                            for half in range(2):
                                if lv > 1:
                                    pe.wait_ge(X_ready, turn * (TB * 12) + (step - 2 + half + 1))
                                for e in range(2):
                                    h = 2 * half + e
                                    last = nc.tensor.matmul(yps[half][:, e, :], M[:, h, lv, :], X[:, half, 0, e, :],
                                                            start=True, stop=True)
                                last.then_inc(y_ready, 1)
                            nxt = following(hg, ch, last_heads)
                            if nxt:
                                if lv == TURN:
                                    turn_keys(*nxt)
                            for half in range(2):
                                pe.wait_ge(y_copied, turn * (TB * 12) + (step + half + 1))
                                for e in range(2):
                                    h = 2 * half + e
                                    last = nc.tensor.matmul(wps[half][:, 0, e, :], X[:, half, 1, e, :], Y[:, h, :],
                                                            start=True, stop=True)
                                    if lv < LEVELS - 1:
                                        last = nc.tensor.matmul(wps[half][:, 1, e, :], Y[:, h, :], X[:, half, 1, e, :],
                                                                start=True, stop=True)
                                last.then_inc(w_ready, 1)
                            if nxt and lv == GRAM:
                                gram(*nxt)
                            if nxt and lv == FIRST:
                                turn_first(*nxt)
                        if nxt:
                            pe.wait_ge(dd_ready, at + 1)
                            pe.wait_ge(PT_ready, at + 1)
                        for e in range(2):
                            last = nc.tensor.matmul(r_ps[:, e, :], kqT[:, k, 2 + e, :], S[:, e, :], start=True, stop=True)
                        last.then_inc(r_ready, 1)
                        pe.wait_ge(Tm_ready, at)
                        pe.wait_ge(B_ready, at)
                        for h in range(4):
                            last = nc.tensor.matmul(u_ps[:, h, :], Tm[:, h // 2, h % 2, :], Bm[:, h, :],
                                                    start=True, stop=True)
                        last.then_inc(u_ready, 1)
                        pe.wait_ge(U_ready, at)
                        pe.wait_ge(PT_ready, at)
                        for e in range(2):
                            nc.tensor.matmul(o_ps[:, e * P:(e + 1) * P], kqT[:, k, 4 + e, :], S[:, e, :], start=True,
                                             stop=False, skip_group_check=True)
                            for h in (2 * e, 2 * e + 1):
                                last = nc.tensor.matmul(o_ps[:, h * DK:(h + 1) * DK], PT[:, k, h, :], U[:, h, :], start=False,
                                                        stop=True, skip_group_check=True)
                        last.then_inc(o_ready, 1)
                        if ch < TB - 1:
                            for e in range(2):
                                last = nc.tensor.matmul(s_ps[:, e, :], Kd[:, k, 2 * e:2 * e + 2], U[:, 2 * e:2 * e + 2],
                                                        start=True, stop=True)
                            last.then_inc(s_ready, 1)

                turn_keys(0, 0, first=True)
                gram(0, 0, first=True)
                turn_first(0, 0)
                by_heads(pe, group)
                stage_end(pe, b, 1)
                for half in range(2):
                    pe.wait_ge(on_ready, b * 2 + (half + 1))
                    for n in range(half * (OG // 2), (half + 1) * (OG // 2)):
                        if n >= 2:
                            pe.wait_ge(oT_copied, b * OG + (n - 1))
                        for k in range(4):
                            m, t = n % (OG // 2) * 2 + k // 2, half * (TB // 2) + k % 2
                            last = nc.tensor.transpose(proj[n % 2][:, k * P:(k + 1) * P], o[:, t, m * P:(m + 1) * P], c.ident[:])
                        last.then_inc(oT_ready, 1)
                    pe.wait_ge(oT_copied, b * OG + (half + 1) * (OG // 2))
                    for t in range(half * (TB // 2), (half + 1) * (TB // 2)):
                        if t >= 2:
                            pe.wait_ge(added, b * TB + (t - 1))
                        for m in range(HV * DK // P):
                            last = nc.tensor.matmul(zps[t % 2][:, 0:D], oT[:, m, t * P:(t + 1) * P], wout[:, m, :],
                                                    start=(m == 0), stop=(m == HV * DK // P - 1))
                        last.then_inc(out_ready, 1)
                stage_end(pe, b, 2)


HPG = 4
SP = 4 * SW
KW = 64


def lay_attention(name, a, rows, wq, bq, wk, bk, wv, bv, wo, bo, heads):
    d = wv.shape[1] // heads

    def twice(w):
        w = w.reshape(*w.shape[:-1], -1, KW)
        return np.concatenate([w, w], -1)

    n = wq.shape[1] // KW
    stacks = lambda w: rows(twice(w).reshape(D, n * P)).reshape(P, DC, n, P).transpose(2, 0, 1, 3)
    p = np.arange(P)[:, None]
    return {
        f"{name}_wqk": np.stack([stacks(wq), stacks(wk)], 2),
        f"{name}_bqk": np.stack([twice(bq).T, twice(bk).T], 1),
        f"{name}_member": (p % KW // d == np.arange(HPG)).astype(np.float32),
        f"{name}_wv": rows(wv),
        f"{name}_bv": bv,
        f"{name}_wo": np.concatenate([wo.reshape(heads, d, D).transpose(1, 0, 2)] * 2, 0),
        f"{name}_bo": bo,
    }


def lay_masked_attention(a, rows, cols):
    g = lambda n: a["L0_xattn_" + n]
    o = lay_attention("xa0", a, rows, g("Wq"), g("bq"), g("Wk"), g("bk"), g("Wv"), g("bv"), g("Wo"), g("bo"), 16)
    bytes_ = np.pad(a["mask_BxSxS2_bk1"].view(np.uint8).reshape(B, TB, P, S2), [(0, 0)] * 3 + [(0, SP - S2)],
                    constant_values=1)
    o["mask"] = bytes_.view(np.int32)
    return o


def lay_full_attention(a, rows, cols):
    g = lambda n: a["L1_xattn_" + n]
    return lay_attention("xa1", a, rows, g("W_q").T, g("b_q"), g("W_k").T, g("b_k"), g("W_v").T, g("b_v"),
                         g("W_o").T, g("b_o"), 16)


def masked_attention(nc, c):
    attention(nc, c, "xa0", heads=16, dk=64, masked=True)


def full_attention(nc, c):
    attention(nc, c, "xa1", heads=16, dk=16, masked=False)


def attention(nc, c, name, heads, dk, masked):
    layernorm(nc, c, f"{name}_ln", c.x, c.xnT)
    wide_heads = dk == KW
    NG = heads // HPG
    VW = 256
    MV = 2 * dk
    UN = HPG * TB
    PAIRS = UN // 2
    SCALE = float(dk) ** -0.5
    KC = [(n * 512, min(512, S2 - n * 512)) for n in range(-(-S2 // 512))]
    SWW = SW + SW % 2
    if wide_heads:
        KC = KC[:2] + KC[:1:-1]
    WIDE = 3 * SW + SWW
    G4 = [(g, min(g + 4, KT)) for g in range(0, KT, 4)]
    GN = len(G4)
    NPT = 1 if wide_heads else 2
    WB = 1
    NP = 1 + len(KC)
    with Scope(nc, name) as s:
        wv = s.sb("wv", [P, DC, heads * dk])
        wo = s.sb("wo", [MV, heads, D])
        bqk = s.sb("bqk", [P, 2, heads * dk // KW])
        bv = s.sb("bv", [P, heads * dk])
        bo = s.sb("bo", [P, D])
        ctxT = s.sb("ctxT", [P, DC, S2])
        wqk = s.sb("wqk", [P, WB, 2, DC, P])
        Vf = s.sb("Vf", [P, KT, VW])
        V = s.sb("V", [P, KT, HPG, 2, dk], F32R)
        Q = s.sb("Q", [P, 2, 2, T], F32R)
        K = s.sb("K", [P, 2 if wide_heads else NG, WIDE], F32R)
        prob = s.sb("prob", [P, 2, SP])
        PT = s.sb("PT", [P, NPT, 2, KT, 2, P], F32R)
        mx = s.sb("mx", [P, 2])
        neg = s.sb("neg", [P, 2])
        total = s.sb("total", [P, 2])
        rtotal = s.sb("rtotal", [P, 2])
        diag = s.sb("diag", [P, 2, 2, P])
        share = s.sb("share", [MV, 2 * P])
        attT = s.sb("attT", [MV, HPG, T])
        if masked:
            mask8 = s.sb("mask8", [P, TB, SW], I32)
        mask = s.sb("mask", [P, TB if masked else 1, SP], BF16)
        if not wide_heads:
            member = s.sb("member", [P, HPG])
            qf = s.sb("qf", [P, NG, T])
        sps = s.ps("sps", [P, 4, 512])
        tps = [s.ps(f"tps{k}", [P, 4, P]) for k in range(2)]
        pv = s.ps("pv", [P, 512])
        proj = s.ps("proj", [P, 512])
        flat = [t[:].rearrange("p a b -> p (a b)") for t in tps]
        banks = [proj[:], *flat]

        loaded = s.sem("loaded")
        pad_ready = s.sem("pad_ready")
        ctx_loaded = s.sem("ctx_loaded")
        mask_loaded = s.sem("mask_loaded")
        mask_ready = s.sem("mask_ready")
        w_loaded = [s.sem(f"w_loaded{k}") for k in range(WB)]
        v_ready = s.sem("v_ready")
        v_copied = s.sem("v_copied")
        v_hi = s.sem("v_hi")
        v_lo = s.sem("v_lo")
        proj_ready = s.sem("proj_ready")
        proj_hi = s.sem("proj_hi")
        proj_lo = s.sem("proj_lo")
        q_hi = s.sem("q_hi")
        q_lo = s.sem("q_lo")
        s_ready = s.sem("s_ready")
        max_ready = s.sem("max_ready")
        neg_ready = s.sem("neg_ready")
        p_ready = s.sem("p_ready")
        t_ready = s.sem("t_ready")
        t_hi = s.sem("t_hi")
        t_lo = s.sem("t_lo")
        inv_ready = s.sem("inv_ready")
        diag_ready = s.sem("diag_ready")
        pv_ready = s.sem("pv_ready")
        share_ready = s.sem("share_ready")
        att_ready = s.sem("att_ready")
        out_ready = s.sem("out_ready")
        added = s.sem("added")
        based = s.sem("based")
        passed = s.sem("passed")
        block = s.block()
        LOADS = (5 if wide_heads else 6) * 16
        PADS = 2 if masked else 4
        START = 2
        OUTS = 2 * HPG if wide_heads else 2
        FREE = 1
        WAHEAD = 1 + (WB - 1) * NP
        SN = NG * HPG if wide_heads else NG

        def seen(eng):
            eng.sem_inc(passed, 1)

        def keys(kt):
            return P if kt < KT - 1 else LAST

        def chunk(n):
            return (0, T) if n == 0 else KC[n - 1]

        VP = 2 if wide_heads else 1

        def value_parts(gr):
            n = HPG // VP
            start = lambda h: h * dk if wide_heads else gr * (HPG * dk) + h * dk
            return [(slice(k * n, (k + 1) * n), ds(start(k * n), n * dk)) for k in range(VP)]

        def by_groups(eng, group):
            with eng.Fori(0, NG - 1) as gr:
                group(gr, False)
            group(NG - 1, True)

        def following(gr, u, last):
            return (gr, u + 1) if u + 1 < UN else None if last else (gr + 1, 0)

        def next_head(gr, hh, last):
            return (gr, hh + 1) if hh + 1 < HPG else None if last else (gr + 1, 0)

        TBANKS = 2 if wide_heads else 3

        def turned_bank(u, g):
            return (*tps, proj[:].rearrange("p (k q) -> p k q", q=P))[(u * GN + g) % TBANKS]

        NEXT = {(0, "B"): 0, (1, "A"): 1, (1, "B"): 2, (1, "C"): 3, (2, "A"): 4} if wide_heads else {}
        OUT = {(3, "A"): 0, (3, "B"): 1} if wide_heads else {}
        places = [(hh, q, p) for hh in range(HPG) for q, p in ((0, "A" if hh else "C"), (2, "B"), (3, "A"), (3, "C"))
                  if not (hh and (q, p) in OUT)]
        VALUES = {place: kt for kt, place in enumerate(places)} if wide_heads else {}

        def bank_of(n):
            return pv if n == 2 else proj

        def half_bank(half):
            return pv if half else proj

        def behind(u):
            return u // 2 - (1 if wide_heads else 2) if u % 2 == 0 and u >= 2 * NPT else None

        @block.sync
        def _(sp):
            for dst, src in ((bqk, "bqk"), (wv, "wv"), (wo, "wo")) + (() if wide_heads else ((member, "member"),)):
                sp.dma_start(dst[:], c.dram[f"{name}_{src}"]).then_inc(loaded, 16)
            for dst, src in ((bv, "bv"), (bo, "bo")):
                sp.dma_start(dst[:], c.dram[f"{name}_{src}"].partition_broadcast(P)).then_inc(loaded, 16)
            with sp.Fori(0, B) as b:
                sp.wait_ge(proj_ready, b * (SN * NP) + WAHEAD)
                sp.dma_start(ctxT[:], c.dram["ctxT"][ds(b, 1)].rearrange("a p c s -> (a p) c s")).then_inc(ctx_loaded, 16)
                if masked:
                    sp.wait_ge(mask_ready, b + FREE)
                    sp.dma_start(mask8[:], c.dram["mask"][ds(b, 1)].rearrange("a t p s -> (a p) t s")).then_inc(mask_loaded, 16)
                with sp.Fori(0, SN // WB) as i:
                    for k in range(WB):
                        sp.wait_ge(proj_ready, (b * SN + i * WB) * NP + ((k + 1 - WB) * NP + WAHEAD))
                        sp.dma_start(wqk[:, k], c.dram[f"{name}_wqk"][ds(i * WB + k, 1)].rearrange("a p e c m -> (a p) e c m")
                                     ).then_inc(w_loaded[k], 16)

        @block.scalar
        def _(act):
            act.wait_ge(loaded, LOADS)
            with act.Fori(0, B) as b:
                def high(gr, hh, n, bank):
                    stack, col = ((b * NG + gr) * HPG + hh, gr * HPG + hh) if wide_heads else (b * NG + gr, gr)
                    act.wait_ge(proj_ready, stack * NP + (n + 1 + WAHEAD))
                    seen(act)
                    k0, w = chunk(n)
                    dst = (K[:, hh % 2 if wide_heads else gr, k0:k0 + w] if n else
                           Q[:, hh % 2, 0, :] if wide_heads else qf[:, gr, :])
                    nc.scalar.activation(dst, bank[:, 0:w], ACT.Identity, bias=bqk[:, min(n, 1), ds(col, 1)]).then_inc(proj_hi, 1)

                def head_rows(gr, hh):
                    nc.scalar.activation(Q[:, hh % 2, 0, :], qf[:, ds(gr, 1), :].rearrange("p a t -> p (a t)"), ACT.Copy,
                                         scale=member[:, hh:hh + 1]).then_inc(q_hi, 1)

                def exps(gr, u):
                    e = u % 2
                    act.wait_ge(neg_ready, (b * NG + gr) * UN + (u + 1))
                    nc.scalar.activation(prob[:, e, :], prob[:, e, :], ACT.Exp, bias=neg[:, e:e + 1], scale=SCALE,
                                         accum_out=total[:, e:e + 1]).then_inc(p_ready, 1)

                def group(gr, last):
                    turn = b * NG + gr

                    def turned_high(u, g):
                        k0, k1 = G4[g]
                        act.wait_ge(t_ready, (turn * UN + u) * GN + (g + 1))
                        if u >= 2 * NPT and u % 2 == 0 and g == 0:
                            act.wait_ge(pv_ready, turn * PAIRS + (u // 2 + 1 - NPT))
                        n = keys(k1 - 1) if k1 - k0 == 1 else P
                        nc.scalar.activation(PT[0:n, u // 2 % NPT, 0, k0:k1, u % 2, :], turned_bank(u, g)[0:n, 0:k1 - k0, :], ACT.Copy
                                             ).then_inc(t_hi, 1)

                    def spread_share(pair):
                        act.wait_ge(pv_ready, turn * PAIRS + (pair + 1))
                        nc.scalar.activation(share[:], pv[0:MV, 2 * P:4 * P], ACT.Copy).then_inc(share_ready, 1)

                    act.wait_ge(v_copied, (turn if wide_heads else b) * KT + KT)
                    seen(act)
                    for heads, cols in value_parts(gr):
                        nc.scalar.activation(V[:, :, heads, 0, :], Vf[:, :, cols].rearrange("p k (h d) -> p k h d", d=dk), ACT.Copy
                                             ).then_inc(v_hi, 1)
                    for u in range(UN):
                        hh, q = divmod(u, TB)
                        nxt = following(gr, u, last)

                        def beside(place):
                            if (q, place) in NEXT and next_head(gr, hh, last):
                                high(*next_head(gr, hh, last), NEXT[q, place], bank_of(NEXT[q, place]))

                        first = wide_heads and behind(u) is not None
                        if behind(u) is not None and not wide_heads:
                            spread_share(behind(u))
                        beside("A")
                        if first and nxt:
                            exps(*nxt)
                        turned_high(u, 0)
                        turned_high(u, 1)
                        if nxt and not first:
                            exps(*nxt)
                        beside("B")
                        turned_high(u, 2)
                        turned_high(u, 3)
                        beside("C")
                        if behind(u) is not None and wide_heads:
                            spread_share(behind(u))
                        if not wide_heads and q == 0 and next_head(gr, hh, last):
                            head_rows(*next_head(gr, hh, last))
                    for pair in range(PAIRS - NPT, PAIRS):
                        spread_share(pair)

                if wide_heads:
                    for n in range(NP):
                        high(0, 0, n, proj)
                else:
                    for m in range(NG * NP):
                        high(m // NP, 0, m % NP, banks[m % 3])
                    act.wait_ge(proj_hi, b * (NG * NP) + NG * NP)
                    seen(act)
                    head_rows(0, 0)
                exps(0, 0)
                by_groups(act, group)

        @block.vector
        def _(dve):
            nc.vector.memset(K[:].bitcast(F32), 0.0).then_inc(pad_ready, 1)
            nc.vector.memset(Vf[:, KT - 1, :], 0.0).then_inc(pad_ready, 1)
            if not masked:
                nc.vector.memset(mask[:], 0.0).then_inc(pad_ready, 1)
                dve.wait_ge(pad_ready, 3)
                nc.vector.memset(mask[:, 0, S2:], NEG).then_inc(pad_ready, 1)
            dve.wait_ge(pad_ready, PADS)
            dve.wait_ge(loaded, LOADS)
            with dve.Fori(0, B) as b:
                xb = c.x[:, ds(b * TB, TB), :]
                nc.vector.tensor_tensor(xb, xb, bo[:].unsqueeze(1).broadcast_to([P, TB, D]), ALU.add).then_inc(based, 1)
                dve.wait_ge(based, b + 1)
                seen(dve)
                if masked:
                    dve.wait_ge(mask_loaded, b * 16 + 16)
                    nc.vector.tensor_scalar(mask[:], mask8[:].bitcast(U8), NEG, None, ALU.mult).then_inc(mask_ready, 1)
                    dve.wait_ge(mask_ready, b + (1 + FREE))
                    seen(dve)

                def copy_values(gr, kt, bank):
                    n = keys(kt)
                    col = gr * VW if wide_heads else 0
                    dve.wait_ge(v_ready, (b * NG + gr if wide_heads else b) * KT + (kt + 1))
                    nc.vector.tensor_tensor(Vf[0:n, kt, :], bank[0:n, 0:VW], bv[0:n, ds(col, VW)], ALU.add).then_inc(v_copied, 1)

                def low(gr, hh, n, bank):
                    stack, col = ((b * NG + gr) * HPG + hh, gr * HPG + hh) if wide_heads else (b * NG + gr, gr)
                    k0, w = chunk(n)
                    dve.wait_ge(proj_hi, stack * NP + (n + 1))
                    if n == 0 and not wide_heads:
                        if gr >= 1:
                            dve.wait_ge(proj_lo, stack * NP)
                        dve.sem_inc(proj_lo, 1)
                        return
                    if n == 0:
                        rows, hi, lo = slice(0, P), Q[:, hh % 2, 0, :], Q[:, hh % 2, 1, :]
                    else:
                        rows = slice(P // 2, P)
                        hi = lo = K[rows, hh % 2 if wide_heads else gr, k0:k0 + w]
                    nc.vector.scalar_tensor_tensor(out=lo, in0=bank[rows, 0:w], scalar=bqk[rows, min(n, 1), ds(col, 1)],
                                                   in1=hi.bitcast(F32), op0=ALU.add, op1=ALU.subtract).then_inc(proj_lo, 1)

                def head_rows(gr, hh):
                    dve.wait_ge(q_hi, (b * NG + gr) * HPG + (hh + 1))
                    seen(dve)
                    nc.vector.scalar_tensor_tensor(out=Q[:, hh % 2, 1, :], in0=qf[:, ds(gr, 1), :].rearrange("p a t -> p (a t)"),
                                                   scalar=member[:, hh:hh + 1], in1=Q[:, hh % 2, 0, :].bitcast(F32),
                                                   op0=ALU.mult, op1=ALU.subtract).then_inc(q_lo, 1)

                def row_max(gr, u):
                    e = u % 2
                    at = (b * NG + gr) * UN + (u + 1)
                    dve.wait_ge(s_ready, at)
                    seen(dve)
                    parts = lambda v: v.rearrange("p (n k) -> p n k", k=SW)
                    nc.vector.tensor_tensor_reduce(parts(prob[:, e, :]), sps[:, :, 0:SW], parts(mask[:, u % TB if masked else 0, :]),
                                                   1.0, -3.0e38, ALU.add, ALU.max, mx[:, e:e + 1]).then_inc(max_ready, 1)
                    dve.wait_ge(max_ready, at)
                    nc.vector.tensor_scalar(neg[:, e:e + 1], mx[:, e:e + 1], -SCALE, None, ALU.mult).then_inc(neg_ready, 1)

                def group(gr, last):
                    turn = b * NG + gr

                    def turned_low(u, g):
                        k0, k1 = G4[g]
                        dve.wait_ge(t_hi, (turn * UN + u) * GN + (g + 1))
                        n = keys(k1 - 1) if k1 - k0 == 1 else P
                        nc.vector.tensor_tensor(PT[0:n, u // 2 % NPT, 1, k0:k1, u % 2, :], turned_bank(u, g)[0:n, 0:k1 - k0, :],
                                                PT[0:n, u // 2 % NPT, 0, k0:k1, u % 2, :].bitcast(F32), ALU.subtract
                                                ).then_inc(t_lo, 1)

                    def shares(u):
                        e = u % 2
                        dve.wait_ge(p_ready, turn * UN + (u + 1))
                        nc.vector.reciprocal(rtotal[:, e:e + 1], total[:, e:e + 1]).then_inc(inv_ready, 1)
                        dve.wait_ge(inv_ready, turn * UN + (u + 1))
                        nc.vector.tensor_scalar(diag[:, u // 2 % 2, e, :], c.ident[:], rtotal[:, e:e + 1], None, ALU.mult
                                                ).then_inc(diag_ready, 1)

                    def scale_output(pair):
                        hh, half = divmod(pair, 2)
                        dve.wait_ge(share_ready, turn * PAIRS + (pair + 1))
                        nc.vector.tensor_tensor(attT[:, hh, half * 2 * P:(half + 1) * 2 * P], pv[0:MV, 0:2 * P], share[:],
                                                ALU.mult).then_inc(att_ready, 1)

                    def add_output(number, half):
                        rows = c.x[:, ds(b * TB + half * (TB // 2), TB // 2), :]
                        dve.wait_ge(out_ready, turn * OUTS + (number + 1))
                        nc.vector.tensor_tensor(rows, rows, half_bank(half)[:].rearrange("p (t d) -> p t d", d=D), ALU.add
                                                ).then_inc(added, 1)

                    def low_values():
                        for n, (heads, cols) in enumerate(value_parts(gr)):
                            dve.wait_ge(v_hi, turn * VP + (n + 1))
                            seen(dve)
                            nc.vector.tensor_tensor(V[:, :, heads, 1, :], Vf[:, :, cols].rearrange("p k (h d) -> p k h d", d=dk),
                                                    V[:, :, heads, 0, :].bitcast(F32), ALU.subtract).then_inc(v_lo, 1)
                        if wide_heads:
                            dve.wait_ge(v_lo, turn * VP + VP)
                            seen(dve)

                    if not wide_heads:
                        low_values()
                    for u in range(UN):
                        hh, q = divmod(u, TB)
                        nxt = following(gr, u, last)

                        def beside(place):
                            if (q, place) in NEXT and next_head(gr, hh, last):
                                low(*next_head(gr, hh, last), NEXT[q, place], bank_of(NEXT[q, place]))
                            if hh >= 1 and (q, place) in OUT:
                                add_output((hh - 1) * 2 + OUT[q, place], OUT[q, place])
                            if (hh, q, place) in VALUES and not last:
                                copy_values(gr + 1, VALUES[hh, q, place], proj)

                        if behind(u) is not None and not wide_heads:
                            scale_output(behind(u))
                        if nxt:
                            row_max(*nxt)
                        shares(u)
                        beside("A")
                        turned_low(u, 0)
                        turned_low(u, 1)
                        beside("B")
                        turned_low(u, 2)
                        turned_low(u, 3)
                        if u == 0 and wide_heads:
                            low_values()
                        beside("C")
                        if behind(u) is not None and wide_heads:
                            scale_output(behind(u))
                        if not wide_heads and q == 0 and next_head(gr, hh, last):
                            head_rows(*next_head(gr, hh, last))
                    for pair in range(PAIRS - NPT, PAIRS):
                        scale_output(pair)
                    for half in range(2):
                        add_output(OUTS - 2 + half, half)

                if wide_heads:
                    done = 0
                    for n in range(NP):
                        low(0, 0, n, proj)
                        upto = KT * (n + 1) // NP
                        for kt in range(done, upto):
                            copy_values(0, kt, flat[kt % 2])
                        done = upto
                else:
                    for kt in range(KT):
                        copy_values(0, kt, flat[kt % 2])
                    for m in range(NG * NP):
                        low(m // NP, 0, m % NP, banks[m % 3])
                    head_rows(0, 0)
                row_max(0, 0)
                by_groups(dve, group)

        @block.tensor
        def _(pe):
            for sem, n in ((proj_ready, WAHEAD), (mask_ready, FREE), (added, START)):
                pe.sem_inc(sem, n)
            pe.wait_ge(loaded, LOADS)
            pe.wait_ge(pad_ready, PADS)
            with pe.Fori(0, B) as b:
                pe.wait_ge(ctx_loaded, b * 16 + 16)
                seen(pe)

                def values(gr, kt, bank):
                    n = keys(kt)
                    col = gr * VW if wide_heads else 0
                    for k in range(DC):
                        last = nc.tensor.matmul(bank[0:n, 0:VW], ctxT[:, k, kt * P:kt * P + n], wv[:, k, ds(col, VW)],
                                                start=(k == 0), stop=(k == DC - 1))
                    last.then_inc(v_ready, 1)

                def project(gr, hh, n, bank):
                    stack = (b * NG + gr) * HPG + hh if wide_heads else b * NG + gr
                    buf = 0 if wide_heads else gr % WB
                    if n == 0:
                        loads = stack * 16 + 16 if wide_heads else b * (NG // WB * 16) + (gr // WB * 16 + 16)
                        pe.wait_ge(w_loaded[buf], loads)
                        seen(pe)
                    k0, w = chunk(n)
                    for k in range(DC):
                        rhs = c.xnT[:, k, ds(b * T, T)] if n == 0 else ctxT[:, k, k0:k0 + w]
                        last = nc.tensor.matmul(bank[:, 0:w], wqk[:, buf, min(n, 1), k, :], rhs,
                                                start=(k == 0), stop=(k == DC - 1))
                    last.then_inc(proj_ready, 1)

                def scores(gr, u):
                    hh, q = divmod(u, TB)
                    turn = b * NG + gr
                    if q == 0 and wide_heads:
                        pe.wait_ge(proj_lo, (turn * HPG + hh) * NP + NP)
                    if q == 0 and not wide_heads:
                        pe.wait_ge(q_lo, turn * HPG + (hh + 1))
                    if u >= 1 or not isinstance(gr, int):
                        pe.wait_ge(max_ready, turn * UN + u)
                    seen(pe)
                    for n in range(4):
                        for e in range(2):
                            k = K[:, hh % 2, n * SW:n * SW + SWW] if wide_heads else K[:, ds(gr, 1), n * SW:n * SW + SWW].rearrange(
                                "p a k -> p (a k)")
                            last = nc.tensor.matmul(sps[:, n, 0:SWW], Q[:, hh % 2, e, q * P:(q + 1) * P], k,
                                                    start=(e == 0), stop=(e == 1))
                    last.then_inc(s_ready, 1)

                def group(gr, last_group):
                    turn = b * NG + gr

                    def turned(u, g):
                        k0, k1 = G4[g]
                        if g == 0:
                            pe.wait_ge(p_ready, turn * UN + (u + 1))
                        if u * GN + g >= TBANKS:
                            pe.wait_ge(t_lo, (turn * UN + u) * GN + (g + 1 - TBANKS))
                        elif g == 2:
                            pe.wait_ge(added, turn * OUTS + (START - 1))
                        for kt in range(k0, k1):
                            n = keys(kt)
                            last = nc.tensor.transpose(turned_bank(u, g)[0:n, kt - k0, :], prob[:, u % 2, kt * P:kt * P + n], c.ident[:])
                        last.then_inc(t_ready, 1)

                    def output(pair, kts, halves=0):
                        hh = pair // 2
                        if kts[0] == 0:
                            pe.wait_ge(added, turn * OUTS + (halves + START))
                            pe.wait_ge(t_lo, (turn * UN + 2 * pair + 2) * GN)
                            pe.wait_ge(diag_ready, turn * UN + (2 * pair + 2))
                            if pair == 0:
                                pe.wait_ge(v_lo, turn * VP + VP)
                            else:
                                pe.wait_ge(att_ready, turn * PAIRS + pair)
                        for kt in kts:
                            n = keys(kt)
                            for part in range(2):
                                nc.tensor.matmul(pv[0:MV, 0:2 * P], V[0:n, kt, hh].rearrange("p e d -> p (e d)"),
                                                 PT[0:n, pair % NPT, part, kt].rearrange("p a q -> p (a q)"),
                                                 start=(kt == 0 and part == 0), stop=(kt == KT - 1 and part == 1))
                        if kts[-1] == KT - 1:
                            nc.tensor.matmul(pv[0:MV, 2 * P:4 * P], c.ones[:, 0:MV],
                                             diag[:, pair % 2].rearrange("p a q -> p (a q)"),
                                             start=True, stop=True).then_inc(pv_ready, 1)

                    def out_product(number, half, members, tiles, pairs):
                        pe.wait_ge(added, turn * OUTS + (number - half + START))
                        if tiles and not half and not last_group:
                            pe.wait_ge(v_copied, (turn + 1) * KT + tiles)
                        pe.wait_ge(att_ready, turn * PAIRS + pairs)
                        seen(pe)
                        for t in range(TB // 2):
                            at = half * (TB // 2) + t
                            for hh in members:
                                last = nc.tensor.matmul(half_bank(half)[:, t * D:(t + 1) * D], attT[:, hh, at * P:(at + 1) * P],
                                                        wo[:, ds(gr * HPG + hh, 1), :].rearrange("p a d -> p (a d)"),
                                                        start=(hh == members[0]), stop=(hh == members[-1]))
                        last.then_inc(out_ready, 1)

                    for u in range(UN):
                        hh, q = divmod(u, TB)
                        nxt = following(gr, u, last_group)

                        def beside(place):
                            stack = (turn * HPG + hh + 1) * NP
                            if (hh, q, place) in VALUES and not last_group:
                                kt = VALUES[hh, q, place]
                                if kt:
                                    pe.wait_ge(v_copied, (turn + 1) * KT + kt)
                                if (q, place) == (3, "C") and hh:
                                    pe.wait_ge(added, turn * OUTS + (2 * hh - 1 + START))
                                if (q, place) == (0, "C"):
                                    pe.wait_ge(proj_lo, stack + 1)
                                if (q, place) == (2, "B"):
                                    pe.wait_ge(proj_lo, stack + 5)
                                seen(pe)
                                values(gr + 1, kt, proj)
                            if (q, place) in NEXT and next_head(gr, hh, last_group):
                                n = NEXT[q, place]
                                if n == 0:
                                    if not last_group and hh:
                                        pe.wait_ge(v_copied, (turn + 1) * KT + (VALUES[hh, 0, "A"] + 1))
                                    pe.wait_ge(added, turn * OUTS + (2 * max(hh - 1, 0) + START))
                                elif n == 2:
                                    pe.wait_ge(att_ready, turn * PAIRS + 2 * hh)
                                else:
                                    pe.wait_ge(proj_lo, stack + (n if n != 3 else 2))
                                    if n == 1 and not hh and not last_group:
                                        pe.wait_ge(v_copied, (turn + 1) * KT + 1)
                                seen(pe)
                                project(*next_head(gr, hh, last_group), n, bank_of(n))
                            if wide_heads and place == "A" and q % 2 == 0 and u >= 2:
                                if q == 2 and next_head(gr, hh, last_group):
                                    pe.wait_ge(proj_lo, stack + 3)
                                output(u // 2 - 1, range(KT), 2 * max(hh - 1, 0))
                            if not wide_heads and place != "C" and u >= 2:
                                n = u % 2 * 2 + (place == "B")
                                output(u // 2 - 1, range(KT * n // 4, KT * (n + 1) // 4))
                            if hh >= 1 and (q, place) in OUT:
                                half = OUT[q, place]
                                out_product((hh - 1) * 2 + half, half, [hh - 1], VALUES.get((hh, 2, "B"), -1) + 1, 2 * hh + half)

                        if nxt:
                            scores(*nxt)
                        beside("A")
                        turned(u, 0)
                        turned(u, 1)
                        beside("B")
                        turned(u, 2)
                        turned(u, 3)
                        beside("C")
                    output(PAIRS - 1, range(KT), OUTS - 2)
                    for half in range(2):
                        out_product(OUTS - 2 + half, half, [HPG - 1] if wide_heads else list(range(HPG)), KT if wide_heads else 0,
                                    PAIRS)

                pe.wait_ge(added, b * (NG * OUTS) + START)
                seen(pe)
                if wide_heads:
                    done = 0
                    for n in range(NP):
                        if n >= 1:
                            pe.wait_ge(proj_lo, b * (SN * NP) + n)
                            seen(pe)
                        project(0, 0, n, proj)
                        upto = KT * (n + 1) // NP
                        for kt in range(done, upto):
                            if kt >= 2:
                                pe.wait_ge(v_copied, b * (NG * KT) + (kt - 1))
                                seen(pe)
                            values(0, kt, flat[kt % 2])
                        done = upto
                    pe.wait_ge(v_copied, b * (NG * KT) + KT)
                    pe.wait_ge(proj_lo, b * (SN * NP) + NP)
                else:
                    for kt in range(KT):
                        if kt >= 2:
                            pe.wait_ge(v_copied, b * KT + (kt - 1))
                            seen(pe)
                        values(0, kt, flat[kt % 2])
                    pe.wait_ge(v_copied, b * KT + KT)
                    seen(pe)
                    for m in range(NG * NP):
                        if m >= 3:
                            pe.wait_ge(proj_lo, b * (NG * NP) + (m - 2))
                            seen(pe)
                        project(m // NP, 0, m % NP, banks[m % 3])
                    pe.wait_ge(proj_lo, b * (NG * NP) + NG * NP)
                seen(pe)
                scores(0, 0)
                by_groups(pe, group)


DH = 1024
MH = DH // P


def lay_ternary_mlp(a, rows, cols):
    g = lambda n: a["L0_ffn_" + n]
    o = {f"ffn_{n}": rows(g(n + "_w").T) for n in ("w1", "w2", "h1", "h2", "w3")}
    o.update({f"ffn_{n}_s": cols(g(n + "_s")) for n in ("w1", "w2", "h1", "h2")})
    o["ffn_w3_s"] = g("w3_s")
    return o


def ternary_mlp(nc, c):
    layernorm(nc, c, "ffn_ln", c.x, c.xnT)
    NB = B * T // 512
    NT4 = 512 // P
    with Scope(nc, "ffn") as s:
        names = ("w1", "w2", "h1", "h2", "w3")
        w = {n: s.sb(n, list(c.dram[f"ffn_{n}"].shape)) for n in names}
        sc = {n: s.sb(n + "_s", [P, MH]) for n in names[:4]}
        w3_s = s.sb("w3_s", [P, D])
        gate = s.sb("gate", [P, 2, 512])
        hid = [s.sb(f"hid{k}", [P, MH, 512]) for k in range(3)]
        scaled = s.sb("scaled", [P, 2, D])
        up = [s.ps(f"up{k}", [P, 512]) for k in range(2)]
        lin = [s.ps(f"lin{k}", [P, 512]) for k in range(2)]
        mid = [s.ps(f"mid{k}", [P, 512]) for k in range(2)]
        low = [s.ps(f"low{k}", [P, 512]) for k in range(2)]
        loaded = {n: s.sem(n + "_loaded") for n in names}
        scales = s.sem("scales")
        up_ready = s.sem("up_ready")
        gate_ready = s.sem("gate_ready")
        hid_ready = s.sem("hid_ready")
        mid_ready = [s.sem(f"mid_ready{k}") for k in range(2)]
        act_ready = [s.sem(f"act_ready{k}") for k in range(2)]
        out_ready = s.sem("out_ready")
        scaled_ready = s.sem("scaled_ready")
        added = s.sem("added")
        block = s.block()
        SCALES = 5 * 16

        @block.sync
        def _(sp):
            for n in ("w1", "w2", "h1", "h2"):
                sp.dma_start(sc[n][:], c.dram[f"ffn_{n}_s"]).then_inc(scales, 16)
            sp.dma_start(w3_s[:], c.dram["ffn_w3_s"].partition_broadcast(P)).then_inc(scales, 16)
            for n in names:
                sp.dma_start(w[n][:], c.dram[f"ffn_{n}"]).then_inc(loaded[n], 16)

        @block.scalar
        def _(act):
            act.wait_ge(scales, SCALES)
            with act.Fori(0, NB) as i:
                for m in range(MH):
                    act.wait_ge(up_ready, i * MH + (m + 1))
                    if m >= 2:
                        act.wait_ge(hid_ready, i * MH + (m - 1))
                    nc.scalar.activation(gate[:, m % 2, :], up[m % 2][:], ACT.Silu, scale=sc["w1"][:, m:m + 1]
                                         ).then_inc(gate_ready, 1)
                for k, n in enumerate(("h1", "h2")):
                    for m in range(MH):
                        act.wait_ge(mid_ready[k], i * MH + (m + 1))
                        nc.scalar.activation(hid[1 + k][:, m, :], mid[m % 2][:], ACT.Gelu, scale=sc[n][:, m:m + 1]
                                             ).then_inc(act_ready[k], 1)

        @block.vector
        def _(dve):
            dve.wait_ge(scales, SCALES)
            with dve.Fori(0, NB) as i:
                for m in range(MH):
                    dve.wait_ge(gate_ready, i * MH + (m + 1))
                    nc.vector.scalar_tensor_tensor(out=hid[0][:, m, :], in0=lin[m % 2][:], scalar=sc["w2"][:, m:m + 1],
                                                   in1=gate[:, m % 2, :], op0=ALU.mult, op1=ALU.mult
                                                   ).then_inc(hid_ready, 1)
                for t in range(NT4):
                    row = c.x[:, ds(i * NT4 + t, 1), :].rearrange("p a d -> p (a d)")
                    dve.wait_ge(out_ready, i * NT4 + (t + 1))
                    nc.vector.tensor_tensor(scaled[:, t % 2, :], low[t % 2][:, 0:D], w3_s[:], ALU.mult
                                            ).then_inc(scaled_ready, 1)
                    dve.wait_ge(scaled_ready, i * NT4 + (t + 1))
                    nc.vector.tensor_tensor(row, row, scaled[:, t % 2, :], ALU.add).then_inc(added, 1)

        @block.tensor
        def _(pe):
            with pe.Fori(0, NB) as i:
                pe.wait_ge(loaded["w1"], 16)
                pe.wait_ge(loaded["w2"], 16)
                for m in range(MH):
                    if m >= 2:
                        pe.wait_ge(hid_ready, i * MH + (m - 1))
                    for dst, n in ((lin, "w2"), (up, "w1")):
                        for k in range(DC):
                            last = nc.tensor.matmul(dst[m % 2][:], w[n][:, k, m * P:(m + 1) * P], c.xnT[:, k, ds(i * 512, 512)],
                                                    start=(k == 0), stop=(k == DC - 1))
                    last.then_inc(up_ready, 1)
                for e, n in enumerate(("h1", "h2")):
                    pe.wait_ge(loaded[n], 16)
                    pe.wait_ge(hid_ready if e == 0 else act_ready[0], i * MH + MH)
                    for m in range(MH):
                        if e == 1 and m < 2:
                            pass
                        elif m >= 2:
                            pe.wait_ge(act_ready[e], i * MH + (m - 1))
                        for k in range(MH):
                            last = nc.tensor.matmul(mid[m % 2][:], w[n][:, k, m * P:(m + 1) * P], hid[e][:, k, :],
                                                    start=(k == 0), stop=(k == MH - 1))
                        last.then_inc(mid_ready[e], 1)
                pe.wait_ge(loaded["w3"], 16)
                pe.wait_ge(act_ready[1], i * MH + MH)
                for t in range(NT4):
                    if t >= 2:
                        pe.wait_ge(added, i * NT4 + (t - 1))
                    for k in range(MH):
                        last = nc.tensor.matmul(low[t % 2][:, 0:D], hid[2][:, k, t * P:(t + 1) * P], w["w3"][:, k, :],
                                                start=(k == 0), stop=(k == MH - 1))
                    last.then_inc(out_ready, 1)


CH = 2 * D
CC = CH // P
NS, RANK = 16, D // 16
DBC = RANK + 2 * NS
LOW = 64
SOL = 0.1
TWO_PI_HIGH = 6.28125
TWO_PI_LOW = 2 * np.pi - TWO_PI_HIGH
TO_WHOLE = 1.5 * 2.0 ** 23
PI = 3.1415925


def lay_selective_scan(a, rows, cols):
    g = lambda n: a["L1_attn_" + n]
    gap = np.zeros((CH, LOW - DBC), np.float32)
    pick = np.zeros((LOW + DBC, NS, 2, P), np.float32)
    for n in range(NS):
        for e in range(2):
            row = RANK + e * NS + n
            pick[[row, LOW + row], n, e] = 1
    per_head = lambda v: cols(np.repeat(v, D // v.shape[0]))
    return {
        "scan_ln": np.stack([cols(g(n)) for n in ("ln1_g", "ln1_b", "ln2_g", "ln2_b")], 1),
        "scan_win": rows(g("W_in")), "scan_bin": cols(g("b_in")),
        "scan_conv": g("conv_w").reshape(CC, P, CONV).transpose(1, 0, 2), "scan_conv_b": cols(g("conv_b")),
        "scan_wxp": rows(np.concatenate([g("W_xp"), gap, g("W_xp")], 1)),
        "scan_wdt": g("W_dt"), "scan_bdt": cols(g("b_dt")),
        "scan_A_log": g("A_log").reshape(CC, P, NS).transpose(1, 0, 2),
        "scan_skip": cols(g("D_skip")),
        "scan_wout": rows(g("W_out")), "scan_bout": g("b_out"),
        "scan_pick": pick,
        "wave_wsi": rows(g("W_si")), "wave_bsi": cols(g("b_si")),
        "wave_gates": np.stack([per_head(g("gates")[:, k]) for k in range(3)], 1),
        "wave_alpha": per_head(g("alpha")),
        "wave_wso": rows(g("W_so")), "wave_bso": g("b_so"),
    }


def selective_scan(nc, c):
    with Scope(nc, "ss") as s:
        ln = s.sb("ln", [P, 4, DC])
        xa = s.sb("xa", [P, NT, D])
        load_norms(nc, c, ln)
        layernorm(nc, c, "ss_ln0", c.x, c.xnT, keep=xa)
        layernorm(nc, c, "ss_ln1", xa, c.xnT, gain=ln[:, 0, :], shift=ln[:, 1, :])
        scan_channels(nc, c, xa)
        layernorm(nc, c, "ss_ln2", xa, c.xnT, gain=ln[:, 2, :], shift=ln[:, 3, :])
        waves(nc, c, xa)


def load_norms(nc, c, ln):
    with Scope(nc, "ss_norms") as s:
        loaded = s.sem("loaded")
        block = s.block()

        @block.sync
        def _(sp):
            sp.dma_start(ln[:], c.dram["scan_ln"]).then_inc(loaded, 16)
            sp.wait_ge(loaded, 16)


def scan_channels(nc, c, xa):
    with Scope(nc, "scan") as s:
        win = s.sb("win", [P, DC, 2 * CH])
        b_in = s.sb("bin", [P, 2 * CC])
        convw = s.sb("convw", [P, CC, CONV])
        conv_b = s.sb("conv_b", [P, CC])
        wxp = s.sb("wxp", [P, CC, LOW + DBC])
        wdt = s.sb("wdt", [RANK, CH])
        b_dt = s.sb("bdt", [P, CC])
        neg_a = s.sb("neg_a", [P, CC, NS])
        skip = s.sb("skip", [P, CC])
        wout = s.sb("wout", [P, CC, D])
        b_out = s.sb("bout", [P, D])
        pick = s.sb("pick", [LOW + DBC, NS, 2, P])
        xp = s.sb("xp", [P, 2, T])
        conv = s.sb("conv", [P, 2, T])
        xc = s.sb("xc", [P, CC, T])
        zs = s.sb("zs", [P, CC, T])
        whole = s.sb("whole", [LOW + DBC, T], F32R)
        parts = s.sb("parts", [LOW + DBC, T], F32R)
        low_rank = s.sb("low_rank", [RANK, T])
        v = s.sb("v", [P, CC, T])
        dt = s.sb("dt", [P, CC, T])
        dtx = s.sb("dtx", [P, CC, T])
        picked = s.sb("picked", [LOW + DBC, 2, 2, P], F32R)
        Bs = s.sb("Bs", [P, 2, T])
        dA = s.sb("dA", [P, 2, CC, T])
        dBx = s.sb("dBx", [P, 2, CC, T])
        h = s.sb("h", [P, CC, T])
        hC = s.sb("hC", [P, 2, CC, T])
        e1, e2 = dA[:, 0], dBx[:, 0]
        gated = dBx[:, 1]
        y_ps = [s.ps(f"y{k}", [P, T]) for k in range(CC)]
        B_ps = [s.ps(f"B{k}", [P, T]) for k in range(2)]
        C_ps = [s.ps(f"C{k}", [P, T]) for k in range(2)]

        loaded = s.sem("loaded")
        ready0 = s.sem("ready0")
        proj_ready = s.sem("proj_ready")
        xp_ready = s.sem("xp_ready")
        conv_ready = s.sem("conv_ready")
        xc_ready = s.sem("xc_ready")
        z_ready = s.sem("z_ready")
        dbc_ready = s.sem("dbc_ready")
        whole_ready = s.sem("whole_ready")
        parts_ready = s.sem("parts_ready")
        rank_ready = s.sem("rank_ready")
        step_ready = s.sem("step_ready")
        v_ready = s.sem("v_ready")
        w_ready = s.sem("w_ready")
        log_ready = s.sem("log_ready")
        exp_ready = s.sem("exp_ready")
        dt_ready = s.sem("dt_ready")
        dtx_ready = s.sem("dtx_ready")
        skip_ready = s.sem("skip_ready")
        zero_ready = s.sem("zero_ready")
        pick_ready = s.sem("pick_ready")
        B_spread = s.sem("B_spread")
        C_spread = s.sem("C_spread")
        B_ready = s.sem("B_ready")
        dA_ready = s.sem("dA_ready")
        dBx_ready = s.sem("dBx_ready")
        scanned = s.sem("scanned")
        hC_ready = s.sem("hC_ready")
        summed = s.sem("summed")
        gated_ready = s.sem("gated_ready")
        out_ready = s.sem("out_ready")
        added = s.sem("added")
        vec = s.sem("vec")
        act_a = s.sem("act_a")
        meet = s.sem("meet")
        passed = s.sem("passed")
        block = s.block()
        LOADS = 12 * 16
        WORKERS = 4
        START = 1
        FREE = 2

        def sequence_end(eng, b):
            eng.drain().then_inc(meet, 1)
            eng.wait_ge(meet, b * WORKERS + WORKERS)
            eng.sem_inc(passed, 1)

        @block.sync
        def _(sp):
            for dst, src in ((win, "win"), (b_in, "bin"), (convw, "conv"), (conv_b, "conv_b"), (wxp, "wxp"), (wdt, "wdt"),
                             (b_dt, "bdt"), (neg_a, "A_log"), (skip, "skip"), (wout, "wout"), (pick, "pick")):
                sp.dma_start(dst[:], c.dram[f"scan_{src}"]).then_inc(loaded, 16)
            sp.dma_start(b_out[:], c.dram["scan_bout"].partition_broadcast(P)).then_inc(loaded, 16)

        @block.gpsimd
        def _(pool):
            pool.wait_ge(loaded, LOADS)
            nc.gpsimd.tensor_tensor(xa[:], xa[:], b_out[:].unsqueeze(1).broadcast_to([P, NT, D]), ALU.add
                                    ).then_inc(ready0, 1)
            with pool.Fori(0, B) as b:
                pool.wait_ge(dt_ready, b + 1)
                pool.sem_inc(passed, 1)
                for k in range(2):
                    last = nc.gpsimd.memset(dA[:, k, :, 0:1], 0.0)
                last.then_inc(zero_ready, 1)
                pool.wait_ge(dtx_ready, b + 1)
                pool.sem_inc(passed, 1)
                with pool.Fori(0, NS // 2) as i:
                    for k in range(2):
                        turn = b * NS + i * 2
                        pool.wait_ge(B_ready, turn + (k + 1 + START))
                        pool.wait_ge(scanned, turn + (k + FREE - 1))
                        nc.gpsimd.tensor_tensor(dBx[:, k], dtx[:], Bs[:, k, :].unsqueeze(1).broadcast_to([P, CC, T]),
                                                ALU.mult).then_inc(dBx_ready, 1)
                sequence_end(pool, b)

        @block.scalar
        def _(act):
            act.wait_ge(loaded, LOADS)
            nc.scalar.activation(neg_a[:], neg_a[:], ACT.Exp).then_inc(ready0, 1)
            with act.Fori(0, B) as b:
                chain = Chain(act, act_a, per=1)
                chain.start(b)
                for m in range(CC):
                    act.wait_ge(proj_ready, b * (2 * CC) + (m + 1))
                    if m >= 2:
                        act.wait_ge(conv_ready, b * CC + (m - 1))
                    nc.scalar.activation(xp[:, m % 2, :], y_ps[m][:], ACT.Identity, bias=b_in[:, m:m + 1]
                                         ).then_inc(xp_ready, 1)
                    if m >= 1:
                        act.wait_ge(conv_ready, b * CC + m)
                        nc.scalar.activation(xc[:, m - 1, :], conv[:, (m - 1) % 2, :], ACT.Silu, bias=conv_b[:, m - 1:m]
                                             ).then_inc(xc_ready, 1)
                act.wait_ge(conv_ready, b * CC + CC)
                nc.scalar.activation(xc[:, CC - 1, :], conv[:, (CC - 1) % 2, :], ACT.Silu, bias=conv_b[:, CC - 1:CC]
                                     ).then_inc(xc_ready, 1)
                for m in range(CC):
                    act.wait_ge(proj_ready, b * (2 * CC) + (CC + m + 1))
                    nc.scalar.activation(zs[:, m, :], y_ps[m][:], ACT.Silu, bias=b_in[:, CC + m:CC + m + 1]
                                         ).then_inc(z_ready, 1)
                act.wait_ge(dbc_ready, b + 1)
                nc.scalar.activation(low_rank[:], B_ps[0][0:RANK, :], ACT.Copy).then_inc(rank_ready, 1)
                nc.scalar.activation(whole[:], B_ps[0][0:LOW + DBC, :], ACT.Copy).then_inc(whole_ready, 1)
                for m in range(CC):
                    act.wait_ge(step_ready, b * CC + (m + 1))
                    last = nc.scalar.activation(v[:, m, :], y_ps[m][:], ACT.Identity, bias=b_dt[:, m:m + 1])
                last.then_inc(v_ready, 1)
                act.wait_ge(v_ready, b + 1)
                chain.link(nc.scalar.activation(e1, v[:], ACT.Abs))
                nc.scalar.activation(e1, e1, ACT.Exp, scale=-1.0).then_inc(exp_ready, 1)
                act.wait_ge(w_ready, b + 1)
                nc.scalar.activation(dt[:], e2, ACT.Ln).then_inc(log_ready, 1)
                chain.close()

                def pick_rows(k, n, sync):
                    if sync is not None:
                        act.wait_ge(C_spread, sync + (1 + START))
                    nc.scalar.activation(picked[:, k], pick[:, ds(n, 1)].rearrange("p a e q -> p (a e) q"), ACT.Copy
                                         ).then_inc(pick_ready, 1)

                def spread_and_decay(k, n, turn):
                    act.wait_ge(B_spread, turn + (1 + START))
                    act.wait_ge(dBx_ready, turn + (FREE - 1))
                    nc.scalar.activation(Bs[:, k, :], B_ps[k][:], ACT.Copy).then_inc(B_ready, 1)
                    act.wait_ge(scanned, turn + (FREE - 1))
                    act.sem_inc(passed, 1)
                    for m in range(CC):
                        last = nc.scalar.activation(dA[:, k, m, 1:], dt[:, m, 1:], ACT.Exp, scale=neg_a[:, m, ds(n, 1)])
                    last.then_inc(dA_ready, 1)

                pick_rows(0, 0, None)
                pick_rows(1, 1, None)
                act.wait_ge(dt_ready, b + 1)
                act.sem_inc(passed, 1)
                with act.Fori(0, NS // 2 - 1) as i:
                    for k in range(2):
                        turn = b * NS + i * 2 + k
                        spread_and_decay(k, i * 2 + k, turn)
                        pick_rows(k, i * 2 + (k + 2), turn)
                for k in range(2):
                    spread_and_decay(k, NS - 2 + k, b * NS + (NS - 2 + k))
                sequence_end(act, b)

        @block.vector
        def _(dve):
            dve.sem_inc(scanned, FREE)
            dve.wait_ge(loaded, LOADS)
            dve.wait_ge(ready0, 2)
            nc.vector.tensor_scalar(neg_a[:], neg_a[:], -1.0, None, ALU.mult).then_inc(ready0, 1)
            dve.wait_ge(ready0, 3)
            with dve.Fori(0, B) as b:
                chain = Chain(dve, vec, per=CC * (CONV - 1) + 2)
                chain.start(b)
                for m in range(CC):
                    dve.wait_ge(xp_ready, b * CC + (m + 1))
                    if m >= 2:
                        dve.wait_ge(xc_ready, b * CC + (m - 1))
                    y, x = conv[:, m % 2, :], xp[:, m % 2, :]
                    chain.link(nc.vector.tensor_scalar(y, x, convw[:, m, CONV - 1:CONV], None, ALU.mult))
                    for back in range(1, CONV):
                        last = nc.vector.scalar_tensor_tensor(
                            out=y[:, back:], in0=x[:, :T - back], scalar=convw[:, m, CONV - 1 - back:CONV - back],
                            in1=y[:, back:], op0=ALU.mult, op1=ALU.add)
                        if back < CONV - 1:
                            chain.link(last)
                    last.then_inc(conv_ready, 1)
                dve.wait_ge(whole_ready, b + 1)
                nc.vector.tensor_copy(parts[0:LOW, :], whole[0:LOW, :])
                nc.vector.tensor_tensor(parts[LOW:, :], B_ps[0][LOW:LOW + DBC, :], whole[LOW:, :].bitcast(F32), ALU.subtract
                                        ).then_inc(parts_ready, 1)
                for m in range(CC):
                    last = nc.vector.tensor_scalar(hC[:, 1, m, :], xc[:, m, :], skip[:, m:m + 1], None, ALU.mult)
                last.then_inc(skip_ready, 1)
                dve.wait_ge(exp_ready, b + 1)
                nc.vector.tensor_scalar(e2, e1, 1.0, None, ALU.add).then_inc(w_ready, 1)
                dve.wait_ge(w_ready, b + 1)
                chain.link(nc.vector.scalar_tensor_tensor(out=e1, in0=e2, scalar=1.0, in1=e1, op0=ALU.subtract,
                                                          op1=ALU.subtract))
                chain.link(nc.vector.scalar_tensor_tensor(out=e1, in0=v[:], scalar=0.0, in1=e1, op0=ALU.max,
                                                          op1=ALU.subtract))
                dve.wait_ge(log_ready, b + 1)
                nc.vector.tensor_tensor(dt[:], dt[:], e1, ALU.add).then_inc(dt_ready, 1)
                dve.wait_ge(dt_ready, b + 1)
                nc.vector.tensor_tensor(dtx[:], dt[:], xc[:], ALU.mult).then_inc(dtx_ready, 1)
                dve.wait_ge(zero_ready, b + 1)
                dve.sem_inc(passed, 1)
                flat = lambda v: v.rearrange("p c t -> p (c t)")
                with dve.Fori(0, NS // 2) as i:
                    for k in range(2):
                        turn = b * NS + i * 2
                        dve.wait_ge(dA_ready, turn + (k + 1))
                        dve.wait_ge(dBx_ready, turn + (k + FREE + 1))
                        dve.wait_ge(hC_ready, turn + (k + START))
                        nc.vector.tensor_tensor_scan(flat(h[:]), flat(dA[:, k]), flat(dBx[:, k]), 0.0, ALU.mult, ALU.add
                                                     ).then_inc(scanned, 1)
                        dve.wait_ge(scanned, turn + (k + 1 + FREE))
                        dve.wait_ge(C_spread, turn + (k + 1 + START))
                        dve.wait_ge(summed, b * (NS + 1) + i * 2 + (k + START))
                        nc.vector.tensor_tensor(hC[:, k], h[:], C_ps[k][:].unsqueeze(1).broadcast_to([P, CC, T]), ALU.mult
                                                ).then_inc(hC_ready, 1)
                dve.wait_ge(summed, b * (NS + 1) + (NS + 1 + START))
                for m in range(CC):
                    last = nc.vector.tensor_tensor(gated[:, m, :], y_ps[m][:], zs[:, m, :], ALU.mult)
                last.then_inc(gated_ready, 1)
                for t in range(TB):
                    row = xa[:, ds(b * TB + t, 1), :].rearrange("p a d -> p (a d)")
                    dve.wait_ge(out_ready, b * TB + (t + 1))
                    nc.vector.tensor_tensor(row, row, B_ps[t % 2][:, 0:D], ALU.add).then_inc(added, 1)
                chain.close()
                sequence_end(dve, b)

        @block.tensor
        def _(pe):
            pe.sem_inc(dBx_ready, FREE)
            for sem in (B_ready, hC_ready, B_spread, C_spread, summed):
                pe.sem_inc(sem, START)
            pe.wait_ge(loaded, LOADS)
            with pe.Fori(0, B) as b:
                for m in range(2 * CC):
                    if m >= CC:
                        pe.wait_ge(xp_ready, b * CC + (m - CC + 1))
                    for k in range(DC):
                        last = nc.tensor.matmul(y_ps[m % CC][:], win[:, k, m * P:(m + 1) * P], c.xnT[:, k, ds(b * T, T)],
                                                start=(k == 0), stop=(k == DC - 1))
                    last.then_inc(proj_ready, 1)
                pe.wait_ge(xc_ready, b * CC + CC)
                for m in range(CC):
                    last = nc.tensor.matmul(B_ps[0][0:LOW + DBC, :], wxp[:, m, :], xc[:, m, :], start=(m == 0),
                                            stop=(m == CC - 1))
                last.then_inc(dbc_ready, 1)
                pe.wait_ge(rank_ready, b + 1)
                pe.wait_ge(z_ready, b * CC + CC)
                for m in range(CC):
                    nc.tensor.matmul(y_ps[m][:], wdt[:, m * P:(m + 1) * P], low_rank[:], start=True, stop=True
                                     ).then_inc(step_ready, 1)

                def spread(e, k, turn):
                    dst, sem = ((B_ps, B_spread), (C_ps, C_spread))[e]
                    pe.wait_ge(pick_ready, turn + 1)
                    pe.sem_inc(passed, 1)
                    nc.tensor.matmul(dst[k][:], picked[:, k, e, :], parts[:], start=True, stop=True).then_inc(sem, 1)

                def add_up(k, first):
                    for m in range(CC):
                        last = nc.tensor.matmul(y_ps[m][:], c.ident[:], hC[:, k, m, :], start=first, stop=True,
                                                skip_group_check=True)
                    last.then_inc(summed, 1)

                pe.wait_ge(parts_ready, b + 1)
                spread(0, 0, b * NS)
                spread(1, 0, b * NS)
                pe.wait_ge(v_ready, b + 1)
                pe.wait_ge(skip_ready, b + 1)
                add_up(1, True)
                pe.wait_ge(B_ready, b * NS + START)
                pe.wait_ge(hC_ready, b * NS + START)
                spread(0, 1, b * NS + 1)
                spread(1, 1, b * NS + 1)
                pe.wait_ge(B_ready, b * NS + (1 + START))
                spread(0, 0, b * NS + 2)

                def step(turn, k, last):
                    pe.wait_ge(hC_ready, turn + START)
                    spread(1, 1 - k, turn + 1)
                    if not last:
                        pe.wait_ge(B_ready, turn + (1 + START))
                        spread(0, k, turn + 2)
                    add_up(1 - k, False)

                with pe.Fori(0, NS // 2 - 2) as i:
                    for k in (1, 0):
                        step(b * NS + i * 2 + (2 - k), k, False)
                step(b * NS + (NS - 3), 1, False)
                step(b * NS + (NS - 2), 0, True)
                end = b * NS + (NS - 2)
                for k in range(2):
                    pe.wait_ge(hC_ready, end + (k + 1 + START))
                    add_up(k, False)
                pe.wait_ge(gated_ready, b + 1)
                for t in range(TB):
                    if t >= 2:
                        pe.wait_ge(added, b * TB + (t - 1))
                    for m in range(CC):
                        last = nc.tensor.matmul(B_ps[t % 2][:, 0:D], gated[:, m, t * P:(t + 1) * P], wout[:, m, :],
                                                start=(m == 0), stop=(m == CC - 1))
                    last.then_inc(out_ready, 1)
                sequence_end(pe, b)


def waves(nc, c, xa):
    EDGE = 2
    with Scope(nc, "wave") as s:
        wsi = s.sb("wsi", [P, DC, D])
        b_si = s.sb("bsi", [P, DC])
        gates = s.sb("gates", [P, 3, DC])
        alpha = s.sb("alpha", [P, DC])
        wso = s.sb("wso", [P, DC, D])
        b_so = s.sb("bso", [P, D])
        up = s.sb("up", [P, DC, T + 2 * EDGE])
        wide = lambda n: s.sb(n, [P, DC, T])
        turns, angle, sine, d1, d2, f, kdv, s1, heat, du = (
            wide(n) for n in ("turns", "angle", "sine", "d1", "d2", "f", "kdv", "s1", "heat", "du"))
        u_ps = [s.ps(f"u{k}", [P, T]) for k in range(DC)]
        out_ps = [s.ps(f"out{k}", [P, T]) for k in range(TB)]
        loaded = s.sem("loaded")
        ready0 = s.sem("ready0")
        based = s.sem("based")
        u_ready = s.sem("u_ready")
        inner_ready = s.sem("inner_ready")
        up_ready = s.sem("up_ready")
        angle_ready = s.sem("angle_ready")
        sine_ready = s.sem("sine_ready")
        kdv_ready = s.sem("kdv_ready")
        du_ready = s.sem("du_ready")
        out_ready = s.sem("out_ready")
        added = s.sem("added")
        vec = s.sem("vec")
        gps = s.sem("gps")
        passed = s.sem("passed")
        block = s.block()
        LOADS = 6 * 16
        START = 1
        at = lambda o: up[:, :, o:o + T]

        @block.sync
        def _(sp):
            for dst, src in ((wsi, "wsi"), (b_si, "bsi"), (gates, "gates"), (alpha, "alpha"), (wso, "wso")):
                sp.dma_start(dst[:], c.dram[f"wave_{src}"]).then_inc(loaded, 16)
            sp.dma_start(b_so[:], c.dram["wave_bso"].partition_broadcast(P)).then_inc(loaded, 16)

        @block.tensor
        def _(pe):
            pe.sem_inc(inner_ready, START)
            pe.sem_inc(du_ready, START)
            pe.sem_inc(sine_ready, START)
            pe.sem_inc(out_ready, START)
            pe.wait_ge(loaded, LOADS)
            with pe.Fori(0, B) as b:
                pe.wait_ge(inner_ready, b + START)
                for m in range(DC):
                    for k in range(DC):
                        last = nc.tensor.matmul(u_ps[m][:], wsi[:, k, m * P:(m + 1) * P], c.xnT[:, k, ds(b * T, T)],
                                                start=(k == 0), stop=(k == DC - 1))
                last.then_inc(u_ready, 1)
                pe.wait_ge(du_ready, b + (1 + START))
                for t in range(TB):
                    for k in range(DC):
                        last = nc.tensor.matmul(out_ps[t][:, 0:D], du[:, k, t * P:(t + 1) * P], wso[:, k, :],
                                                start=(k == 0), stop=(k == DC - 1))
                last.then_inc(out_ready, 1)

        @block.scalar
        def _(act):
            act.wait_ge(loaded, LOADS)
            with act.Fori(0, B) as b:
                act.wait_ge(u_ready, b + 1)
                act.wait_ge(du_ready, b + START)
                act.sem_inc(passed, 1)
                for m in range(DC):
                    last = nc.scalar.activation(up[:, m, EDGE:EDGE + T], u_ps[m][:], ACT.Identity, bias=b_si[:, m:m + 1])
                last.then_inc(inner_ready, 1)
                act.wait_ge(inner_ready, b + (1 + START))
                act.sem_inc(passed, 1)
                for to, edge in ((0, EDGE), (EDGE + T, EDGE + T - 1)):
                    last = nc.scalar.activation(up[:, :, to:to + EDGE], up[:, :, edge:edge + 1].broadcast_to([P, DC, EDGE]),
                                                ACT.Copy)
                last.then_inc(up_ready, 1)
                act.wait_ge(angle_ready, b + 1)
                nc.scalar.activation(sine[:], angle[:], ACT.Sin).then_inc(sine_ready, 1)

        @block.gpsimd
        def _(pool):
            pool.wait_ge(loaded, LOADS)
            nc.gpsimd.tensor_tensor(xa[:], xa[:], b_so[:].unsqueeze(1).broadcast_to([P, NT, D]), ALU.add).then_inc(based, 1)
            pool.wait_ge(based, 1)
            nc.gpsimd.tensor_tensor(c.x[:], c.x[:], xa[:], ALU.add).then_inc(based, 1)
            with pool.Fori(0, B) as b:
                chain = Chain(pool, gps, per=2)
                chain.start(b)
                pool.wait_ge(up_ready, b + 1)
                pool.sem_inc(passed, 1)
                nc.gpsimd.tensor_tensor(d1[:], at(3), at(1), ALU.subtract)
                chain.link(nc.gpsimd.tensor_scalar(f[:], at(2), -3.0, 1.0, ALU.mult, ALU.add))
                pool.wait_ge(du_ready, b + START)
                pool.sem_inc(passed, 1)
                chain.link(nc.gpsimd.tensor_tensor(kdv[:], f[:], d1[:], ALU.mult))
                nc.gpsimd.tensor_tensor(d2[:], at(4), at(0), ALU.subtract).then_inc(kdv_ready, 1)
                chain.close()

        @block.vector
        def _(dve):
            dve.wait_ge(loaded, LOADS)
            nc.vector.tensor_scalar(gates[:], gates[:], SOL, None, ALU.mult).then_inc(ready0, 1)
            dve.wait_ge(ready0, 1)
            dve.wait_ge(based, 2)
            with dve.Fori(0, B) as b:
                chain = Chain(dve, vec, per=9 + DC)
                chain.start(b)
                dve.wait_ge(up_ready, b + 1)
                dve.sem_inc(passed, 1)
                chain.link(nc.vector.tensor_scalar(turns[:], at(2), 1 / (2 * np.pi), TO_WHOLE, ALU.mult, ALU.add))
                chain.link(nc.vector.tensor_scalar(turns[:], turns[:], -TO_WHOLE, None, ALU.add))
                chain.link(nc.vector.scalar_tensor_tensor(out=angle[:], in0=turns[:], scalar=-TWO_PI_HIGH, in1=at(2),
                                                          op0=ALU.mult, op1=ALU.add))
                chain.link(nc.vector.scalar_tensor_tensor(out=angle[:], in0=turns[:], scalar=-TWO_PI_LOW, in1=angle[:],
                                                          op0=ALU.mult, op1=ALU.add))
                nc.vector.tensor_scalar(angle[:], angle[:], -PI, PI, ALU.max, ALU.min).then_inc(angle_ready, 1)
                chain.link(nc.vector.tensor_tensor(s1[:], at(3), at(1), ALU.add))
                nc.vector.scalar_tensor_tensor(out=s1[:], in0=at(2), scalar=-2.0, in1=s1[:], op0=ALU.mult, op1=ALU.add)
                for m in range(DC):
                    last = nc.vector.tensor_scalar(heat[:, m, :], up[:, m, EDGE:EDGE + T], alpha[:, m:m + 1], 1.0, ALU.mult, ALU.add)
                chain.link(last)
                chain.link(nc.vector.tensor_tensor(heat[:], heat[:], s1[:], ALU.mult))
                dve.wait_ge(kdv_ready, b + 1)
                chain.link(nc.vector.scalar_tensor_tensor(out=kdv[:], in0=d2[:], scalar=-0.5, in1=kdv[:], op0=ALU.mult, op1=ALU.add))
                dve.wait_ge(out_ready, b + START)
                dve.wait_ge(sine_ready, b + (1 + START))
                dve.sem_inc(passed, 1)
                for m in range(DC):
                    chain.link(nc.vector.tensor_scalar(sine[:, m, :], sine[:, m, :], gates[:, 0, m:m + 1], None, ALU.mult))
                for k, term in ((1, kdv), (2, heat)):
                    for m in range(DC):
                        last = nc.vector.scalar_tensor_tensor(out=du[:, m, :], in0=term[:, m, :], scalar=gates[:, k, m:m + 1],
                                                              in1=(sine if k == 1 else du)[:, m, :], op0=ALU.mult, op1=ALU.add)
                    if k == 1:
                        chain.link(last)
                last.then_inc(du_ready, 1)
                for t in range(TB):
                    row = c.x[:, ds(b * TB + t, 1), :].rearrange("p a d -> p (a d)")
                    dve.wait_ge(out_ready, b + (1 + START))
                    last = nc.vector.tensor_tensor(row, row, out_ps[t][:, 0:D], ALU.add)
                last.then_inc(added, 1)
                chain.close()


NE = 8
CAPACITY = -(-B * T * 5 // (NE * 4))
ST = -(-CAPACITY // P)


def slots_of(j):
    return min(P, CAPACITY - j * P)


def lay_experts(a, rows, cols):
    p, f = np.arange(P)[:, None], np.arange(2 * B * T)[None, :]
    return {
        "moe_router": rows(a["L1_ffn_router_w"].T),
        "moe_w1": a["L1_ffn_W1"].reshape(NE, DC, P, DH).transpose(0, 2, 1, 3),
        "moe_b1": a["L1_ffn_b1"].reshape(NE, MH, P).transpose(2, 0, 1),
        "moe_w2": a["L1_ffn_W2"].reshape(NE, MH, P, D).transpose(0, 2, 1, 3),
        "moe_b2": a["L1_ffn_b2"].reshape(1, NE, D),
        "moe_before": (f - B * T < p).astype(np.float32),
        "moe_nth": np.tile(np.arange(CAPACITY, dtype=np.float32), (P, 1)),
        "moe_slot": (np.arange(P)[:, None] + P * np.arange(ST, (NE * ST))[None, :]).astype(np.float32),
        "moe_order": np.tile(np.arange(NE, 0, -1, dtype=np.float32), (P, 1)),
    }


def experts(nc, c):
    with Scope(nc, "moe_kept") as kept:
        xn = kept.sb("xn", [P, NT, D])
        nth = kept.sb("nth", [P, NE - 1, NT])
        where = kept.sb("where", [P, B * T])
        layernorm(nc, c, "moe_ln", c.x, c.xnT, keep=xn)
        route(nc, c, nth, where)
        yhi = kept.sb("yhi", [P, (NE - 1) * ST, D], F32R)
        ylo = kept.sb("ylo", [P, (NE - 1) * ST, D], F32R)
        own_slots(nc, c, xn, nth, yhi, ylo)
        scatter(nc, c, where, yhi, ylo)


def route(nc, c, nth, where):
    NB = B * T // 512
    NT4 = 512 // P
    GR = NT // 4
    with Scope(nc, "moe_route") as s:
        router = s.sb("router", [P, DC, NE])
        order = s.sb("order", [P, NE])
        before = s.sb("before", [P, 2 * B * T])
        logits = s.sb("logits", [P, NT, NE])
        top = s.sb("top", [P, NT])
        is_top = s.sb("is_top", [P, NT, NE])
        mine = s.sb("mine", [P, 2, NT])
        wide = s.sb("wide", [P, 2, 2, 4, P])
        row = s.sb("row", [P, 2, B * T])
        rival = s.sb("rival", [P, B * T])
        hit = s.sb("hit", [P, B * T])
        place = s.sb("place", [P, NT, 2])
        keep = s.sb("keep", [P, NT])
        at_zero = s.sb("at_zero", [P, NT])
        w1 = s.sb("w1", [P, DC, DH])
        w2 = s.sb("w2", [P, MH, D])
        b1 = s.sb("b1", [P, NE, MH])
        b2 = s.sb("b2", [1, D])
        hid = [s.sb(f"hid{k}", [P, MH, 512]) for k in range(2)]
        y0 = s.sb("y0", [P, NT, D])
        l_ps = s.ps("l_ps", [P, NT, NE])
        r_ps = [s.ps(f"r_ps{k}", [P, 512]) for k in range(2)]
        mid = [s.ps(f"mid{k}", [P, 512]) for k in range(2)]
        low = [s.ps(f"low{k}", [P, 512]) for k in range(2)]
        loaded = s.sem("loaded")
        l_ready = s.sem("l_ready")
        less_ready = s.sem("less_ready")
        exp_ready = s.sem("exp_ready")
        vec = s.sem("vec")
        vec_t = s.sem("vec_t")
        wide_ready = s.sem("wide_ready")
        turned = s.sem("turned")
        row_ready = s.sem("row_ready")
        w_loaded = s.sem("w_loaded")
        mid_ready = s.sem("mid_ready")
        hid_ready = s.sem("hid_ready")
        out_ready = s.sem("out_ready")
        y0_ready = s.sem("y0_ready")
        passed = s.sem("passed")
        block = s.block()

        @block.sync
        def _(sp):
            for dst, src in ((router, "router"), (order, "order"), (before, "before")):
                sp.dma_start(dst[:], c.dram[f"moe_{src}"]).then_inc(loaded, 16)
            sp.dma_start(b1[:], c.dram["moe_b1"]).then_inc(w_loaded, 16)
            sp.dma_start(b2[:], c.dram["moe_b2"][:, 0]).then_inc(w_loaded, 16)
            sp.dma_start(w1[:], c.dram["moe_w1"][0]).then_inc(w_loaded, 16)
            sp.dma_start(w2[:], c.dram["moe_w2"][0]).then_inc(w_loaded, 16)

        @block.tensor
        def _(pe):
            pe.wait_ge(loaded, 48)
            for t in range(NT):
                for k in range(DC):
                    last = nc.tensor.matmul(l_ps[:, t, :], c.xnT[:, k, t * P:(t + 1) * P], router[:, k, :],
                                            start=(k == 0), stop=(k == DC - 1))
            last.then_inc(l_ready, 1)
            for g in range(GR):
                pe.wait_ge(wide_ready, g + 1)
                if g >= 1:
                    pe.wait_ge(row_ready, g)
                for e in range(2):
                    for t in range(4):
                        last = nc.tensor.transpose(r_ps[e][:, t * P:(t + 1) * P], wide[:, g % 2, e, t, :], c.ident[:])
                last.then_inc(turned, 1)
            pe.sem_inc(hid_ready, 2)
            pe.sem_inc(y0_ready, 2)
            pe.wait_ge(w_loaded, 64)
            with pe.Fori(0, NB // 2) as i:
                for k in range(2):
                    for m in range(MH):
                        pe.wait_ge(hid_ready, (i * 2 + k) * MH + (m + 1))
                        for d in range(DC):
                            last = nc.tensor.matmul(mid[m % 2][:], w1[:, d, m * P:(m + 1) * P],
                                                    c.xnT[:, d, ds((i * 2 + k) * 512, 512)], start=(d == 0), stop=(d == DC - 1))
                        last.then_inc(mid_ready, 1)
                    pe.wait_ge(hid_ready, (i * 2 + k) * MH + (MH + 2))
                    for t in range(NT4):
                        pe.wait_ge(y0_ready, (i * 2 + k) * NT4 + (t + 1))
                        pe.sem_inc(passed, 1)
                        nc.tensor.matmul(low[t % 2][:, 0:D], c.ones[0:1, :], b2[:], start=True, stop=False)
                        for m in range(MH):
                            last = nc.tensor.matmul(low[t % 2][:, 0:D], hid[k][:, m, t * P:(t + 1) * P], w2[:, m, :],
                                                    start=False, stop=(m == MH - 1))
                        last.then_inc(out_ready, 1)
            for g in range(GR):
                pe.wait_ge(wide_ready, GR + g + 1)
                if g >= 2:
                    pe.wait_ge(row_ready, GR + g - 1)
                for t in range(4):
                    last = nc.tensor.transpose(r_ps[g % 2][:, t * P:(t + 1) * P], wide[:, g % 2, 0, t, :], c.ident[:])
                last.then_inc(turned, 1)

        @block.scalar
        def _(act):
            act.wait_ge(less_ready, 1)
            nc.scalar.activation(is_top[:], logits[:], ACT.Exp).then_inc(exp_ready, 1)
            for g in range(GR):
                act.wait_ge(turned, g + 1)
                for e in range(2):
                    last = nc.scalar.activation(row[:, e, g * 512:(g + 1) * 512], r_ps[e][:], ACT.Copy)
                last.then_inc(row_ready, 1)
            act.wait_ge(w_loaded, 64)
            with act.Fori(0, NB // 2) as i:
                for k in range(2):
                    for m in range(MH):
                        act.wait_ge(mid_ready, (i * 2 + k) * MH + (m + 1))
                        nc.scalar.activation(hid[k][:, m, :], mid[m % 2][:], ACT.Relu, bias=b1[:, 0, m:m + 1]).then_inc(hid_ready, 1)
                    for t in range(NT4):
                        act.wait_ge(out_ready, (i * 2 + k) * NT4 + (t + 1))
                        act.sem_inc(passed, 1)
                        nc.scalar.activation(y0[:, ds((i * 2 + k) * NT4 + t, 1), :].rearrange("p a d -> p (a d)"),
                                             low[t % 2][:, 0:D], ACT.Copy).then_inc(y0_ready, 1)
            for g in range(GR):
                act.wait_ge(turned, GR + g + 1)
                nc.scalar.activation(where[:, g * 512:(g + 1) * 512], r_ps[g % 2][:], ACT.Copy).then_inc(row_ready, 1)

        @block.vector
        def _(dve):
            chain = Chain(dve, vec)
            over = lambda v: v.unsqueeze(2).broadcast_to([P, NT, NE])

            def widen(v, g, e):
                return nc.vector.tensor_copy(wide[:, g % 2, e], v[:, g * 4:(g + 1) * 4].unsqueeze(2).broadcast_to([P, 4, P]))

            dve.wait_ge(loaded, 48)
            dve.wait_ge(l_ready, 1)
            chain.link(nc.vector.tensor_reduce(top[:], l_ps[:], AX, ALU.max))
            nc.vector.tensor_tensor(logits[:], l_ps[:], over(top[:]), ALU.subtract).then_inc(less_ready, 1)
            dve.wait_ge(exp_ready, 1)
            chain.link(nc.vector.tensor_reduce(top[:], is_top[:], AX, ALU.add))
            chain.link(nc.vector.reciprocal(mine[:, 1, :], top[:]))
            chain.link(nc.vector.scalar_tensor_tensor(out=is_top[:], in0=logits[:], scalar=0.0,
                                                      in1=order[:].unsqueeze(1).broadcast_to([P, NT, NE]),
                                                      op0=ALU.is_equal, op1=ALU.mult))
            chain.link(nc.vector.tensor_reduce(mine[:, 0, :], is_top[:], AX, ALU.max))
            for g in range(GR):
                if g >= 2:
                    dve.wait_ge(turned, g - 1)
                for e in range(2):
                    last = widen(mine[:, e, :], g, e)
                last.then_inc(wide_ready, 1)
            dve.wait_ge(row_ready, GR)
            one = lambda v, t: v[:, ds(t, 1)]
            with dve.Fori(0, NT) as t:
                chain_t = Chain(dve, vec_t, per=3)
                chain_t.start(t)
                chain_t.link(nc.vector.scalar_tensor_tensor(out=rival[:], in0=row[:, 0, :], scalar=one(mine[:, 0, :], t),
                                                            in1=row[:, 1, :], op0=ALU.is_equal, op1=ALU.mult))
                chain_t.link(nc.vector.tensor_scalar(hit[:], rival[:], one(mine[:, 1, :], t), 0.0, ALU.is_gt, ALU.add,
                                                     accum_out=place[:, ds(t, 1), 0]))
                chain_t.link(nc.vector.scalar_tensor_tensor(out=hit[:], in0=rival[:], scalar=one(mine[:, 1, :], t),
                                                            in1=before[:, ds(t * -P + B * T, B * T)], op0=ALU.is_equal,
                                                            op1=ALU.mult, accum_out=place[:, ds(t, 1), 1]))
                chain_t.close()
            chain.link(nc.vector.tensor_tensor(top[:], place[:, :, 0], place[:, :, 1], ALU.add))
            chain.link(nc.vector.tensor_scalar(keep[:], top[:], float(CAPACITY), None, ALU.is_lt))
            chain.link(nc.vector.tensor_scalar(mine[:, 0, :], mine[:, 0, :], -1.0, float(NE), ALU.mult, ALU.add))
            chain.link(nc.vector.tensor_tensor(mine[:, 0, :], mine[:, 0, :], keep[:], ALU.mult))
            chain.link(nc.vector.tensor_scalar(top[:], top[:], float(CAPACITY - 1), None, ALU.min))
            chain.link(nc.vector.scalar_tensor_tensor(out=keep[:], in0=mine[:, 0, :], scalar=float(ST * P), in1=top[:],
                                                      op0=ALU.mult, op1=ALU.add))
            for g in range(GR):
                if g >= 2:
                    dve.wait_ge(turned, GR + g - 1)
                widen(keep, g, 0).then_inc(wide_ready, 1)
            chain.link(nc.vector.tensor_scalar(at_zero[:], mine[:, 0, :], 0.0, None, ALU.is_equal))
            chain.link(nc.vector.scalar_tensor_tensor(out=rival[:, 0:NT], in0=mine[:, 0, :], scalar=float(CAPACITY), in1=top[:],
                                                      op0=ALU.mult, op1=ALU.add))
            for e in range(NE - 1):
                nc.vector.tensor_scalar(nth[:, e, :], rival[:, 0:NT], -float((e + 1) * CAPACITY), None, ALU.add)
            for t in range(NT):
                dve.wait_ge(y0_ready, t + 1 + 2)
                nc.vector.scalar_tensor_tensor(out=c.x[:, t, :], in0=y0[:, t, :], scalar=at_zero[:, t:t + 1], in1=c.x[:, t, :],
                                               op0=ALU.mult, op1=ALU.add)


def own_slots(nc, c, xn, nth, yhi, ylo):
    HT = NT // 2
    E = NE - 1
    with Scope(nc, "moe_own") as s:
        xhi, xlo = (s.sb(n, [P, NT, D], F32R) for n in ("xhi", "xlo"))
        numbers = s.sb("numbers", [P, CAPACITY])
        sits = s.sb("sits", [P, 2, HT, CAPACITY], F32R)
        own = s.sb("own", [P, DC, CAPACITY])
        w1 = s.sb("w1", [P, 2, DC, DH])
        w2 = s.sb("w2", [P, 2, MH, D])
        b1 = s.sb("b1", [P, NE, MH])
        b2 = s.sb("b2", [1, 2, D])
        hid = s.sb("hid", [P, MH, CAPACITY])
        own_ps = [s.ps(f"own_ps{d}", [P, 512]) for d in range(DC)]
        mid = [s.ps(f"mid{k}", [P, 512]) for k in range(2)]
        low = [s.ps(f"low{j}", [P, 512]) for j in range(ST)]
        loaded = s.sem("loaded")
        w_loaded = [s.sem(f"w_loaded{k}") for k in range(2)]
        xhi_ready = s.sem("xhi_ready")
        xlo_ready = s.sem("xlo_ready")
        sits_ready = s.sem("sits_ready")
        gathered = s.sem("gathered")
        own_ready = s.sem("own_ready")
        mid_ready = s.sem("mid_ready")
        hid_ready = s.sem("hid_ready")
        out_ready = s.sem("out_ready")
        yhi_ready = s.sem("yhi_ready")
        ylo_ready = s.sem("ylo_ready")
        passed = s.sem("passed")
        block = s.block()
        assert E % 2

        def by_experts(eng, expert):
            with eng.Fori(0, E // 2) as i:
                for k in range(2):
                    expert(i, k, False)
            expert(E // 2, 0, True)

        @block.sync
        def _(sp):
            sp.dma_start(b1[:], c.dram["moe_b1"]).then_inc(loaded, 16)
            sp.dma_start(numbers[:], c.dram["moe_nth"]).then_inc(loaded, 16)

            def expert(i, k, last):
                e = i * 2 + k
                sp.wait_ge(out_ready, e * ST + ST)
                sp.dma_start(w1[:, k], c.dram["moe_w1"][ds(e + 1, 1)].rearrange("a p c m -> (a p) c m")).then_inc(w_loaded[k], 16)
                sp.dma_start(w2[:, k], c.dram["moe_w2"][ds(e + 1, 1)].rearrange("a p c m -> (a p) c m")).then_inc(w_loaded[k], 16)
                sp.dma_start(b2[:, k], c.dram["moe_b2"][:, ds(e + 1, 1)].rearrange("a e d -> a (e d)")).then_inc(w_loaded[k], 16)
            by_experts(sp, expert)

        @block.scalar
        def _(act):
            def take(e):
                act.wait_ge(gathered, e * 2 + 2)
                for d in range(DC):
                    last = nc.scalar.activation(own[:, d, :], own_ps[d][:, 0:CAPACITY], ACT.Copy)
                last.then_inc(own_ready, 1)

            def expert(i, k, last):
                e = i * 2 + k
                for m in range(MH):
                    act.wait_ge(mid_ready, e * MH + (m + 1))
                    act.sem_inc(passed, 1)
                    nc.scalar.activation(hid[:, m, :], mid[m % 2][:, 0:CAPACITY], ACT.Relu, bias=b1[:, ds(e + 1, 1), m]
                                         ).then_inc(hid_ready, 1)
                if not last:
                    take(e + 1)
                for j in range(ST):
                    n = slots_of(j)
                    act.wait_ge(out_ready, e * ST + (j + 1 + 2 * ST))
                    act.sem_inc(passed, 1)
                    nc.scalar.activation(yhi[0:n, ds(e * ST + j, 1), :].rearrange("p a d -> p (a d)"), low[j][0:n, 0:D], ACT.Copy
                                         ).then_inc(yhi_ready, 1)

            nc.scalar.activation(xhi[:], xn[:], ACT.Copy).then_inc(xhi_ready, 1)
            act.wait_ge(loaded, 32)
            take(0)
            by_experts(act, expert)

        @block.vector
        def _(dve):
            def seats(e):
                for half in range(2):
                    dve.wait_ge(gathered, e * 2 + (half - 1))
                    dve.sem_inc(passed, 1)
                    for t in range(HT):
                        last = nc.vector.tensor_scalar(sits[:, half, t, :], numbers[:], nth[:, ds(e, 1), half * HT + t], None,
                                                       ALU.is_equal)
                    last.then_inc(sits_ready, 1)

            def expert(i, k, last):
                e = i * 2 + k
                if not last:
                    seats(e + 1)
                for j in range(ST):
                    n = slots_of(j)
                    dve.wait_ge(yhi_ready, e * ST + (j + 1))
                    dve.sem_inc(passed, 1)
                    slot = lambda v: v[0:n, ds(e * ST + j, 1), :].rearrange("p a d -> p (a d)")
                    nc.vector.tensor_tensor(slot(ylo), low[j][0:n, 0:D], slot(yhi).bitcast(F32), ALU.subtract).then_inc(ylo_ready, 1)

            dve.wait_ge(loaded, 32)
            for half in range(2):
                for t in range(HT):
                    last = nc.vector.tensor_scalar(sits[:, half, t, :], numbers[:], nth[:, 0:1, half * HT + t], None, ALU.is_equal)
                last.then_inc(sits_ready, 1)
            dve.wait_ge(xhi_ready, 1)
            nc.vector.tensor_tensor(xlo[:], xn[:], xhi[:].bitcast(F32), ALU.subtract).then_inc(xlo_ready, 1)
            by_experts(dve, expert)

        @block.tensor
        def _(pe):
            pe.sem_inc(out_ready, 2 * ST)
            pe.sem_inc(hid_ready, 2)
            pe.sem_inc(ylo_ready, ST)

            def gather(e):
                for half in range(2):
                    pe.wait_ge(sits_ready, e * 2 + (half + 1))
                    pe.sem_inc(passed, 1)
                    for t in range(HT):
                        for part in range(2):
                            for d in range(DC):
                                x = (xhi, xlo)[part]
                                last = nc.tensor.matmul(own_ps[d][:, 0:CAPACITY], x[:, half * HT + t, d * P:(d + 1) * P],
                                                        sits[:, half, t, :], start=(half == 0 and t == 0 and part == 0),
                                                        stop=(half == 1 and t == HT - 1 and part == 1))
                    last.then_inc(gathered, 1)

            def expert(i, k, last_expert):
                e = i * 2 + k
                pe.wait_ge(own_ready, e + 1)
                pe.wait_ge(w_loaded[k], i * 48 + 48)
                for m in range(MH):
                    pe.wait_ge(hid_ready, e * MH + (m + 1))
                    pe.sem_inc(passed, 1)
                    for d in range(DC):
                        last = nc.tensor.matmul(mid[m % 2][:, 0:CAPACITY], w1[:, k, d, m * P:(m + 1) * P], own[:, d, :],
                                                start=(d == 0), stop=(d == DC - 1))
                    last.then_inc(mid_ready, 1)
                if not last_expert:
                    gather(e + 1)
                pe.wait_ge(hid_ready, e * MH + (MH + 2))
                for j in range(ST):
                    n = slots_of(j)
                    pe.wait_ge(ylo_ready, e * ST + (j + 1))
                    pe.sem_inc(passed, 1)
                    nc.tensor.matmul(low[j][0:n, 0:D], c.ones[0:1, 0:n], b2[:, k, :], start=True, stop=False)
                    for m in range(MH):
                        last = nc.tensor.matmul(low[j][0:n, 0:D], hid[:, m, j * P:j * P + n], w2[:, k, m, :],
                                                start=False, stop=(m == MH - 1))
                    last.then_inc(out_ready, 1)

            pe.wait_ge(xlo_ready, 1)
            gather(0)
            by_experts(pe, expert)


def scatter(nc, c, where, yhi, ylo):
    NB = B * T // 512
    NT4 = 512 // P
    tiles = [(e * ST + j, slots_of(j)) for e in range(NE - 1) for j in range(ST)]
    with Scope(nc, "moe_back") as s:
        slot = s.sb("slot", [P, len(tiles)])
        sits = s.sb("sits", [P, 2, len(tiles), 512], F32R)
        back = [s.ps(f"back{t}", [P, 512]) for t in range(2 * NT4)]
        loaded = s.sem("loaded")
        sits_ready = s.sem("sits_ready")
        rows_ready = s.sem("rows_ready")
        block = s.block()

        @block.sync
        def _(sp):
            sp.dma_start(slot[:], c.dram["moe_slot"]).then_inc(loaded, 16)

        @block.vector
        def _(dve):
            def seats(g):
                for j, n in tiles:
                    last = nc.vector.tensor_scalar(sits[0:n, g % 2, j, :], where[0:n, g * 512:(g + 1) * 512], slot[0:n, j:j + 1], None,
                                                   ALU.is_equal)
                last.then_inc(sits_ready, 1)

            dve.wait_ge(loaded, 16)
            seats(0)
            for g in range(NB):
                if g + 1 < NB:
                    if g >= 1:
                        dve.wait_ge(rows_ready, g * NT4)
                    seats(g + 1)
                for t in range(NT4):
                    dve.wait_ge(rows_ready, g * NT4 + t + 1)
                    tile = c.x[:, g * NT4 + t, :]
                    nc.vector.tensor_tensor(tile, tile, back[g % 2 * NT4 + t][:, 0:D], ALU.add)

        @block.tensor
        def _(pe):
            with pe.Fori(0, NB // 2) as i:
                for k in range(2):
                    pe.wait_ge(sits_ready, i * 2 + (k + 1))
                    for t in range(NT4):
                        for j, n in tiles:
                            for part in range(2):
                                y = (yhi, ylo)[part]
                                last = nc.tensor.matmul(back[k * NT4 + t][:, 0:D], sits[0:n, k, j, t * P:(t + 1) * P], y[0:n, j, :],
                                                        start=(j == 0 and part == 0), stop=(j == len(tiles) - 1 and part == 1))
                        last.then_inc(rows_ready, 1)


def store(nc, c):
    with Scope(nc, "store") as s:
        stored = s.sem("stored")
        block = s.block()

        @block.sync
        def _(sp):
            sp.dma_start(c.dram["out"], c.x[:]).then_inc(stored, 16)
            sp.wait_ge(stored, 16)


class Core:

    def __init__(self, dram):
        self.dram = dram


LAYERS = [gated_delta_net, masked_attention, ternary_mlp, selective_scan, full_attention, experts]


def program(nc, dram, layers=LAYERS):
    c = Core(dram)
    with ExitStack() as stack:
        c.x = stack.enter_context(nc.sbuf_tensor("x", [P, NT, D], F32))
        c.xnT = stack.enter_context(nc.sbuf_tensor("xnT", [P, DC, B * T], F32))
        c.ident = stack.enter_context(nc.sbuf_tensor("ident", [P, P], F32))
        c.ones = stack.enter_context(nc.sbuf_tensor("ones", [P, P], F32))
        c.eps = stack.enter_context(nc.sbuf_tensor("eps", [P, 1], F32))
        constants(nc, c)
        for layer in layers:
            layer(nc, c)
        store(nc, c)


def laid_out(inputs):
    a = {k: np.asarray(v) for k, v in inputs.items()}
    heads = lambda v, h: v.reshape(h, -1).T
    twice = lambda v: np.concatenate([v, v], 0)
    cols = lambda v: v.reshape(-1, P).T
    rows = lambda w: w.reshape(-1, P, w.shape[-1]).transpose(1, 0, 2)
    o = {
        "x": a["x"].reshape(NT, P, D).transpose(1, 0, 2),
        "ctxT": a["ctx_1024"].transpose(0, 2, 1).reshape(B, DC, P, S2).transpose(0, 2, 1, 3),
    }
    o.update(lay_gated_delta_net(a, rows, cols))
    o.update(lay_masked_attention(a, rows, cols))
    o.update(lay_ternary_mlp(a, rows, cols))
    o.update(lay_selective_scan(a, rows, cols))
    o.update(lay_full_attention(a, rows, cols))
    o.update(lay_experts(a, rows, cols))
    return {k: np.ascontiguousarray(v) for k, v in o.items()}


def kernel(**inputs):
    import concourse.bacc as bacc
    from concourse.bass_utils import run_bass_kernel_spmd

    nc = bacc.Bacc("TRN2", target_bir_lowering=False, num_devices=1)
    arrays = laid_out(inputs)
    dram = {k: nc.dram_tensor(f"in_{k}", v.shape, mybir.dt.from_np(v.dtype), kind="ExternalInput").ap()
            for k, v in arrays.items()}
    dram["out"] = nc.dram_tensor("out_0", [P, NT, D], F32, kind="ExternalOutput").ap()
    program(nc, dram)
    r = run_bass_kernel_spmd(nc, [{f"in_{k}": v for k, v in arrays.items()}], core_ids=[0])
    return r.results[0]["out_0"].transpose(1, 0, 2).reshape(B, T, D)
```
